# Optimizing a Trainium2 kernel written in Bass

```python
import numpy as np
import jax
import jax.numpy as jnp

def _softmax(x, axis=-1):
    return jax.nn.softmax(x, axis=axis)

def _gelu(x):
    return jax.nn.gelu(x, approximate=True)

def _silu(x):
    return jax.nn.silu(x)

def _sigmoid(x):
    return jax.nn.sigmoid(x)

def _layernorm(x, axis=-1, eps=1e-05):
    m = jnp.mean(x, axis=axis, keepdims=True)
    v = jnp.var(x, axis=axis, keepdims=True)
    return (x - m) / jnp.sqrt(v + eps)

def _scatter_add(tgt, idx, src, axis=0):
    return tgt.at[idx].add(src)

def _segment_sum(src, seg, n):
    return jax.ops.segment_sum(src, seg, n)
kernel_name = 'mk_flamingo_gated_d2_seqx_r4_f47b0b'

def setup_inputs(seed: int=0):
    np.random.seed(seed)
    _w = jnp.asarray

    def _rec_inputs():
        import jax
        import jax.numpy as jnp
        _rk = jax.random.key(seed)
        x = -0.0002928 + 1 * jax.random.normal(jax.random.fold_in(_rk, 1), (8, 256, 256), jnp.float32)
        _lenS = 256 - jax.random.randint(jax.random.fold_in(_rk, 7), (8,), 0, max(1, 256 // 4) + 1, jnp.int32)
        _lenS2 = 77 - jax.random.randint(jax.random.fold_in(_rk, 8), (8,), 0, max(1, 77 // 4) + 1, jnp.int32)
        _ctx_1024P = jax.random.normal(jax.random.fold_in(_rk, 11), (8, 16, 256), jnp.float32)
        _ctx_1024c = jax.random.dirichlet(jax.random.fold_in(_rk, 511), 0.3 * jnp.ones((16,), jnp.float32), (8, 77))
        _ctx_1024t = jnp.einsum('bsk,bkd->bsd', _ctx_1024c, _ctx_1024P)
        _ctx_1024t = _ctx_1024t * jax.lax.rsqrt(jnp.mean(jnp.square(_ctx_1024t)) + 1e-12) * 0.953939
        ctx_1024 = 4.13588e-05 + 0.999923 * (_ctx_1024t + 0.3 * jax.random.normal(jax.random.fold_in(_rk, 611), (8, 77, 256), jnp.float32))
        _g = jax.random.normal(jax.random.fold_in(_rk, 9001), (2, 2), jnp.float32)
        _g = jnp.sign(_g) * jnp.maximum(jnp.abs(_g), 1.0) + (_g == 0) * 1.0
        g_xattn = _g[0]
        g_ffn = _g[1]
        return (x, ctx_1024, g_xattn, g_ffn)
    x, ctx_1024, g_xattn, g_ffn = _rec_inputs()

    def _L0_xattn_setup():
        import jax, jax.numpy as jnp
        import numpy as np
        D_MODEL = 256
        N_HEADS = 16
        D_HEAD = D_MODEL // N_HEADS
        key = jax.random.key(seed)
        ks = jax.random.split(key, 6)
        query = jax.random.normal(ks[0], (2, 512, D_MODEL), dtype=jnp.float32)
        context = jax.random.normal(ks[1], (2, 1024, D_MODEL), dtype=jnp.float32)
        s = 1.0 / np.sqrt(D_MODEL)
        Wq = jax.random.normal(ks[2], (D_MODEL, D_MODEL), dtype=jnp.float32) * s
        Wk = jax.random.normal(ks[3], (D_MODEL, D_MODEL), dtype=jnp.float32) * s
        Wv = jax.random.normal(ks[4], (D_MODEL, D_MODEL), dtype=jnp.float32) * s
        Wo = jax.random.normal(ks[5], (D_MODEL, D_MODEL), dtype=jnp.float32) * s
        return {'query': query, 'context': context, 'Wq': Wq, 'Wk': Wk, 'Wv': Wv, 'Wo': Wo}
    _L0_xattn_all = _L0_xattn_setup()
    _L0_xattn_in = {k: v for k, v in _L0_xattn_all.items() if k in ('Wq', 'Wk', 'Wv', 'Wo')}
    del _L0_xattn_all

    def _L0_ffn_setup():
        import jax, jax.numpy as jnp
        import numpy as np
        key = jax.random.key(seed)
        ks = jax.random.split(key, 4)
        B, T, M, E, F = (4, 512, 256, 8, 1024)
        hidden_states = jax.random.normal(ks[0], (B, T, M), dtype=jnp.float32)
        wg = jax.random.normal(ks[1], (M, E), dtype=jnp.float32) * (1.0 / np.sqrt(M))
        w1 = jax.random.normal(ks[2], (E, M, F), dtype=jnp.float32) * (1.0 / np.sqrt(M))
        b1 = jnp.zeros((E, F), dtype=jnp.float32)
        w2 = jax.random.normal(ks[3], (E, F, M), dtype=jnp.float32) * (1.0 / np.sqrt(F))
        b2 = jnp.zeros((E, M), dtype=jnp.float32)
        return {'hidden_states': hidden_states, 'wg': wg, 'w1': w1, 'b1': b1, 'w2': w2, 'b2': b2}
    _L0_ffn_all = _L0_ffn_setup()
    _L0_ffn_in = {k: v for k, v in _L0_ffn_all.items() if k in ('wg', 'w1', 'b1', 'w2', 'b2')}
    del _L0_ffn_all

    def _L1_xattn_setup():
        import jax, jax.numpy as jnp
        import numpy as np
        import math
        D_MODEL = 256
        NHEAD = 16
        FACTOR = 1
        B, L = (2, 1024)

        def _autocorr_forward(query, key, value, Wq, bq, Wk, bk, Wv, bv, Wo, bo):
            Bq, Lq, d = query.shape
            Lk = key.shape[1]
            H = NHEAD
            Dk = d // H
            Q = (query @ Wq + bq).reshape(Bq, Lq, H, Dk).transpose(0, 2, 1, 3)
            K = (key @ Wk + bk).reshape(Bq, Lk, H, Dk).transpose(0, 2, 1, 3)
            V = (value @ Wv + bv).reshape(Bq, Lk, H, Dk).transpose(0, 2, 1, 3)
            if Lk > Lq:
                K = K[:, :, :Lq, :]
                V = V[:, :, :Lq, :]
            elif Lq > Lk:
                pad = [(0, 0), (0, 0), (0, Lq - Lk), (0, 0)]
                K = jnp.pad(K, pad)
                V = jnp.pad(V, pad)
            Lloc = Lq
            Qf = jnp.fft.rfft(Q, axis=2)
            Kf = jnp.fft.rfft(K, axis=2)
            corr = jnp.fft.irfft(Qf * jnp.conj(Kf), n=Lloc, axis=2)
            corr_mean = corr.mean(axis=-1)
            top_k = min(max(1, int(FACTOR * math.log(Lloc + 1))), Lloc)
            w, idx = jax.lax.top_k(corr_mean, top_k)
            w = jax.nn.softmax(w, axis=-1)
            ar = jnp.arange(Lloc)
            shifted = (ar[None, None, None, :] + idx[..., None]) % Lloc
            rolled = jnp.take_along_axis(V[:, :, None, :, :], shifted[..., None], axis=3)
            out = jnp.einsum('bhk,bhkld->bhld', w, rolled)
            out = out.transpose(0, 2, 1, 3).reshape(Bq, Lq, d)
            return out @ Wo + bo
        key = jax.random.key(seed)
        ks = jax.random.split(key, 12)
        s = 0.02
        inp = {'query': jax.random.normal(ks[0], (B, L, D_MODEL), dtype=jnp.float32), 'key': jax.random.normal(ks[1], (B, L, D_MODEL), dtype=jnp.float32), 'value': jax.random.normal(ks[2], (B, L, D_MODEL), dtype=jnp.float32), 'Wq': jax.random.normal(ks[3], (D_MODEL, D_MODEL), dtype=jnp.float32) * s, 'bq': jnp.zeros((D_MODEL,), dtype=jnp.float32), 'Wk': jax.random.normal(ks[4], (D_MODEL, D_MODEL), dtype=jnp.float32) * s, 'bk': jnp.zeros((D_MODEL,), dtype=jnp.float32), 'Wv': jax.random.normal(ks[5], (D_MODEL, D_MODEL), dtype=jnp.float32) * s, 'bv': jnp.zeros((D_MODEL,), dtype=jnp.float32), 'Wo': jax.random.normal(ks[6], (D_MODEL, D_MODEL), dtype=jnp.float32) * s, 'bo': jnp.zeros((D_MODEL,), dtype=jnp.float32)}
        return inp
    _L1_xattn_all = _L1_xattn_setup()
    _L1_xattn_in = {k: v for k, v in _L1_xattn_all.items() if k in ('Wq', 'bq', 'Wk', 'bk', 'Wv', 'bv', 'Wo', 'bo')}
    del _L1_xattn_all

    def _L1_ffn_setup():
        import jax, jax.numpy as jnp
        import numpy as np
        QMAX = 127.0

        def _ste_round(v):
            return v + jax.lax.stop_gradient(jnp.round(v) - v)

        def _act_fake_quant(x, clip_factor):
            scale = jax.nn.sigmoid(clip_factor) * jnp.max(jnp.abs(x)) / QMAX
            return jnp.clip(_ste_round(x / scale), -QMAX - 1.0, QMAX) * scale

        def _weight_fake_quant(w):
            scale = jnp.max(jnp.abs(w), axis=1, keepdims=True) / QMAX
            return jnp.clip(_ste_round(w / scale), -QMAX - 1.0, QMAX) * scale
        key = jax.random.key(seed)
        k1, k2, k3, k4 = jax.random.split(key, 4)
        B, S, H, I = (8, 2048, 256, 704)
        return {'x': jax.random.normal(k1, (B, S, H), dtype=jnp.float32), 'clip_x': jnp.full((1,), 4.0, dtype=jnp.float32), 'clip_down': jnp.full((1,), 4.0, dtype=jnp.float32), 'w_gate': jax.random.normal(k2, (I, H), dtype=jnp.float32) * 0.02, 'w_up': jax.random.normal(k3, (I, H), dtype=jnp.float32) * 0.02, 'w_down': jax.random.normal(k4, (H, I), dtype=jnp.float32) * 0.02}
    _L1_ffn_all = _L1_ffn_setup()
    _L1_ffn_in = {k: v for k, v in _L1_ffn_all.items() if k in ('clip_x', 'clip_down', 'w_gate', 'w_up', 'w_down')}
    del _L1_ffn_all
    return {'x': x, 'ctx_1024': ctx_1024, 'g_xattn': g_xattn, 'g_ffn': g_ffn, 'L0_xattn_Wq': _L0_xattn_in['Wq'], 'L0_xattn_Wk': _L0_xattn_in['Wk'], 'L0_xattn_Wv': _L0_xattn_in['Wv'], 'L0_xattn_Wo': _L0_xattn_in['Wo'], 'L0_ffn_wg': _L0_ffn_in['wg'], 'L0_ffn_w1': _L0_ffn_in['w1'], 'L0_ffn_b1': _L0_ffn_in['b1'], 'L0_ffn_w2': _L0_ffn_in['w2'], 'L0_ffn_b2': _L0_ffn_in['b2'], 'L1_xattn_Wq': _L1_xattn_in['Wq'], 'L1_xattn_bq': _L1_xattn_in['bq'], 'L1_xattn_Wk': _L1_xattn_in['Wk'], 'L1_xattn_bk': _L1_xattn_in['bk'], 'L1_xattn_Wv': _L1_xattn_in['Wv'], 'L1_xattn_bv': _L1_xattn_in['bv'], 'L1_xattn_Wo': _L1_xattn_in['Wo'], 'L1_xattn_bo': _L1_xattn_in['bo'], 'L1_ffn_clip_x': _L1_ffn_in['clip_x'], 'L1_ffn_clip_down': _L1_ffn_in['clip_down'], 'L1_ffn_w_gate': _L1_ffn_in['w_gate'], 'L1_ffn_w_up': _L1_ffn_in['w_up'], 'L1_ffn_w_down': _L1_ffn_in['w_down']}

def reference(x, ctx_1024, g_xattn, g_ffn, L0_xattn_Wq, L0_xattn_Wk, L0_xattn_Wv, L0_xattn_Wo, L0_ffn_wg, L0_ffn_w1, L0_ffn_b1, L0_ffn_w2, L0_ffn_b2, L1_xattn_Wq, L1_xattn_bq, L1_xattn_Wk, L1_xattn_bk, L1_xattn_Wv, L1_xattn_bv, L1_xattn_Wo, L1_xattn_bo, L1_ffn_clip_x, L1_ffn_clip_down, L1_ffn_w_gate, L1_ffn_w_up, L1_ffn_w_down):
    import jax
    import jax.numpy as jnp

    def _L0_xattn_ref(query, context, Wq, Wk, Wv, Wo):
        import jax, jax.numpy as jnp
        import numpy as np
        D_MODEL = 256
        N_HEADS = 16
        D_HEAD = D_MODEL // N_HEADS
        B, T_q, D = query.shape
        T_c = context.shape[1]
        Q = (query @ Wq.T).reshape(B, T_q, N_HEADS, D_HEAD)
        K = (context @ Wk.T).reshape(B, T_c, N_HEADS, D_HEAD)
        V = (context @ Wv.T).reshape(B, T_c, N_HEADS, D_HEAD)
        scale = jnp.sqrt(jnp.asarray(D_HEAD, dtype=query.dtype))
        scores = jnp.einsum('bqhd,bkhd->bhqk', Q, K) / scale
        attn = jax.nn.softmax(scores, axis=-1)
        out = jnp.einsum('bhqk,bkhd->bqhd', attn, V).reshape(B, T_q, D)
        return out @ Wo.T

    def _L0_ffn_ref(hidden_states, wg, w1, b1, w2, b2):
        import jax, jax.numpy as jnp
        import numpy as np
        B, T, M = hidden_states.shape
        E = wg.shape[1]
        S = B * T
        MIN_CAPACITY = 4
        C = max((S + E - 1) // E, MIN_CAPACITY)
        x = hidden_states.reshape(S, M)
        logits = x @ wg
        gates = jax.nn.softmax(logits, axis=-1)
        idx = jnp.argmax(gates, axis=-1)
        mask1 = jax.nn.one_hot(idx, E, dtype=gates.dtype)
        l_aux = jnp.sum(gates.mean(0) * mask1.mean(0)) * E
        locations1 = jnp.cumsum(mask1, axis=0) - 1.0
        mask1 = mask1 * (locations1 < C)
        gates1_s = jnp.sum(gates * mask1, axis=1)
        loc_s = jnp.sum(locations1 * mask1, axis=1).astype(jnp.int32)
        loc_sc = jax.nn.one_hot(loc_s, C, dtype=gates.dtype)
        combine_weights = jnp.einsum('se,sc->sec', gates1_s[:, None] * mask1, loc_sc)
        dispatch_mask = (combine_weights > 0).astype(x.dtype)
        dispatched = jnp.einsum('sec,sm->ecm', dispatch_mask, x)
        h = jax.nn.gelu(jnp.einsum('ecm,emf->ecf', dispatched, w1) + b1[:, None, :])
        expert_out = jnp.einsum('ecf,efm->ecm', h, w2) + b2[:, None, :]
        out = jnp.einsum('sec,ecm->sm', combine_weights, expert_out)
        return out.reshape(B, T, M)

    def _L1_xattn_ref(query, key, value, Wq, bq, Wk, bk, Wv, bv, Wo, bo):
        import jax, jax.numpy as jnp
        import numpy as np
        import math
        D_MODEL = 256
        NHEAD = 16
        FACTOR = 1
        B, L = (2, 1024)

        def _autocorr_forward(query, key, value, Wq, bq, Wk, bk, Wv, bv, Wo, bo):
            Bq, Lq, d = query.shape
            Lk = key.shape[1]
            H = NHEAD
            Dk = d // H
            Q = (query @ Wq + bq).reshape(Bq, Lq, H, Dk).transpose(0, 2, 1, 3)
            K = (key @ Wk + bk).reshape(Bq, Lk, H, Dk).transpose(0, 2, 1, 3)
            V = (value @ Wv + bv).reshape(Bq, Lk, H, Dk).transpose(0, 2, 1, 3)
            if Lk > Lq:
                K = K[:, :, :Lq, :]
                V = V[:, :, :Lq, :]
            elif Lq > Lk:
                pad = [(0, 0), (0, 0), (0, Lq - Lk), (0, 0)]
                K = jnp.pad(K, pad)
                V = jnp.pad(V, pad)
            Lloc = Lq
            Qf = jnp.fft.rfft(Q, axis=2)
            Kf = jnp.fft.rfft(K, axis=2)
            corr = jnp.fft.irfft(Qf * jnp.conj(Kf), n=Lloc, axis=2)
            corr_mean = corr.mean(axis=-1)
            top_k = min(max(1, int(FACTOR * math.log(Lloc + 1))), Lloc)
            w, idx = jax.lax.top_k(corr_mean, top_k)
            w = jax.nn.softmax(w, axis=-1)
            ar = jnp.arange(Lloc)
            shifted = (ar[None, None, None, :] + idx[..., None]) % Lloc
            rolled = jnp.take_along_axis(V[:, :, None, :, :], shifted[..., None], axis=3)
            out = jnp.einsum('bhk,bhkld->bhld', w, rolled)
            out = out.transpose(0, 2, 1, 3).reshape(Bq, Lq, d)
            return out @ Wo + bo
        return _autocorr_forward(query, key, value, Wq, bq, Wk, bk, Wv, bv, Wo, bo)

    def _L1_ffn_ref(x, clip_x, clip_down, w_gate, w_up, w_down):
        import jax, jax.numpy as jnp
        import numpy as np
        QMAX = 127.0

        def _ste_round(v):
            return v + jax.lax.stop_gradient(jnp.round(v) - v)

        def _act_fake_quant(x, clip_factor):
            scale = jax.nn.sigmoid(clip_factor) * jnp.max(jnp.abs(x)) / QMAX
            return jnp.clip(_ste_round(x / scale), -QMAX - 1.0, QMAX) * scale

        def _weight_fake_quant(w):
            scale = jnp.max(jnp.abs(w), axis=1, keepdims=True) / QMAX
            return jnp.clip(_ste_round(w / scale), -QMAX - 1.0, QMAX) * scale
        xq = _act_fake_quant(x, clip_x[0])
        gate = jnp.einsum('bsh,ih->bsi', xq, _weight_fake_quant(w_gate))
        up = jnp.einsum('bsh,ih->bsi', xq, _weight_fake_quant(w_up))
        h = _act_fake_quant(jax.nn.silu(gate) * up, clip_down[0])
        return jnp.einsum('bsi,hi->bsh', h, _weight_fake_quant(w_down))
    x = x + jnp.tanh(g_xattn[0]) * _L0_xattn_ref(_layernorm(x, axis=-1), ctx_1024, L0_xattn_Wq, L0_xattn_Wk, L0_xattn_Wv, L0_xattn_Wo)
    x = x + jnp.tanh(g_ffn[0]) * _L0_ffn_ref(_layernorm(x, axis=-1), L0_ffn_wg, L0_ffn_w1, L0_ffn_b1, L0_ffn_w2, L0_ffn_b2)
    x = x + jnp.tanh(g_xattn[1]) * _L1_xattn_ref(_layernorm(x, axis=-1), ctx_1024, ctx_1024, L1_xattn_Wq, L1_xattn_bq, L1_xattn_Wk, L1_xattn_bk, L1_xattn_Wv, L1_xattn_bv, L1_xattn_Wo, L1_xattn_bo)
    x = x + jnp.tanh(g_ffn[1]) * _L1_ffn_ref(_layernorm(x, axis=-1), L1_ffn_clip_x, L1_ffn_clip_down, L1_ffn_w_gate, L1_ffn_w_up, L1_ffn_w_down)
    return x

_drawn_inputs = setup_inputs


def setup_inputs(seed=0):
    import zlib

    import numpy as np

    out = dict(_drawn_inputs(seed))
    spreads = {'g_ffn': (-1.0, 0.6),
     'L0_ffn_b1': (0.0, 0.439),
     'L0_ffn_b2': (0.0, 0.309),
     'L1_xattn_bq': (0.0, 0.8),
     'L1_xattn_bk': (0.0, 0.517),
     'L1_xattn_bv': (0.0, 0.698),
     'L1_xattn_bo': (0.0, 0.1)}
    factors = {}
    for name, (base, spread) in spreads.items():
        noise = np.random.default_rng([zlib.crc32(name.encode()), seed]).standard_normal(out[name].shape)
        drawn = base * np.exp(spread * noise) if base else spread * noise
        out[name] = jnp.asarray(drawn.astype(out[name].dtype))
    for name, factor in factors.items():
        out[name] = (out[name] * factor).astype(out[name].dtype)
    return out
```

```python
from contextlib import ExitStack

import numpy as np

import concourse.bass as bass
from concourse import mybir

F32 = mybir.dt.float32
BF16 = mybir.dt.bfloat16
U32 = mybir.dt.uint32
ALU = mybir.AluOpType
ACT = mybir.ActivationFunctionType
AX_X = mybir.AxisListType.X
ABSMAX = bass.bass_isa.ReduceOp.absmax

P = 128
B, TQ, D = 8, 256, 256
TC = 77
H, DH = 16, 16
DK = D // P
NT = B * TQ // P
E, F = 8, 1024
FK = F // P
CAP = B * TQ // E
SLOTS = E * CAP
I = 704
IK = (I + P - 1) // P
TAIL = I - (IK - 1) * P
NB = 512
TOPK = 5
EPS = 1e-5
QMAX = 127.0
MAGIC = 1.5 * 2.0 ** 23
SH = 6
HG = 4


class Round:

    def __init__(self, i, off, count):
        self.i, self.off, self.count = i, off, count
        self.parity = off % 2
        self.static = isinstance(i, int)
        self.n = 2 * i + off if self.static else i * 2 + off

    def shift(self, k):
        return Round(self.i, self.off + k, self.count)

    @property
    def valid(self):
        return not self.static or 0 <= self.n < self.count

    @property
    def half(self):
        return self.i + self.off // 2


class Stage:

    def __init__(self, sem, per):
        self.sem, self.per = sem, per

    def at(self, r, step=None):
        return r.n * self.per + (self.per if step is None else step)


def rounds(eng, body, count, first, last, lo, hi):
    for n in range(first, 2 * lo):
        body(Round(0, n, count))
    with eng.Fori(lo, hi) as i:
        body(Round(i, 0, count))
        body(Round(i, 1, count))
    for n in range(2 * hi, last + 1):
        body(Round(0, n, count))


def build(nc, a, out):
    with ExitStack() as ctx:
        def sb(name, shape, dt=F32):
            return ctx.enter_context(nc.sbuf_tensor(name, shape, dt))

        def sem(name):
            return ctx.enter_context(nc.semaphore(name))

        def stage(name, per):
            return Stage(sem(name), per)

        def carve(base, shapes):
            at, out = 0, []
            for shape in shapes:
                size = int(np.prod(shape))
                axes = "abcd"[:len(shape)]
                v = base[:, at:at + size]
                if len(shape) > 1:
                    v = v.rearrange(f"p ({' '.join(axes)}) -> p {' '.join(axes)}", **dict(zip(axes, shape)))
                out.append(v)
                at += size
            assert at <= base.shape[1], (at, base.shape)
            return out

        pool = sb("pool", [P, 9 * 2048])
        (kbd, prob, probT, k0T, xnT, qT, ao, aoT, x2T, zeros) = carve(pool, [
            (2, DK, P // DH, TC),
            (2, H, TC), (2, H, P), (DK, B * TC), (DK, TQ), (2, DK, TQ), (2, D), (2, DK, P), (2, DK, P), (1024,)])
        probT = probT[0:TC]
        (hid, yex, yg, KVF, wdTw) = carve(pool, [
            (2, FK, CAP), (2, CAP // P, D),
            (NT, D),
            (B, 2, 2 * D),
            (IK * D // 2,)])
        wdT = wdTw.bitcast(BF16).rearrange("p (m d) -> p m d", m=IK)
        hT = pool[:, 0:IK * B * TQ].rearrange("p (m s) -> p m s", m=IK)
        wbuf = sb("wbuf", [P, 4 * DK * F])
        w1, w2 = carve(wbuf, [(2, DK, F), (2, FK, D)])
        (xh, prod, corr, wts, wtT, wf, u1, u2, of, oT) = carve(wbuf, [
            (2, DK, TQ), (4, D), (TQ,), (TOPK, TQ), (DK, P), (4, P), (2, D), (2, D), (2, DK, D), (2, DK, TQ)])
        hr, hqw = carve(wbuf, [(2, IK, TQ), (2 * IK * TQ // 2,)])
        hq = hqw.bitcast(BF16).rearrange("p (u m s) -> p u m s", u=2, m=IK)
        w0b = sb("w0b", [P, 4 * DK * D])
        w0, = carve(w0b, [(4, DK, D)])
        wgT = w0b[:, 0:DK * I].bitcast(BF16).rearrange("p (g k i) -> p g k i", g=2, k=DK)
        w1b = sb("w1b", [P, 4 * DK * D])
        w1a, = carve(w1b, [(4, DK, D)])
        xqT = w1b[:].bitcast(BF16).rearrange("p (k s) -> p k s", k=DK)

        x = sb("x", [P, NT, D])
        ctxT = sb("ctxT", [P, DK, B * TC])
        ctxb = sb("ctxb", [P, 2, DK, TC])
        wg = sb("wg", [P, DK, E])
        ident = sb("ident", [P, P])
        identb = sb("identb", [P, P], BF16)
        onesf = sb("onesf", [P, P])
        onesb = sb("onesb", [P, P], BF16)
        trib = sb("trib", [P, P], BF16)
        headmask = sb("headmask", [P, P // DH])
        iota8 = sb("iota8", [P, E])
        iotaT = sb("iotaT", [P, TQ])
        mhalf = sb("mhalf", [P, 2])
        epsc = sb("epsc", [P, 2])
        gates4 = sb("gates4", [P, 4])
        clips = sb("clips", [P, 2])
        clipr = sb("clipr", [P, 2])
        bkv = sb("bkv", [TC, 2 * D])
        bq = sb("bq", [1, D])
        bo = sb("bo", [P, D])
        b1 = sb("b1", [P, E * FK])
        dft = sb("dft", [P, DK, TQ])
        idft = sb("idft", [P, DK, TQ])
        corrm = sb("corrm", [P, 4, TQ])
        wdft = sb("wdft", [P, 4, DK, P])
        dcrow = sb("dcrow", [1, P])

        st = sb("st", [P, 2, 6])
        mv = sb("mv", [P, 2, 2])
        vare = sb("vare", [P, 2])
        rstd = sb("rstd", [P, 2])
        st2 = sb("st2", [P, 2, 6])
        mv2 = sb("mv2", [P, 2, 2])
        vare2 = sb("vare2", [P, 2])
        rstd2 = sb("rstd2", [P, 2])
        xn = sb("xn", [P, 2, 2, D])
        xn2 = sb("xn2", [P, 2, 2, D])
        v0 = sb("v0", [TC, 2, H, DH + 1])
        mx = sb("mx", [P, 2, H])
        rden = sb("rden", [P, 2, H])
        top = sb("top", [P, 2, 8])
        topi = sb("topi", [P, 2, 8], U32)
        eidx = sb("eidx", [P, 2, 2])
        ntop = sb("ntop", [P, 2])
        mask = sb("mask", [P, 2, 2, E], BF16)
        seen = sb("seen", [P, 2, E], BF16)
        seen1 = sb("seen1", [P, E])
        gexp = sb("gexp", [P, 2, E])
        gsum = sb("gsum", [P, 2])
        lm = sb("lm", [P, 2, E])
        pos = sb("pos", [P, 2])
        slot = sb("slot", [P, 2])
        keep = sb("keep", [P, 2])
        skip = sb("skip", [P, 2])
        grec = sb("grec", [P, 2])
        slots = sb("slots", [P, 2, 2], U32)
        slotg = sb("slotg", [P, NT], U32)
        gk = sb("gk", [P, NT])
        b2 = sb("b2", [P, 2, D])
        dsp = sb("dsp", [P, 2, CAP // P, D])
        dspT = sb("dspT", [P, 2, DK, CAP])
        kv = sb("kv", [TC, 2, 2 * D])
        pc = sb("pc", [P, 4, B, H])
        c8 = sb("c8", [P, 8])
        ci = sb("ci", [P, 8], U32)
        cif = sb("cif", [P, 8])
        nc0 = sb("nc0", [P, 1])
        cw = sb("cw", [P, TOPK])
        cs = sb("cs", [P, 1])
        cr = sb("cr", [P, 1])
        amax = sb("amax", [P, NT])
        am1 = sb("am1", [P, 1])
        am2 = sb("am2", [P, 1])
        sx = sb("sx", [P, 2])
        wnat = sb("wnat", [P, IK, D])
        wab = sb("wab", [P, IK])
        wrec = sb("wrec", [P, IK])
        wsc = sb("wsc", [P, 3, IK])
        wq = sb("wq", [P, IK, D], BF16)
        hmaxs = sb("hmaxs", [P, IK * B * TQ // NB])
        sgu = sb("sgu", [P, 2, IK])
        diag = sb("diag", [P, DK, P])
        dscale = sb("dscale", [P, D])
        xq = sb("xq", [P, 2, 2, D], BF16)

        ps = ctx.enter_context(nc.psum_tensor("ps", [P, 8, 512], F32))

        disp = nc.dram_tensor("dispatched", [SLOTS, D], F32, kind="Internal").ap()
        yexp = nc.dram_tensor("expert_rows", [SLOTS, D], F32, kind="Internal").ap()

        ld = {n: sem("loaded_" + n) for n in (
            "x0", "x1", "w0", "w1a", "ctxT", "small", "b1", "bias", "dft", "idft", "corrm", "wdft", "wnat0", "wnat1", "wnat2")}
        ldw1 = [sem(f"loaded_w1_{u}") for u in range(2)]
        ldw2 = [sem(f"loaded_w2_{u}") for u in range(2)]
        ldb2 = [sem(f"loaded_b2_{u}") for u in range(2)]
        lddsp = [sem(f"loaded_dispatched_{u}") for u in range(2)]
        zeroed = sem("dispatched_zeroed")
        scat = [[sem(f"scattered_{u}{t}") for t in range(2)] for u in range(2)]
        stored = [sem(f"expert_rows_stored_{u}") for u in range(2)]
        gath = [sem(f"gathered_{t % 2}{t // 2}") for t in range(NT)]
        outs = sem("out_stored")
        passed = sem("waits_passed")
        wtail = sem("weights_tail_set")

        consts = stage("consts_ready", 1)
        tan = stage("gates_tanh", 1)
        ln1, rs1 = stage("ln1", 6), stage("ln1_rstd", 2)
        cb, kb = stage("ctx_batch_copied", 1), stage("keys_block_diagonal", 1)
        pk0, ek0 = stage("k0T_product", 1), stage("k0T_copied", 1)
        pA, eA = stage("xT_v_q_product", 3), stage("xT_v_q_copied", 3)
        pS, ms, ex = stage("scores", 2), stage("scores_less_max", 4), stage("probabilities", 2)
        pPT, ePT, pAV = stage("prob_transposed", 8), stage("probT_copied", 8), stage("attended", 2)
        nv = stage("attended_normalised", 4)
        pOT, eOT, pWO, x1s = stage("ao_transposed", 2), stage("aoT_copied", 2), stage("ao_projected", 2), stage("x1", 2)
        ln2, rs2 = stage("ln2", 6), stage("ln2_rstd", 2)
        pX2, eX2, pLG = stage("x2_transposed", 2), stage("x2T_copied", 2), stage("router_logits", 1)
        ga, gx, pLOC, sl = stage("chosen", 9), stage("gate_exp", 2), stage("positions", 1), stage("slots_known", 11)
        pD, eD = stage("dsp_transposed", 1), stage("dspT_copied", 1)
        pG1, gl, pG2, ye = stage("hidden_product", 4), stage("hidden_gelu", 8), stage("expert_product", 1), stage("expert_rows", 1)
        cb2, pKV, eKV, pKF, eKF = stage("ctx_batch2", 1), stage("kv_product", 1), stage("kv_biased", 1), stage("kv_spectrum", 1), stage("kv_spectrum_copied", 2)
        x2s, ln3, rs3, x2b = stage("x2", 2), stage("ln3", 6), stage("ln3_rstd", 2), stage("x2_bias", 1)
        pXH, eXH, pQF, pr = stage("xn_spectrum", 1), stage("xn_spectrum_copied", 1), stage("q_spectrum", 1), stage("spectra_products", 4)
        pCO, tk, tx, pWT, eWT, pWF, eWF = (stage("correlation", 1), stage("delays", 16), stage("delays_exp", 1), stage("delays_transposed", 1),
                                          stage("delaysT_copied", 1), stage("delay_spectra", 1), stage("delay_spectra_copied", 1))
        uu, uf, pOI, eOI, pY, x3s = stage("rolled_parts", 1), stage("rolled_spectrum", 1), stage("rolled_time", 1), stage("rolled_copied", 1), stage("rolled_projected", 1), stage("x3", 1)
        ln4, rs4 = stage("ln4", 8), stage("ln4_rstd", 2)
        bosc = sem("bias_scaled")
        wp, pwp, ewp = sem("weights_quantised"), sem("weights_transposed"), sem("weightsT_copied")
        sc, arx = sem("activation_scale"), sem("activation_max_all")
        xqs, pXQ, eXQ = stage("x_quantised", 3), stage("xq_transposed", 1), stage("xqT_copied", 1)
        pGU, si, hh = stage("gate_up_product", IK), stage("gate_silu", IK), stage("hidden_gated", IK)
        hmx, arh, hqs = sem("hidden_max"), sem("hidden_max_all"), stage("hidden_quantised", 3)
        sch = sem("hidden_scale")
        pDN, dns, fin = stage("down_product", 1), stage("down_scaled", 1), stage("final", 1)


        sil = xn2[:].rearrange("p u t d -> p u (t d)")

        block = ctx.enter_context(nc.Block())

        def alone(eng):
            eng.sem_inc(passed, 1)

        @block.sync
        def _(sp):
            xv = a["x"].rearrange("(t p) d -> p t d", p=P)
            sp.dma_start(x[:, 0:4, :], xv[:, 0:4, :]).then_inc(ld["x0"], 16)
            sp.dma_start(ctxT[:], a["ctxT"]).then_inc(ld["ctxT"], 16)
            sp.dma_start(w0[:], a["w0"]).then_inc(ld["w0"], 16)
            sp.dma_start(x[:, 4:NT, :], xv[:, 4:NT, :]).then_inc(ld["x1"], 16)
            for dst, src in ((wg[:], a["wg"]), (gates4[:], a["gates"].partition_broadcast(P)), (clips[:], a["clips"].partition_broadcast(P))):
                sp.dma_start(dst, src).then_inc(ld["small"], 16)
            sp.dma_start(b1[:], a["b1"]).then_inc(ld["b1"], 16)
            for e in range(2):
                sp.dma_start(w1[:, e], a["w1"][e]).then_inc(ldw1[e], 16)
                sp.dma_start(w2[:, e], a["w2"][e]).then_inc(ldw2[e], 16)
                sp.dma_start(b2[:, e], a["b2"][e].partition_broadcast(P)).then_inc(ldb2[e], 16)
            sp.dma_start(w1a[:], a["w1a"]).then_inc(ld["w1a"], 16)
            sp.dma_start(dft[:], a["dft"]).then_inc(ld["dft"], 16)
            sp.dma_start(idft[:], a["idft"]).then_inc(ld["idft"], 16)
            sp.dma_start(corrm[:], a["corrm"]).then_inc(ld["corrm"], 16)
            sp.dma_start(wdft[:], a["wdft"]).then_inc(ld["wdft"], 16)
            for dst, src in ((bkv[:], a["bkv"].partition_broadcast(TC)), (bq[:], a["bq"]), (bo[:], a["bo"].partition_broadcast(P)), (dcrow[:], a["dcrow"])):
                sp.dma_start(dst, src).then_inc(ld["bias"], 16)
            for u in range(2):
                for t in range(2):
                    sp.wait_ge(scat[u][t], 16 * (B // 2))
            dv = disp.rearrange("(e t p) d -> e p t d", e=E, p=P)
            yv = yexp.rearrange("(e t p) d -> e p t d", e=E, p=P)

            def load_dsp(r):
                sp.dma_start(dsp[:, r.parity], dv[r.n]).then_inc(lddsp[r.parity], 16)

            def body(r):
                nx = r.shift(2)
                if nx.valid:
                    sp.wait_ge(pD.sem, pD.at(r))
                    load_dsp(nx)
                    sp.wait_ge(pG1.sem, pG1.at(r))
                    sp.dma_start(w1[:, r.parity], a["w1"][nx.n]).then_inc(ldw1[r.parity], 16)
                sp.wait_ge(ye.sem, ye.at(r))
                sp.dma_start(yv[r.n], yex[:, r.parity]).then_inc(stored[r.parity], 16)
                if nx.valid:
                    sp.dma_start(w2[:, r.parity], a["w2"][nx.n]).then_inc(ldw2[r.parity], 16)
                    sp.dma_start(b2[:, r.parity], a["b2"][nx.n].partition_broadcast(P)).then_inc(ldb2[r.parity], 16)

            load_dsp(Round(0, 0, E))
            load_dsp(Round(0, 1, E))
            rounds(sp, body, E, 0, E - 1, 0, (E - 2) // 2)
            sp.wait_ge(wtail, 1)
            for m, n in enumerate(("wnat0", "wnat1")):
                if m == 1:
                    sp.wait_ge(wp, 5)
                sp.dma_start(wnat[:, 0:IK - 1, :], a["wgu"][m, 0:P * (IK - 1), :].rearrange("(m p) d -> p m d", p=P)).then_inc(ld[n], 16)
                sp.dma_start(wnat[0:TAIL, IK - 1, :], a["wgu"][m, P * (IK - 1):I, :]).then_inc(ld[n], 16)
            sp.wait_ge(wp, 10)
            sp.dma_start(wnat[:].rearrange("p m d -> p (m d)")[:, 0:2 * I].rearrange("p (h i) -> p h i", h=2),
                         a["wd"].rearrange("(h p) i -> p h i", p=P)).then_inc(ld["wnat2"], 16)
            ov = out.rearrange("(b t p) d -> b p t d", t=2, p=P)

            def store(r):
                sp.wait_ge(fin.sem, fin.at(r))
                sp.dma_start(ov[r.n], x[:, bass.ds(r.n * 2, 2), :]).then_inc(outs, 16)
            rounds(sp, store, B, 0, B - 1, 0, B // 2)
            sp.wait_ge(outs, 16 * B)

        @block.gpsimd
        def _(gp):
            c = 0

            def const(ins):
                nonlocal c
                c += 1
                ins.then_inc(consts.sem, 1)

            const(gp.memset(zeros[:], 0.0))
            const(gp.memset(ident[:], 0.0))
            const(gp.memset(headmask[:], 1.0))
            const(gp.memset(mhalf[:], -0.5))
            const(gp.memset(epsc[:], EPS))
            const(gp.memset(onesf[:], 1.0))
            const(gp.memset(onesb[:], 1.0))
            const(gp.memset(v0[:], 1.0))
            const(gp.memset(seen[:], 0.0))
            const(gp.iota(iota8[:], [[1, E]], base=0, channel_multiplier=0, allow_small_or_imprecise_dtypes=True))
            const(gp.iota(iotaT[:], [[1, TQ]], base=0, channel_multiplier=0, allow_small_or_imprecise_dtypes=True))
            gp.wait_ge(consts.sem, c)
            for e in range(SLOTS * D // (P * 1024)):
                gp.dma_start(disp.rearrange("(e p t) d -> e p (t d)", p=P, t=4)[e], zeros[:]).then_inc(zeroed, 16)
            const(gp.affine_select(out=ident[:], in_=ident[:], compare_op=ALU.not_equal, fill=1.0, base=0, pattern=[[-1, P]], channel_multiplier=1))
            const(gp.affine_select(out=trib[:], in_=onesb[:], compare_op=ALU.is_ge, fill=0.0, base=0, pattern=[[1, P]], channel_multiplier=-1))
            const(gp.affine_select(out=headmask[:], in_=headmask[:], compare_op=ALU.is_ge, fill=0.0, base=0, pattern=[[-DH, P // DH]], channel_multiplier=1))
            gp.wait_ge(consts.sem, c)
            const(gp.affine_select(out=headmask[:], in_=headmask[:], compare_op=ALU.is_ge, fill=0.0, base=DH - 1, pattern=[[DH, P // DH]], channel_multiplier=-1))
            const(gp.tensor_copy(identb[:], ident[:]))
            assert c == CONSTS
            gp.wait_ge(consts.sem, c)

            def rstd_of(r, ln, rs, step, m, v, o):
                gp.wait_ge(ln.sem, ln.at(r, step))
                gp.tensor_tensor(v[:], m[:, :, 1], epsc[:], ALU.add).then_inc(rs.sem, 1)
                gp.wait_ge(rs.sem, rs.at(r, 1))
                gp.tensor_tensor(o[:], v[:], mhalf[:], ALU.pow).then_inc(rs.sem, 1)

            def keys(r):
                if r.shift(-2).valid:
                    gp.wait_ge(pA.sem, pA.at(r.shift(-2), 2))
                gp.tensor_copy(ctxb[:, r.parity], ctxT[:, :, bass.ds(r.n * TC, TC)]).then_inc(cb.sem, 1)
                if r.shift(-2).valid:
                    gp.wait_ge(pS.sem, pS.at(r.shift(-2)))
                for k in range(DK):
                    ins = gp.tensor_tensor(kbd[:, r.parity, k], k0T[:, k, None, bass.ds(r.n * TC, TC)].broadcast_to([P, P // DH, TC]),
                                           headmask[:, :, None].broadcast_to([P, P // DH, TC]), ALU.mult)
                ins.then_inc(kb.sem, 1)

            def scatter(r):
                gp.wait_ge(sl.sem, sl.at(r))
                alone(gp)
                for t in range(2):
                    gp.indirect_dma_start(out=disp, out_offset=bass.IndirectOffsetOnAxis(ap=slots[:, r.parity, t:t + 1], axis=0),
                                          in_=xn2[:, r.parity, t, :], in_offset=None, bounds_check=SLOTS - 1,
                                          oob_is_err=False).then_inc(scat[r.parity][t], 16)

            gp.wait_ge(ld["ctxT"], 16)
            gp.wait_ge(ek0.sem, 4)
            rstd_of(Round(0, 0, B), ln1, rs1, 4, mv, vare, rstd)
            keys(Round(0, 0, B))
            rstd_of(Round(0, 1, B), ln1, rs1, 4, mv, vare, rstd)
            gp.wait_ge(zeroed, 16 * (SLOTS * D // (P * 1024)))

            def body(r):
                if r.shift(1).valid:
                    keys(r.shift(1))
                if r.shift(-1).valid:
                    rstd_of(r.shift(-1), ln2, rs2, 4, mv2, vare2, rstd2)
                if r.shift(2).valid:
                    rstd_of(r.shift(2), ln1, rs1, 4, mv, vare, rstd)
                if r.shift(-1).valid:
                    scatter(r.shift(-1))
            rounds(gp, body, B, 0, B, 1, 3)

            def ctx2(r):
                if r.shift(-2).valid:
                    gp.wait_ge(pKV.sem, pKV.at(r.shift(-2)))
                else:
                    gp.wait_ge(pA.sem, pA.at(Round(0, B - 1, B), 2))
                gp.tensor_copy(ctxb[:, r.parity], ctxT[:, :, bass.ds(r.n * TC, TC)]).then_inc(cb2.sem, 1)
            rounds(gp, ctx2, B, 0, B - 1, 1, B // 2)

            gp.wait_ge(tan.sem, 2)
            gp.wait_ge(ld["bias"], 64)
            gp.tensor_scalar(bo[:], bo[:], gates4[:, 1:2], None, ALU.mult).then_inc(bosc, 1)
            for u in range(2):
                gp.wait_ge(stored[u], 16 * (E // 2))
            for t in range(NT):
                gp.indirect_dma_start(out=yg[:, t, :], out_offset=None, in_=yexp,
                                      in_offset=bass.IndirectOffsetOnAxis(ap=slotg[:, t:t + 1], axis=0)).then_inc(gath[t], 16)
            gp.wait_ge(bosc, 1)

            def body3(r):
                rstd_of(r, ln3, rs3, 4, mv, vare, rstd)
                gp.wait_ge(ln3.sem, ln3.at(r))
                gp.tensor_tensor(x[:, bass.ds(r.n * 2, 2), :], x[:, bass.ds(r.n * 2, 2), :],
                                 bo[:, None, :].broadcast_to([P, 2, D]), ALU.add).then_inc(x2b.sem, 1)
            rounds(gp, body3, B, 0, B - 1, 0, B // 2)

            def body4(r):
                rstd_of(r, ln4, rs4, 4, mv2, vare2, rstd2)
            rounds(gp, body4, B, 0, B - 1, 0, B // 2)
            gp.wait_ge(sc, 1)
            gp.partition_all_reduce(am2[:], am1[:], P, ABSMAX).then_inc(arx, 1)
            gp.wait_ge(hmx, IK * (B * TQ // NB) + 2)
            gp.partition_all_reduce(am2[:], am1[:], P, ABSMAX).then_inc(arh, 1)

            def last(r):
                gp.wait_ge(dns.sem, dns.at(r))
                gp.tensor_tensor(x[:, bass.ds(r.n * 2, 2), :], x[:, bass.ds(r.n * 2, 2), :], xn[:, r.parity], ALU.add).then_inc(fin.sem, 1)
            rounds(gp, last, B, 0, B - 1, 0, B // 2)

        @block.tensor
        def _(pe):
            ring = (ps[:, 4], ps[:, 5])

            def mm(o, l, r, k, n):
                return pe.matmul(o, l, r, start=(k == 0), stop=(k == n - 1))

            def k0():
                pe.wait_ge(ld["ctxT"], 16)
                pe.wait_ge(ld["w0"], 16)
                for c in range(DK):
                    for n in range(2):
                        cols = slice(n * B * TC // 2, (n + 1) * B * TC // 2)
                        for k in range(DK):
                            ins = mm(ps[:, 2 * c + n, 0:B * TC // 2], w0[:, 1, k, c * P:(c + 1) * P], ctxT[:, k, cols], k, DK)
                        ins.then_inc(pk0.sem, 1)

            def proj(r):
                pe.wait_ge(ln1.sem, ln1.at(r))
                prev = r.shift(-1)
                if prev.valid:
                    pe.wait_ge(ePT.sem, ePT.at(prev, 3))
                for t in range(2):
                    for k in range(DK):
                        ins = pe.transpose(ring[0][:, k * TQ + t * P:k * TQ + (t + 1) * P], xn[:, r.parity, t, k * P:(k + 1) * P], ident[:])
                ins.then_inc(pA.sem, 1)
                pe.wait_ge(cb.sem, cb.at(r))
                if r.shift(-2).valid:
                    pe.wait_ge(eOT.sem, eOT.at(r.shift(-2), 2))
                for k in range(DK):
                    ins = mm(ps[0:TC, 7, 0:D], ctxb[:, r.parity, k], w0[:, 2, k], k, DK)
                ins.then_inc(pA.sem, 1)
                pe.wait_ge(eA.sem, eA.at(r, 1))
                if prev.valid:
                    pe.wait_ge(ePT.sem, ePT.at(prev, 4))
                for c in range(DK):
                    for k in range(DK):
                        ins = mm(ring[1][:, c * TQ:(c + 1) * TQ], w0[:, 0, k, c * P:(c + 1) * P], xnT[:, k], k, DK)
                ins.then_inc(pA.sem, 1)

            def scores(r, t):
                pe.wait_ge(eA.sem, eA.at(r))
                pe.wait_ge(kb.sem, kb.at(r))
                p = r if t else r.shift(-1)
                if p.valid:
                    pe.wait_ge(ms.sem, ms.at(p, 2 if t else 4))
                for h0, h1 in ((0, 6), (6, 8), (8, 12), (12, 16)):
                    c, n = h0 // 8, h0 // SH
                    ins = pe.matmul(ps[:, n, (h0 - n * SH) * TC:(h1 - n * SH) * TC], qT[:, r.parity, c, t * P:(t + 1) * P],
                                    kbd[:, r.parity, c, h0 - 8 * c:h1 - 8 * c, :].rearrange("p h k -> p (h k)"), start=True, stop=True)
                ins.then_inc(pS.sem, 1)

            def attend(r, t):
                pe.wait_ge(ex.sem, ex.at(r, t + 1))

                def turn(g):
                    if g >= 2:
                        pe.wait_ge(ePT.sem, ePT.at(r, 4 * t + g - 1))
                    elif t:
                        if r.shift(1).valid:
                            pe.wait_ge(eA.sem, eA.at(r.shift(1), 1 + 2 * g))
                        else:
                            pe.wait_ge(ePT.sem, ePT.at(r, 3 + g))
                    elif r.shift(-1).valid:
                        pe.wait_ge(ePT.sem, ePT.at(r.shift(-1), 7 + g))
                    else:
                        pe.wait_ge(eA.sem, eA.at(r))
                    for h in range(HG):
                        ins = pe.transpose(ring[g % 2][0:TC, h * P:(h + 1) * P], prob[:, t, g * HG + h], ident[:])
                    ins.then_inc(pPT.sem, 1)

                def values(g):
                    pe.wait_ge(ePT.sem, ePT.at(r, 4 * t + g + 1))
                    for h in range(g * HG, (g + 1) * HG):
                        ins = pe.matmul(ps[:, 6, h * (DH + 1):(h + 1) * (DH + 1)], probT[:, t, h], v0[:, r.parity, h], start=True, stop=True)
                    return ins

                turn(0)
                turn(1)
                turn(2)
                p = r if t else r.shift(-1)
                if p.valid:
                    pe.wait_ge(nv.sem, nv.at(p, 2 if t else 4))
                pe.wait_ge(eA.sem, eA.at(r, 2))
                values(0)
                turn(3)
                values(1)
                values(2)
                values(3).then_inc(pAV.sem, 1)

            def turn_out(r, t):
                pe.wait_ge(nv.sem, nv.at(r, 2 * t + 2))
                if t == 0 and r.shift(1).valid:
                    pe.wait_ge(eA.sem, eA.at(r.shift(1), 2))
                if t == 1 and r.shift(-1).valid:
                    pe.wait_ge(eX2.sem, eX2.at(r.shift(-1), 2))
                for k in range(DK):
                    ins = pe.transpose(ps[:, 7, k * P:(k + 1) * P], ao[:, t, k * P:(k + 1) * P], ident[:])
                ins.then_inc(pOT.sem, 1)

            def project(r, t):
                pe.wait_ge(eOT.sem, eOT.at(r, t + 1))
                if t and r.shift(-1).valid:
                    pe.wait_ge(sl.sem, sl.at(r.shift(-1), 1))
                if not t and r.shift(-1).valid:
                    pe.wait_ge(gx.sem, gx.at(r.shift(-1)))
                if t and not r.shift(-1).valid:
                    pe.wait_ge(x1s.sem, x1s.at(r, 1))
                for k in range(DK):
                    ins = mm(ps[:, 3, 0:D], aoT[:, t, k], w0[:, 3, k], k, DK)
                ins.then_inc(pWO.sem, 1)

            def router(r):
                pe.wait_ge(ln2.sem, ln2.at(r))
                for t in range(2):
                    if t == 1:
                        pe.wait_ge(eX2.sem, eX2.at(r, 1))
                    elif r.shift(1).valid:
                        pe.wait_ge(eOT.sem, eOT.at(r.shift(1), 1))
                    for k in range(DK):
                        ins = pe.transpose(ps[:, 7, k * P:(k + 1) * P], xn2[:, r.parity, t, k * P:(k + 1) * P], ident[:])
                    ins.then_inc(pX2.sem, 1)
                for t in range(2):
                    pe.wait_ge(eX2.sem, eX2.at(r, t + 1))
                    for k in range(DK):
                        ins = mm(ps[:, 3, t * E:(t + 1) * E], x2T[:, t, k], wg[:, k], k, DK)
                ins.then_inc(pLG.sem, 1)

            def positions(r):
                pe.wait_ge(ga.sem, ga.at(r))
                pe.wait_ge(gx.sem, gx.at(r))
                if r.shift(1).valid:
                    pe.wait_ge(x1s.sem, x1s.at(r.shift(1), 1))
                for t in range(2):
                    o = ps[:, 3, t * E:(t + 1) * E]
                    pe.matmul(o, onesb[:], seen[:, r.parity], start=True, stop=False)
                    if t:
                        pe.matmul(o, onesb[:], mask[:, r.parity, 0], start=False, stop=False)
                    ins = pe.matmul(o, trib[:], mask[:, r.parity, t], start=False, stop=True)
                ins.then_inc(pLOC.sem, 1)

            def body(r):
                b, p, n = r, r.shift(-1), r.shift(1)
                if b.valid:
                    scores(b, 1)
                if p.valid:
                    turn_out(p, 1)
                if b.valid:
                    attend(b, 0)
                if p.valid:
                    project(p, 1)
                if n.valid:
                    proj(n)
                    scores(n, 0)
                if b.valid:
                    turn_out(b, 0)
                if p.valid:
                    router(p)
                if b.valid:
                    attend(b, 1)
                    project(b, 0)
                if p.valid:
                    positions(p)

            pe.wait_ge(consts.sem, CONSTS)
            k0()
            pe.wait_ge(ek0.sem, 4)
            pe.wait_ge(ld["small"], 48)
            rounds(pe, body, B, -1, B, 1, 3)

            pe.wait_ge(ld["w1a"], 16)
            pe.wait_ge(ld["dft"], 16)

            def kv_time(r):
                pe.wait_ge(cb2.sem, cb2.at(r))
                if r.shift(-1).valid:
                    pe.wait_ge(eKV.sem, eKV.at(r.shift(-1)))
                else:
                    pe.wait_ge(ms.sem, ms.at(Round(0, B - 1, B)))
                for half in range(2):
                    for k in range(DK):
                        ins = mm(ps[0:TC, 0, half * D:(half + 1) * D], ctxb[:, r.parity, k], w1a[:, 1 + half, k], k, DK)
                ins.then_inc(pKV.sem, 1)

            def kv_freq(r):
                pe.wait_ge(eKV.sem, eKV.at(r))
                if r.shift(-1).valid:
                    pe.wait_ge(eKF.sem, eKF.at(r.shift(-1)))
                for m in range(2):
                    ins = pe.matmul(ps[:, 2 + m, :], dft[0:TC, 0, m * P:(m + 1) * P], kv[:, r.parity], start=True, stop=True)
                ins.then_inc(pKF.sem, 1)

            def kv_body(r):
                if r.valid:
                    kv_time(r)
                if r.shift(-1).valid:
                    kv_freq(r.shift(-1))
            rounds(pe, kv_body, B, 0, B, 1, B // 2)

            def dsp_turn(r):
                pe.wait_ge(lddsp[r.parity], 16 * (r.half + 1))
                if r.shift(-2).valid:
                    pe.wait_ge(eD.sem, eD.at(r.shift(-2)))
                else:
                    pe.wait_ge(eKF.sem, eKF.at(Round(0, B - 1, B)))
                for t in range(2):
                    for k in range(DK):
                        ins = pe.transpose(ps[:, r.parity, k * CAP + t * P:k * CAP + (t + 1) * P], dsp[:, r.parity, t, k * P:(k + 1) * P], ident[:])
                ins.then_inc(pD.sem, 1)

            def up(r):
                pe.wait_ge(ldw1[r.parity], 16 * (r.half + 1))
                pe.wait_ge(eD.sem, eD.at(r))
                for g in range(FK // 2):
                    if r.shift(-1).valid:
                        pe.wait_ge(gl.sem, gl.at(r.shift(-1), 2 * g + 2))
                    for j in range(2):
                        f = 2 * g + j
                        for k in range(DK):
                            ins = mm(ps[:, 2 + g, j * CAP:(j + 1) * CAP], w1[:, r.parity, k, f * P:(f + 1) * P], dspT[:, r.parity, k], k, DK)
                    ins.then_inc(pG1.sem, 1)

            def down(r):
                pe.wait_ge(ldw2[r.parity], 16 * (r.half + 1))
                pe.wait_ge(gl.sem, gl.at(r))
                if r.shift(-2).valid:
                    pe.wait_ge(ye.sem, ye.at(r.shift(-2)))
                for t in range(2):
                    for f in range(FK):
                        ins = mm(ps[:, 6 + r.parity, t * D:(t + 1) * D], hid[:, r.parity, f, t * P:(t + 1) * P], w2[:, r.parity, f], f, FK)
                ins.then_inc(pG2.sem, 1)

            def expert(r):
                if r.shift(1).valid:
                    dsp_turn(r.shift(1))
                if r.valid:
                    up(r)
                if r.shift(-1).valid:
                    down(r.shift(-1))
            rounds(pe, expert, E, -1, E, 1, 3)

            def turn_gu(m, first):
                pe.wait_ge(wp, 5 * (m + 1))
                for k in range(DK):
                    dst = ps[:, 4 + k, 0:IK * P // 2].bitcast(BF16)
                    if m == 1:
                        pe.wait_ge(ewp, k + 1)
                    else:
                        pe.wait_ge(gl.sem, gl.at(Round(0, E - 1, E)))
                    for i in range(IK):
                        n = P if i < IK - 1 else TAIL
                        ins = pe.transpose(dst[:, i * P:i * P + n], wq[0:n, i, k * P:(k + 1) * P], identb[0:n, 0:n])
                    ins.then_inc(pwp, 1)
            for m in range(2):
                turn_gu(m, m == 0)
            pe.wait_ge(wp, 15)
            wqd = wq[:].rearrange("p m d -> p (m d)")[:, 0:2 * I].rearrange("p (h i) -> p h i", h=2)
            for g in range(2):
                pe.wait_ge(ewp, 3 + g)
                dst = ps[:, 4 + g, 0:3 * D // 2].bitcast(BF16).rearrange("p (m d) -> p m d", m=3)
                for i in range(3):
                    m = 3 * g + i
                    n = P if m < IK - 1 else TAIL
                    for h in range(2):
                        ins = pe.transpose(dst[0:n, i, h * P:(h + 1) * P], wqd[:, h, m * P:m * P + n], identb[:])
                ins.then_inc(pwp, 1)
            pe.wait_ge(wp, 17)
            for h in range(2):
                ins = pe.matmul(ps[:, 2, h * P:(h + 1) * P], onesf[:], diag[:, h], start=True, stop=True)
            ins.then_inc(pwp, 1)

            def xspec(r):
                pe.wait_ge(ln3.sem, ln3.at(r))
                if r.shift(-2).valid:
                    pe.wait_ge(eXH.sem, eXH.at(r.shift(-2)))
                for m in range(DK):
                    for k in range(DK):
                        ins = mm(ps[:, r.parity, m * TQ:(m + 1) * TQ], xn[:, r.parity, k, m * P:(m + 1) * P], dft[:, k], k, DK)
                ins.then_inc(pXH.sem, 1)

            def qspec(r):
                pe.wait_ge(eXH.sem, eXH.at(r))
                if r.shift(-1).valid:
                    pe.wait_ge(pr.sem, pr.at(r.shift(-1), 3))
                else:
                    pe.wait_ge(ye.sem, ye.at(Round(0, E - 1, E)))
                for m in range(2):
                    o = ps[:, 6, m * D:(m + 1) * D]
                    for k in range(DK):
                        ins = pe.matmul(o, xh[:, r.parity, k, m * P:(m + 1) * P], w1a[:, 0, k], start=(k == 0), stop=(m == 1 and k == 1))
                    if m == 0:
                        pe.matmul(o, dcrow[:], bq[:], start=False, stop=True)
                ins.then_inc(pQF.sem, 1)

            def spectra(r):
                if r.valid:
                    xspec(r)
                if r.shift(-1).valid:
                    qspec(r.shift(-1))
            pe.wait_ge(ld["bias"], 64)
            rounds(pe, spectra, B, 0, B, 1, B // 2)
            pe.wait_ge(pr.sem, pr.at(Round(0, B - 1, B)))
            pe.wait_ge(ld["corrm"], 16)
            for j in range(4):
                ins = mm(ps[:, 3, 0:TQ], pc[:, j].rearrange("p b h -> p (b h)"), corrm[:, j], j, 4)
            ins.then_inc(pCO.sem, 1)
            pe.wait_ge(tk.sem, tk.per)
            for k in range(DK):
                ins = pe.transpose(ps[:, 3, TQ + k * P:TQ + (k + 1) * P], wts[:, 0, k * P:(k + 1) * P], ident[:])
            ins.then_inc(pWT.sem, 1)
            pe.wait_ge(eWT.sem, 1)
            pe.wait_ge(ld["wdft"], 16)
            for j in range(4):
                for k in range(DK):
                    ins = mm(ps[:, 7, j * P:(j + 1) * P], wdft[:, j, k], wtT[:, k], k, DK)
            ins.then_inc(pWF.sem, 1)

            def back(r):
                pe.wait_ge(uf.sem, uf.at(r))
                if r.shift(-2).valid:
                    pe.wait_ge(eOI.sem, eOI.at(r.shift(-2)))
                for m in range(DK):
                    for k in range(DK):
                        ins = mm(ps[:, r.parity, m * TQ:(m + 1) * TQ], of[:, r.parity, k, m * P:(m + 1) * P], idft[:, k], k, DK)
                ins.then_inc(pOI.sem, 1)

            def project1(r):
                pe.wait_ge(eOI.sem, eOI.at(r))
                if r.shift(-2).valid:
                    pe.wait_ge(x3s.sem, x3s.at(r.shift(-2)))
                for t in range(2):
                    for k in range(DK):
                        ins = mm(ps[:, 4 + r.parity, t * D:(t + 1) * D], oT[:, r.parity, k, t * P:(t + 1) * P], w1a[:, 3, k], k, DK)
                ins.then_inc(pY.sem, 1)

            def backs(r):
                if r.valid:
                    back(r)
                if r.shift(-1).valid:
                    project1(r.shift(-1))
            pe.wait_ge(ld["idft"], 16)
            pe.wait_ge(ewp, 8)
            rounds(pe, backs, B, 0, B, 1, B // 2)

            def turn_x(r):
                pe.wait_ge(xqs.sem, xqs.at(r))
                if r.shift(-2).valid:
                    pe.wait_ge(eXQ.sem, eXQ.at(r.shift(-2)))
                dst = ps[:, r.parity, 0:TQ].bitcast(BF16).rearrange("p (k s) -> p k s", k=DK)
                for t in range(2):
                    for k in range(DK):
                        ins = pe.transpose(dst[:, k, t * P:(t + 1) * P], xq[:, r.parity, t, k * P:(k + 1) * P], identb[:])
                ins.then_inc(pXQ.sem, 1)
            rounds(pe, turn_x, B, 0, B - 1, 1, B // 2)

            def gate_up(r):
                pe.wait_ge(eXQ.sem, eXQ.at(Round(0, B - 1, B)))
                for m in range(IK):
                    n = P if m < IK - 1 else TAIL
                    q = (r, m - 3) if m >= 3 else (r.shift(-1), m + 3)
                    if q[0].valid:
                        pe.wait_ge(hh.sem, hh.at(q[0], q[1] + 1))
                    for g in range(2):
                        for k in range(DK):
                            ins = mm(ps[0:n, 2 + 2 * (m % 3) + g, :], wgT[:, g, k, m * P:m * P + n], xqT[:, k, bass.ds(r.n * NB, NB)], k, DK)
                    ins.then_inc(pGU.sem, 1)
            rounds(pe, gate_up, B * TQ // NB, 0, B * TQ // NB - 1, 1, B * TQ // NB // 2)

            def down_last(r):
                pe.wait_ge(hqs.sem, hqs.at(r))
                if r.shift(-2).valid:
                    pe.wait_ge(dns.sem, dns.at(r.shift(-2)))
                for t in range(2):
                    for m in range(IK):
                        n = P if m < IK - 1 else TAIL
                        ins = mm(ps[:, r.parity, t * D:(t + 1) * D], hq[0:n, r.parity, m, t * P:(t + 1) * P], wdT[0:n, m], m, IK)
                ins.then_inc(pDN.sem, 1)
            rounds(pe, down_last, B, 0, B - 1, 1, B // 2)

        @block.scalar
        def _(act):
            act.wait_ge(ld["small"], 48)
            act.activation(gates4[:], gates4[:], ACT.Tanh).then_inc(tan.sem, 1)
            act.activation(clips[:], clips[:], ACT.Exp, scale=-1.0).then_inc(tan.sem, 1)
            for n in range(4):
                act.wait_ge(pk0.sem, n + 1)
                act.copy(k0T[:, n // 2, (n % 2) * B * TC // 2:(n % 2 + 1) * B * TC // 2], ps[:, n, 0:B * TC // 2]).then_inc(ek0.sem, 1)

            def probs(r, t):
                act.wait_ge(ms.sem, ms.at(r, 2 * t + 2))
                v = prob[:, t].rearrange("p h k -> p (h k)")
                act.activation(v, v, ACT.Exp).then_inc(ex.sem, 1)

            def copy_out(r, t):
                act.wait_ge(pOT.sem, pOT.at(r, t + 1))
                if r.shift(-1).valid:
                    act.wait_ge(pWO.sem, pWO.at(r.shift(-1), t + 1))
                act.copy(aoT[:, t].rearrange("p k s -> p (k s)"), ps[:, 7, 0:2 * P]).then_inc(eOT.sem, 1)

            def copy_probs(r, t):
                if r.shift(-1).valid:
                    act.wait_ge(pAV.sem, pAV.at(r.shift(-1), t + 1))
                for g in range(4):
                    act.wait_ge(pPT.sem, pPT.at(r, 4 * t + g + 1))
                    act.copy(probT[:, t, g * HG:(g + 1) * HG].rearrange("k h s -> k (h s)"), ps[0:TC, 4 + g % 2, :]).then_inc(ePT.sem, 1)

            def copy_proj(r):
                act.wait_ge(pA.sem, pA.at(r, 1))
                if r.shift(-1).valid:
                    act.wait_ge(pA.sem, pA.at(r.shift(-1), 3))
                act.copy(xnT[:].rearrange("p k s -> p (k s)"), ps[:, 4, :]).then_inc(eA.sem, 1)
                act.wait_ge(pA.sem, pA.at(r, 2))
                if r.shift(-2).valid:
                    act.wait_ge(pAV.sem, pAV.at(r.shift(-2)))
                act.copy(v0[:, r.parity, :, 0:DH], ps[0:TC, 7, 0:D].rearrange("k (h d) -> k h d", h=H)).then_inc(eA.sem, 1)
                act.wait_ge(pA.sem, pA.at(r, 3))
                if r.shift(-2).valid:
                    act.wait_ge(pS.sem, pS.at(r.shift(-2)))
                act.mul(qT[:, r.parity].rearrange("p k s -> p (k s)"), ps[:, 5, :], DH ** -0.5).then_inc(eA.sem, 1)

            def copy_router(r):
                if r.shift(-1).valid:
                    act.wait_ge(pLG.sem, pLG.at(r.shift(-1)))
                for t in range(2):
                    act.wait_ge(pX2.sem, pX2.at(r, t + 1))
                    act.copy(x2T[:, t].rearrange("p k s -> p (k s)"), ps[:, 7, 0:2 * P]).then_inc(eX2.sem, 1)

            def gate(r):
                act.wait_ge(ga.sem, ga.at(r, 5))
                if r.shift(-1).valid:
                    act.wait_ge(sl.sem, sl.at(r.shift(-1)))
                for t in range(2):
                    act.activation(gexp[:, t], ps[:, 3, t * E:(t + 1) * E], ACT.Exp, bias=ntop[:, t:t + 1],
                                   accum_out=gsum[:, t:t + 1]).then_inc(gx.sem, 1)

            def body(r):
                b, p, n = r, r.shift(-1), r.shift(1)
                if p.valid:
                    copy_out(p, 1)
                if b.valid:
                    copy_probs(b, 0)
                    probs(b, 1)
                if n.valid:
                    copy_proj(n)
                if b.valid:
                    copy_out(b, 0)
                if p.valid:
                    copy_router(p)
                if b.valid:
                    copy_probs(b, 1)
                if p.valid:
                    gate(p)
                if n.valid:
                    probs(n, 0)
            act.wait_ge(consts.sem, CONSTS)
            rounds(act, body, B, -1, B, 1, 3)

            def copy_kf(r):
                act.wait_ge(pKF.sem, pKF.at(r))
                for m in range(2):
                    act.copy(KVF[:, r.n, m, :], ps[:, 2 + m, :]).then_inc(eKF.sem, 1)
            rounds(act, copy_kf, B, 0, B - 1, 1, B // 2)

            def gelu(r):
                if r.shift(-2).valid:
                    act.wait_ge(pG2.sem, pG2.at(r.shift(-2)))
                for f in range(FK):
                    act.wait_ge(pG1.sem, pG1.at(r, f // 2 + 1))
                    act.activation(hid[:, r.parity, f], ps[:, 2 + f // 2, (f % 2) * CAP:(f % 2 + 1) * CAP], ACT.Gelu_apprx_tanh,
                                   bias=b1[:, bass.ds(r.n * FK + f, 1)]).then_inc(gl.sem, 1)
            act.wait_ge(ld["b1"], 16)
            rounds(act, gelu, E, 0, E - 1, 1, E // 2)

            for m in range(2):
                for k in range(DK):
                    act.wait_ge(pwp, 2 * m + k + 1)
                    act.copy(wgT[:, m, k], ps[:, 4 + k, 0:I // 2].bitcast(BF16)).then_inc(ewp, 1)
            for g in range(2):
                act.wait_ge(pwp, 5 + g)
                src = ps[:, 4 + g, 0:3 * D // 2].bitcast(BF16)
                if g == 0:
                    act.copy(wdT[:, 0:3].rearrange("p m d -> p (m d)"), src).then_inc(ewp, 1)
                else:
                    act.copy(wdT[:, 3:5].rearrange("p m d -> p (m d)"), src[:, 0:2 * D]).then_inc(ewp, 1)
                    act.copy(wdT[0:TAIL, 5], src[0:TAIL, 2 * D:3 * D]).then_inc(ewp, 1)
            act.wait_ge(pwp, 7)
            act.copy(dscale[:], ps[:, 2, 0:D]).then_inc(ewp, 1)

            def copy_xh(r):
                act.wait_ge(pXH.sem, pXH.at(r))
                if r.shift(-2).valid:
                    act.wait_ge(pQF.sem, pQF.at(r.shift(-2)))
                act.copy(xh[:, r.parity].rearrange("p k s -> p (k s)"), ps[:, r.parity, :]).then_inc(eXH.sem, 1)
            rounds(act, copy_xh, B, 0, B - 1, 1, B // 2)

            act.wait_ge(tk.sem, 4)
            act.activation(cw[:], c8[:, 0:TOPK], ACT.Exp, bias=nc0[:], accum_out=cs[:]).then_inc(tx.sem, 1)
            act.wait_ge(pWT.sem, 1)
            act.copy(wtT[:].rearrange("p k s -> p (k s)"), ps[:, 3, TQ:2 * TQ]).then_inc(eWT.sem, 1)
            act.wait_ge(pWF.sem, 1)
            act.copy(wf[:].rearrange("p j s -> p (j s)"), ps[:, 7, :]).then_inc(eWF.sem, 1)

            def copy_back(r):
                act.wait_ge(pOI.sem, pOI.at(r))
                if r.shift(-2).valid:
                    act.wait_ge(pY.sem, pY.at(r.shift(-2)))
                act.copy(oT[:, r.parity].rearrange("p k s -> p (k s)"), ps[:, r.parity, :]).then_inc(eOI.sem, 1)
            rounds(act, copy_back, B, 0, B - 1, 1, B // 2)

            def copy_xq(r):
                act.wait_ge(pXQ.sem, pXQ.at(r))
                act.copy(xqT[:, :, bass.ds(r.n * TQ, TQ)],
                         ps[:, r.parity, 0:TQ].bitcast(BF16).rearrange("p (k s) -> p k s", k=DK)).then_inc(eXQ.sem, 1)
            rounds(act, copy_xq, B, 0, B - 1, 1, B // 2)

            def silu(r):
                for m in range(IK):
                    n = P if m < IK - 1 else TAIL
                    act.wait_ge(pGU.sem, pGU.at(r, m + 1))
                    q = (r, m - 2) if m >= 2 else (r.shift(-1), m + IK - 2)
                    if q[0].valid:
                        act.wait_ge(hh.sem, hh.at(q[0], q[1] + 1))
                    act.activation(sil[0:n, m % 2], ps[0:n, 2 + 2 * (m % 3), :], ACT.Silu, scale=sgu[0:n, 0, m:m + 1]).then_inc(si.sem, 1)
            act.wait_ge(sc, 4)
            rounds(act, silu, B * TQ // NB, 0, B * TQ // NB - 1, 1, B * TQ // NB // 2)

        @block.vector
        def _(dv):
            def layer_norm(r, ln, rs, s, m, rr, src, dst, free=None):
                alone(dv)
                for t in range(2):
                    dv.bn_stats(s[:, t], src(t)).then_inc(ln.sem, 1)
                dv.wait_ge(ln.sem, ln.at(r, 2))
                alone(dv)
                for t in range(2):
                    dv.bn_aggr(m[:, t], s[:, t]).then_inc(ln.sem, 1)
                if free:
                    free()
                dv.wait_ge(rs.sem, rs.at(r))
                for t in range(2):
                    dv.tensor_scalar(dst(t), src(t), m[:, t, 0:1], rr[:, t:t + 1], ALU.subtract, ALU.mult).then_inc(ln.sem, 1)

            def tile_of(r, t):
                return x[:, r.n * 2 + t, :]

            def norm1(r):
                def free():
                    if r.shift(-2).valid:
                        dv.wait_ge(pA.sem, pA.at(r.shift(-2), 1))
                layer_norm(r, ln1, rs1, st, mv, rstd, lambda t: tile_of(r, t), lambda t: xn[:, r.parity, t], free)

            def less_max(r, t):
                dv.wait_ge(pS.sem, pS.at(r, t + 1))
                whole, n = H // SH, H % SH
                s = ps[:, 0:whole, 0:SH * TC].rearrange("p n (h k) -> p n h k", h=SH)
                s4 = ps[:, whole, 0:n * TC].rearrange("p (h k) -> p h k", h=n)
                dv.tensor_reduce(mx[:, t, 0:whole * SH].rearrange("p (n h) -> p n h", h=SH), s, AX_X, ALU.max)
                dv.tensor_reduce(mx[:, t, whole * SH:H], s4, AX_X, ALU.max).then_inc(ms.sem, 1)
                dv.wait_ge(ms.sem, ms.at(r, 2 * t + 1))
                if r.shift(-1).valid:
                    dv.wait_ge(pPT.sem, pPT.at(r.shift(-1), 4 * t + 4))
                dv.tensor_tensor(prob[:, t, 0:whole * SH].rearrange("p (n h) k -> p n h k", h=SH), s,
                                 mx[:, t, 0:whole * SH].rearrange("p (n h) -> p n h", h=SH)[:, :, :, None].broadcast_to([P, whole, SH, TC]),
                                 ALU.subtract)
                dv.tensor_tensor(prob[:, t, whole * SH:H], s4, mx[:, t, whole * SH:H][:, :, None].broadcast_to([P, n, TC]),
                                 ALU.subtract).then_inc(ms.sem, 1)

            def normalise(r, t):
                dv.wait_ge(pAV.sem, pAV.at(r, t + 1))
                v = ps[:, 6, 0:H * (DH + 1)].rearrange("p (h d) -> p h d", h=H)
                dv.reciprocal(rden[:, t], v[:, :, DH]).then_inc(nv.sem, 1)
                dv.wait_ge(nv.sem, nv.at(r, 2 * t + 1))
                if r.shift(-1).valid:
                    dv.wait_ge(pOT.sem, pOT.at(r.shift(-1), t + 1))
                dv.tensor_tensor(ao[:, t].rearrange("p (h d) -> p h d", h=H), v[:, :, 0:DH],
                                 rden[:, t][:, :, None].broadcast_to([P, H, DH]), ALU.mult).then_inc(nv.sem, 1)

            def residual1(r, t):
                dv.wait_ge(pWO.sem, pWO.at(r, t + 1))
                dv.scalar_tensor_tensor(tile_of(r, t), ps[:, 3, 0:D], gates4[:, 0:1], tile_of(r, t), ALU.mult, ALU.add).then_inc(x1s.sem, 1)

            def norm2(r):
                dv.wait_ge(x1s.sem, x1s.at(r))

                def free():
                    if r.shift(-2).valid:
                        for t in range(2):
                            dv.wait_ge(scat[r.parity][t], 16 * r.half)
                        dv.wait_ge(pX2.sem, pX2.at(r.shift(-2)))
                layer_norm(r, ln2, rs2, st2, mv2, rstd2, lambda t: tile_of(r, t), lambda t: xn2[:, r.parity, t], free)

            def choose(r):
                dv.wait_ge(pLG.sem, pLG.at(r))
                alone(dv)
                lg = ps[:, 3, 0:2 * E].rearrange("p (t e) -> p t e", t=2)
                for t in range(2):
                    dv.max(top[:, t], lg[:, t]).then_inc(ga.sem, 1)
                dv.wait_ge(ga.sem, ga.at(r, 2))
                if r.shift(-1).valid:
                    dv.wait_ge(gx.sem, gx.at(r.shift(-1)))
                dv.tensor_scalar(ntop[:], top[:, :, 0], -1.0, None, ALU.mult).then_inc(ga.sem, 1)
                for t in range(2):
                    dv.max_index(topi[:, t], top[:, t], lg[:, t]).then_inc(ga.sem, 1)
                dv.wait_ge(ga.sem, ga.at(r, 5))
                dv.tensor_copy(eidx[:, r.parity], topi[:, :, 0]).then_inc(ga.sem, 1)
                dv.wait_ge(ga.sem, ga.at(r, 6))
                if r.shift(-2).valid:
                    dv.wait_ge(pLOC.sem, pLOC.at(r.shift(-2)))
                dv.tensor_tensor(mask[:, r.parity], iota8[:, None, :].broadcast_to([P, 2, E]),
                                 eidx[:, r.parity][:, :, None].broadcast_to([P, 2, E]), ALU.is_equal).then_inc(ga.sem, 1)
                dv.wait_ge(ga.sem, ga.at(r, 7))
                dv.tensor_tensor(seen1[:], mask[:, r.parity, 0], mask[:, r.parity, 1], ALU.add).then_inc(ga.sem, 1)
                dv.wait_ge(ga.sem, ga.at(r, 8))
                if r.shift(-1).valid:
                    dv.wait_ge(pLOC.sem, pLOC.at(r.shift(-1)))
                dv.tensor_tensor(seen[:, 1 - r.parity], seen[:, r.parity], seen1[:], ALU.add).then_inc(ga.sem, 1)

            def place(r):
                n = 0

                def step(ins):
                    nonlocal n
                    n += 1
                    ins.then_inc(sl.sem, 1)
                    dv.wait_ge(sl.sem, sl.at(r, n))
                dv.wait_ge(pLOC.sem, pLOC.at(r))
                dv.wait_ge(gx.sem, gx.at(r))
                lo = ps[:, 3, 0:2 * E].rearrange("p (t e) -> p t e", t=2)
                step(dv.tensor_tensor(lm[:], lo, mask[:, r.parity], ALU.mult))
                step(dv.tensor_reduce(pos[:], lm[:], AX_X, ALU.add))
                step(dv.scalar_tensor_tensor(slot[:], eidx[:, r.parity], float(CAP), pos[:], ALU.mult, ALU.add))
                step(dv.tensor_scalar(keep[:], pos[:], float(CAP), None, ALU.is_le))
                step(dv.tensor_scalar(skip[:], keep[:], -2.0 * SLOTS, 2.0 * SLOTS - 1, ALU.mult, ALU.add))
                if r.shift(-2).valid:
                    for t in range(2):
                        dv.wait_ge(scat[r.parity][t], 16 * r.half)
                step(dv.tensor_tensor(slots[:, r.parity], slot[:], skip[:], ALU.add))
                step(dv.tensor_scalar(slot[:], slot[:], -1.0, float(SLOTS - 1), ALU.add, ALU.min))
                step(dv.tensor_copy(slotg[:, bass.ds(r.n * 2, 2)], slot[:]))
                step(dv.reciprocal(grec[:], gsum[:]))
                step(dv.tensor_scalar(grec[:], grec[:], gates4[:, 2:3], None, ALU.mult))
                step(dv.tensor_tensor(gk[:, bass.ds(r.n * 2, 2)], grec[:], keep[:], ALU.mult))
                assert n == sl.per

            def body(r):
                b, p, n = r, r.shift(-1), r.shift(1)
                if b.valid:
                    less_max(b, 1)
                    normalise(b, 0)
                if p.valid:
                    residual1(p, 1)
                    norm2(p)
                if n.valid:
                    less_max(n, 0)
                if r.shift(2).valid:
                    norm1(r.shift(2))
                if p.valid:
                    choose(p)
                if b.valid:
                    normalise(b, 1)
                    residual1(b, 0)
                if p.valid:
                    place(p)
            dv.memset(wnat[TAIL:P, IK - 1, :], 1.0).then_inc(wtail, 1)
            dv.wait_ge(ld["x0"], 16)
            norm1(Round(0, 0, B))
            norm1(Round(0, 1, B))
            dv.wait_ge(tan.sem, 2)
            dv.wait_ge(consts.sem, CONSTS)
            dv.wait_ge(ld["x1"], 16)
            less_max(Round(0, 0, B), 0)
            rounds(dv, body, B, 0, B, 1, 3)

            dv.tensor_scalar(clips[:], clips[:], QMAX, QMAX, ALU.mult, ALU.add).then_inc(sch, 1)
            dv.wait_ge(sch, 1)
            dv.reciprocal(clipr[:], clips[:]).then_inc(sch, 1)

            dv.wait_ge(ld["bias"], 64)

            def bias_kv(r):
                dv.wait_ge(pKV.sem, pKV.at(r))
                if r.shift(-2).valid:
                    dv.wait_ge(pKF.sem, pKF.at(r.shift(-2)))
                dv.tensor_tensor(kv[:, r.parity], ps[0:TC, 0, :], bkv[:], ALU.add).then_inc(eKV.sem, 1)
            rounds(dv, bias_kv, B, 0, B - 1, 1, B // 2)

            def expert(r):
                if r.valid:
                    dv.wait_ge(pD.sem, pD.at(r))
                    if r.shift(-2).valid:
                        dv.wait_ge(pG1.sem, pG1.at(r.shift(-2)))
                    dv.tensor_copy(dspT[:, r.parity].rearrange("p k s -> p (k s)"), ps[:, r.parity, :]).then_inc(eD.sem, 1)
                q = r.shift(-2)
                if q.valid:
                    dv.wait_ge(pG2.sem, pG2.at(q))
                    dv.wait_ge(ldb2[q.parity], 16 * (q.half + 1))
                    if q.shift(-2).valid:
                        dv.wait_ge(stored[q.parity], 16 * q.half)
                    dv.tensor_tensor(yex[:, q.parity], ps[:, 6 + q.parity, :].rearrange("p (t d) -> p t d", t=2),
                                     b2[:, q.parity][:, None, :].broadcast_to([P, 2, D]), ALU.add).then_inc(ye.sem, 1)
            rounds(dv, expert, E, 0, E + 1, 2, 4)

            def quantise(m, v, o, rows, step0):
                nr = v.shape[1]
                dv.tensor_reduce(wab[:, 0:nr], v, AX_X, ALU.max, apply_absolute_value=True).then_inc(wp, 1)
                dv.wait_ge(wp, step0 + 1)
                dv.tensor_scalar(wsc[:, m, 0:nr], wab[:, 0:nr], 1.0 / QMAX, None, ALU.mult).then_inc(wp, 1)
                dv.wait_ge(wp, step0 + 2)
                dv.reciprocal(wrec[:, 0:nr], wsc[:, m, 0:nr]).then_inc(wp, 1)
                dv.wait_ge(wp, step0 + 3)
                dv.tensor_tensor(v, v, wrec[:, 0:nr][:, :, None].broadcast_to([P, nr, v.shape[2]]), ALU.mult).then_inc(wp, 1)
                dv.wait_ge(wp, step0 + 4)
                dv.tensor_scalar(o, v, MAGIC, MAGIC, ALU.add, ALU.subtract).then_inc(wp, 1)

            dv.wait_ge(wtail, 1)
            for m, n in enumerate(("wnat0", "wnat1")):
                dv.wait_ge(ld[n], 32)
                if m == 1:
                    dv.wait_ge(pwp, 2)
                quantise(m, wnat[:], wq[:], IK, 5 * m)
            dv.wait_ge(ld["wnat2"], 16)
            dv.wait_ge(pwp, 4)
            wnd = wnat[:].rearrange("p m d -> p (m d)")[:, 0:2 * I].rearrange("p (h i) -> p h i", h=2)
            wqd = wq[:].rearrange("p m d -> p (m d)")[:, 0:2 * I].rearrange("p (h i) -> p h i", h=2)
            quantise(2, wnd, wqd, 2, 10)
            for h in range(2):
                dv.tensor_scalar(diag[:, h], ident[:], wsc[:, 2, h:h + 1], None, ALU.mult).then_inc(wp, 1)

            def residual2(r):
                for t in range(2):
                    dv.scalar_tensor_tensor(tile_of(r, t), yg[:, r.n * 2 + t, :], gk[:, bass.ds(r.n * 2 + t, 1)], tile_of(r, t),
                                            ALU.mult, ALU.add).then_inc(x2s.sem, 1)
                dv.wait_ge(x2s.sem, x2s.at(r))

                def free():
                    if r.shift(-2).valid:
                        dv.wait_ge(pXH.sem, pXH.at(r.shift(-2)))
                layer_norm(r, ln3, rs3, st, mv, rstd, lambda t: tile_of(r, t), lambda t: xn[:, r.parity, t], free)

            def products(r):
                dv.wait_ge(pQF.sem, pQF.at(r))
                if r.shift(-1).valid:
                    dv.wait_ge(pr.sem, pr.at(r.shift(-1)))
                q = ps[:, 6, :].rearrange("p (m d) -> p m d", m=2)
                dv.tensor_tensor(prod[:, 0:2], q, KVF[:, r.n, :, 0:D], ALU.mult).then_inc(pr.sem, 1)
                dv.tensor_tensor(prod[:, 2], q[:, 1], KVF[:, r.n, 0, 0:D], ALU.mult).then_inc(pr.sem, 1)
                dv.tensor_tensor(prod[:, 3], q[:, 0], KVF[:, r.n, 1, 0:D], ALU.mult).then_inc(pr.sem, 1)
                dv.wait_ge(pr.sem, pr.at(r, 3))
                dv.tensor_reduce(pc[:, :, r.n, :], prod[:].rearrange("p j (h d) -> p j h d", h=H), AX_X, ALU.add).then_inc(pr.sem, 1)

            def layer1(r):
                if r.valid:
                    residual2(r)
                if r.shift(-1).valid:
                    products(r.shift(-1))
            for t in range(NT):
                dv.wait_ge(gath[t], 16)
            rounds(dv, layer1, B, 0, B, 1, B // 2)

            n = 0

            def step(ins):
                nonlocal n
                n += 1
                ins.then_inc(tk.sem, 1)
                dv.wait_ge(tk.sem, n)
            dv.wait_ge(pCO.sem, 1)
            step(dv.tensor_copy(corr[:], ps[:, 3, 0:TQ]))
            step(dv.max(c8[:], corr[:]))
            step(dv.max_index(ci[:], c8[:], corr[:]))
            step(dv.tensor_scalar(nc0[:], c8[:, 0:1], -1.0, None, ALU.mult))
            step(dv.tensor_copy(cif[:], ci[:]))
            dv.wait_ge(tx.sem, 1)
            step(dv.reciprocal(cr[:], cs[:]))
            step(dv.tensor_scalar(cw[:], cw[:], cr[:], None, ALU.mult))
            for k in range(TOPK):
                ins = dv.tensor_scalar(wts[:, k], iotaT[:], cif[:, k:k + 1], cw[:, k:k + 1], ALU.is_equal, ALU.mult)
                n += 1
                ins.then_inc(tk.sem, 1)
            dv.wait_ge(tk.sem, n)
            for k in range(1, TOPK):
                step(dv.tensor_tensor(wts[:, 0], wts[:, 0], wts[:, k], ALU.add))
            assert n == tk.per

            dv.wait_ge(eWF.sem, 1)

            def rolled(r):
                v = KVF[:, r.n, :, D:2 * D].rearrange("p m (h d) -> p m h d", h=H)

                def w(j):
                    return wf[:, j, bass.ds(r.n * H, H)][:, :, None].broadcast_to([P, H, DH])
                if r.shift(-1).valid:
                    dv.wait_ge(uf.sem, uf.at(r.shift(-1)))
                for m in range(2):
                    dv.tensor_tensor(u1[:, m].rearrange("p (h d) -> p h d", h=H), v[:, m], w(m), ALU.mult)
                for m in range(2):
                    ins = dv.tensor_tensor(u2[:, m].rearrange("p (h d) -> p h d", h=H), v[:, 1 - m], w(2 + m), ALU.mult)
                ins.then_inc(uu.sem, 1)
                dv.wait_ge(uu.sem, uu.at(r))
                if r.shift(-2).valid:
                    dv.wait_ge(pOI.sem, pOI.at(r.shift(-2)))
                dv.tensor_tensor(of[:, r.parity], u1[:], u2[:], ALU.add).then_inc(uf.sem, 1)

            def residual3(r):
                dv.wait_ge(pY.sem, pY.at(r))
                dv.wait_ge(x2b.sem, x2b.at(r))
                xv = x[:, bass.ds(r.n * 2, 2), :]
                dv.scalar_tensor_tensor(xv, ps[:, 4 + r.parity, :].rearrange("p (t d) -> p t d", t=2), gates4[:, 1:2], xv,
                                        ALU.mult, ALU.add).then_inc(x3s.sem, 1)
                dv.wait_ge(x3s.sem, x3s.at(r))
                layer_norm(r, ln4, rs4, st2, mv2, rstd2, lambda t: tile_of(r, t), lambda t: yg[:, r.n * 2 + t, :])
                dv.wait_ge(ln4.sem, ln4.at(r, 6))
                for t in range(2):
                    dv.tensor_reduce(amax[:, bass.ds(r.n * 2 + t, 1)], yg[:, r.n * 2 + t, :], AX_X, ALU.max,
                                     apply_absolute_value=True).then_inc(ln4.sem, 1)

            def layer1b(r):
                if r.valid:
                    rolled(r)
                if r.shift(-2).valid:
                    residual3(r.shift(-2))
            rounds(dv, layer1b, B, 0, B + 1, 1, B // 2)

            dv.wait_ge(ln4.sem, ln4.at(Round(0, B - 1, B)))
            dv.tensor_reduce(am1[:], amax[:], AX_X, ALU.max).then_inc(sc, 1)
            dv.wait_ge(arx, 1)
            dv.tensor_scalar(sx[:, 0:1], am2[:], clipr[:, 0:1], None, ALU.mult).then_inc(sc, 1)
            dv.wait_ge(sc, 2)
            dv.reciprocal(sx[:, 1:2], sx[:, 0:1]).then_inc(sc, 1)
            dv.tensor_scalar(sgu[:], wsc[:, 0:2], sx[:, 0:1], None, ALU.mult).then_inc(sc, 1)
            dv.wait_ge(sc, 4)

            def quant_x(r):
                f = yg[:, bass.ds(r.n * 2, 2), :]
                dv.tensor_scalar(f, f, sx[:, 1:2], MAGIC, ALU.mult, ALU.add).then_inc(xqs.sem, 1)
                dv.wait_ge(xqs.sem, xqs.at(r, 1))
                dv.tensor_scalar(f, f, MAGIC, QMAX, ALU.subtract, ALU.min).then_inc(xqs.sem, 1)
                dv.wait_ge(xqs.sem, xqs.at(r, 2))
                if r.shift(-2).valid:
                    dv.wait_ge(pXQ.sem, pXQ.at(r.shift(-2)))
                dv.tensor_scalar(xq[:, r.parity], f, -QMAX - 1.0, None, ALU.max).then_inc(xqs.sem, 1)
            rounds(dv, quant_x, B, 0, B - 1, 1, B // 2)

            dv.memset(hT[TAIL:P, IK - 1, :], 0.0).then_inc(hmx, 1)

            def gated(r):
                for m in range(IK):
                    n = P if m < IK - 1 else TAIL
                    dv.wait_ge(si.sem, si.at(r, m + 1))
                    h = hT[0:n, m, bass.ds(r.n * NB, NB)]
                    dv.scalar_tensor_tensor(h, ps[0:n, 3 + 2 * (m % 3), :], sgu[0:n, 1, m:m + 1], sil[0:n, m % 2], ALU.mult, ALU.mult).then_inc(hh.sem, 1)
            rounds(dv, gated, B * TQ // NB, 0, B * TQ // NB - 1, 1, B * TQ // NB // 2)
            dv.wait_ge(hh.sem, hh.at(Round(0, B * TQ // NB - 1, 4)))
            dv.wait_ge(hmx, 1)
            for m in range(IK * 4):
                v = hT[:, m // 4, (m % 4) * NB:(m % 4 + 1) * NB]
                dv.tensor_reduce(hmaxs[:, m:m + 1], v, AX_X, ALU.max, apply_absolute_value=True).then_inc(hmx, 1)
            dv.wait_ge(hmx, 1 + IK * 4)
            dv.tensor_reduce(am1[:], hmaxs[:], AX_X, ALU.max).then_inc(hmx, 1)
            dv.wait_ge(arh, 1)
            dv.tensor_scalar(sx[:, 0:1], am2[:], clipr[:, 1:2], None, ALU.mult).then_inc(sch, 1)
            dv.wait_ge(sch, 3)
            dv.wait_ge(ewp, 8)
            dv.reciprocal(sx[:, 1:2], sx[:, 0:1]).then_inc(sch, 1)
            dv.tensor_scalar(dscale[:], dscale[:], sx[:, 0:1], gates4[:, 3:4], ALU.mult, ALU.mult).then_inc(sch, 1)
            dv.wait_ge(sch, 5)

            def quant_h(r):
                h, f = hT[:, :, bass.ds(r.n * TQ, TQ)], hr[:, r.parity]
                dv.tensor_scalar(f, h, sx[:, 1:2], MAGIC, ALU.mult, ALU.add).then_inc(hqs.sem, 1)
                dv.wait_ge(hqs.sem, hqs.at(r, 1))
                dv.tensor_scalar(f, f, MAGIC, QMAX, ALU.subtract, ALU.min).then_inc(hqs.sem, 1)
                dv.wait_ge(hqs.sem, hqs.at(r, 2))
                if r.shift(-2).valid:
                    dv.wait_ge(pDN.sem, pDN.at(r.shift(-2)))
                dv.tensor_scalar(hq[:, r.parity], f, -QMAX - 1.0, None, ALU.max).then_inc(hqs.sem, 1)

            def scale_down(r):
                dv.wait_ge(pDN.sem, pDN.at(r))
                if r.shift(-2).valid:
                    dv.wait_ge(fin.sem, fin.at(r.shift(-2)))
                dv.tensor_tensor(xn[:, r.parity], ps[:, r.parity, :].rearrange("p (t d) -> p t d", t=2),
                                 dscale[:, None, :].broadcast_to([P, 2, D]), ALU.mult).then_inc(dns.sem, 1)

            def last(r):
                if r.valid:
                    quant_h(r)
                if r.shift(-1).valid:
                    scale_down(r.shift(-1))
            rounds(dv, last, B, 0, B, 1, B // 2)


CONSTS = 16


def constants():
    n = np.arange(TQ)
    cos = lambda f: np.cos(2 * np.pi * ((np.outer(n, f)) % TQ) / TQ)
    sin = lambda f: np.sin(2 * np.pi * ((np.outer(n, f)) % TQ) / TQ)
    f = np.arange(P)
    c, s, nyq = cos(f), sin(f), cos([P])
    s0 = s.copy()
    s0[:, 0:1] = nyq
    dft = np.concatenate([c, s0], 1)
    weight = np.where(f == 0, 1.0, 2.0) / TQ
    ic, is_ = (c * weight).T, (s * weight).T
    isn = is_.copy()
    isn[0] = nyq[:, 0] / TQ
    idft = np.concatenate([ic, isn], 0)
    m1 = ic.copy()
    m2 = ic.copy()
    m2[0] = nyq[:, 0] / TQ
    corrm = np.stack([m1, m2, is_, -is_]) / DH
    cn = c.copy()
    cn[:, 0:1] = nyq
    wd = np.stack([c, cn, s, -s])
    g = lambda m: np.ascontiguousarray(m, dtype=np.float32)
    dc = np.zeros((1, P))
    dc[0, 0] = TQ
    return {
        "dft": g(dft.reshape(DK, P, TQ).transpose(1, 0, 2)),
        "idft": g(idft.reshape(DK, P, TQ).transpose(1, 0, 2)),
        "corrm": g(corrm.transpose(1, 0, 2)),
        "wdft": g(wd.reshape(4, DK, P, P).transpose(2, 0, 1, 3)),
        "dcrow": g(dc),
    }


def kernel(**inputs):
    import concourse.bacc as bacc
    from concourse.bass_utils import run_bass_kernel_spmd

    v = {n: np.asarray(t) for n, t in inputs.items()}

    def rows(m):
        return m.reshape(DK, P, -1).transpose(1, 0, 2)

    arrays = {
        "x": v["x"].reshape(B * TQ, D),
        "ctxT": rows(v["ctx_1024"].reshape(B * TC, D).T),
        "w0": np.stack([rows(v["L0_xattn_" + n].T) for n in ("Wq", "Wk", "Wv", "Wo")], 1),
        "w1a": np.stack([rows(v["L1_xattn_" + n]) for n in ("Wq", "Wk", "Wv", "Wo")], 1),
        "wg": rows(v["L0_ffn_wg"]),
        "gates": np.concatenate([v["g_xattn"], v["g_ffn"]]),
        "clips": np.concatenate([v["L1_ffn_clip_x"], v["L1_ffn_clip_down"]]),
        "b1": v["L0_ffn_b1"].reshape(E, FK, P).transpose(2, 0, 1).reshape(P, E * FK),
        "w1": v["L0_ffn_w1"].reshape(E, DK, P, F).transpose(0, 2, 1, 3),
        "w2": v["L0_ffn_w2"].reshape(E, FK, P, D).transpose(0, 2, 1, 3),
        "b2": v["L0_ffn_b2"],
        "bkv": np.concatenate([v["L1_xattn_bk"], v["L1_xattn_bv"]]),
        "bq": v["L1_xattn_bq"][None],
        "bo": v["L1_xattn_bo"],
        "wgu": np.stack([v["L1_ffn_w_gate"], v["L1_ffn_w_up"]]),
        "wd": v["L1_ffn_w_down"],
        **constants(),
    }
    arrays = {"in_" + n: np.ascontiguousarray(m) for n, m in arrays.items()}
    nc = bacc.Bacc("TRN2", target_bir_lowering=False, num_devices=1)
    args = {n[3:]: nc.dram_tensor(n, list(m.shape), F32, kind="ExternalInput").ap() for n, m in arrays.items()}
    out = nc.dram_tensor("out", [B * TQ, D], F32, kind="ExternalOutput").ap()
    build(nc, args, out)
    r = run_bass_kernel_spmd(nc, [arrays], core_ids=[0])
    return r.results[0]["out"].reshape(B, TQ, D)
```

```python
from contextlib import ExitStack

import numpy as np

import concourse.bass as bass
from concourse import mybir

F32 = mybir.dt.float32
BF16 = mybir.dt.bfloat16
U32 = mybir.dt.uint32
ALU = mybir.AluOpType
ACT = mybir.ActivationFunctionType
AX_X = mybir.AxisListType.X
ABSMAX = bass.bass_isa.ReduceOp.absmax

P = 128
B, TQ, D = 8, 256, 256
TC = 77
H, DH = 16, 16
DK = D // P
NT = B * TQ // P
E, F = 8, 1024
FK = F // P
CAP = B * TQ // E
SLOTS = E * CAP
I = 704
IK = (I + P - 1) // P
TAIL = I - (IK - 1) * P
NB = 512
TOPK = 5
EPS = 1e-5
QMAX = 127.0
MAGIC = 1.5 * 2.0 ** 23
HA = 2
SH = 6
TCP = 80
HB, KB = 8, 16
KC = TCP // KB
NC = (H // HB) * KC
GROUPS = ((0, 4), (4, 8), (8, NC))
NG = len(GROUPS)


class Round:

    def __init__(self, i, off, count):
        self.i, self.off, self.count = i, off, count
        self.parity = off % 2
        self.static = isinstance(i, int)
        self.n = 2 * i + off if self.static else i * 2 + off

    def shift(self, k):
        return Round(self.i, self.off + k, self.count)

    @property
    def valid(self):
        return not self.static or 0 <= self.n < self.count

    @property
    def half(self):
        return self.i + self.off // 2


class Stage:

    def __init__(self, sem, per):
        self.sem, self.per = sem, per

    def at(self, r, step=None):
        return r.n * self.per + (self.per if step is None else step)


def rounds(eng, body, count, first, last, lo, hi):
    for n in range(first, 2 * lo):
        body(Round(0, n, count))
    with eng.Fori(lo, hi) as i:
        body(Round(i, 0, count))
        body(Round(i, 1, count))
    for n in range(2 * hi, last + 1):
        body(Round(0, n, count))


def build(nc, a, out):
    with ExitStack() as ctx:
        def sb(name, shape, dt=F32):
            return ctx.enter_context(nc.sbuf_tensor(name, shape, dt))

        def sem(name):
            return ctx.enter_context(nc.semaphore(name))

        def stage(name, per):
            return Stage(sem(name), per)

        def carve(base, shapes):
            at, out = 0, []
            for shape in shapes:
                size = int(np.prod(shape))
                axes = "abcd"[:len(shape)]
                v = base[:, at:at + size]
                if len(shape) > 1:
                    v = v.rearrange(f"p ({' '.join(axes)}) -> p {' '.join(axes)}", **dict(zip(axes, shape)))
                out.append(v)
                at += size
            assert at <= base.shape[1], (at, base.shape)
            return out

        pool = sb("pool", [P, 9 * 2048])
        (kbd, prob, probT, k0T, xnT, qT, ao, aoT, x2T, zeros, vblk, vpk) = carve(pool, [
            (2, DK, P // DH, TC),
            (2, H, TCP), (2, NC, P), (DK, B * TC), (DK, TQ), (2, DK, TQ), (2, D), (2, DK, P), (2, DK, P), (1024,),
            (2, NC, HB, DH + 1),
            (KC, B, 2, DH)])
        v0s, = carve(vblk[0:TC].rearrange("p u c h d -> p (u c h d)"), [(HB, B, 2, DH)])
        (hid, yex, KVF, yg, wdTw) = carve(pool, [
            (2, FK, CAP), (2, CAP // P, D),
            (B, 2, 2 * D),
            (NT, D),
            (IK * D // 2,)])
        wdT = wdTw.bitcast(BF16).rearrange("p (m d) -> p m d", m=IK)
        hT = pool[:, 0:IK * B * TQ].rearrange("p (m s) -> p m s", m=IK)
        wbuf = sb("wbuf", [P, 4 * DK * F])
        w1, w2 = carve(wbuf, [(2, DK, F), (2, FK, D)])
        (xh, prod, corr, wts, wtT, wf, of, oT) = carve(wbuf, [
            (2, DK, TQ), (4, D), (TQ,), (TOPK, TQ), (DK, P), (4, P), (2, DK, D), (2, DK, TQ)])
        (u1, u2) = carve(wbuf, [(2, 2, D), (2, 2, D)])
        hr, hqw = carve(wbuf, [(2, IK, TQ), (2 * IK * TQ // 2,)])
        hq = hqw.bitcast(BF16).rearrange("p (u m s) -> p u m s", u=2, m=IK)
        w0b = sb("w0b", [P, 4 * DK * D])
        w0, = carve(w0b, [(4, DK, D)])
        wgT = w0b[:, 0:DK * I].bitcast(BF16).rearrange("p (g k i) -> p g k i", g=2, k=DK)
        w1b = sb("w1b", [P, 4 * DK * D])
        w1a, = carve(w1b, [(4, DK, D)])
        xqT = w1b[:].bitcast(BF16).rearrange("p (k s) -> p k s", k=DK)

        x = sb("x", [P, NT, D])
        ctxT = sb("ctxT", [P, DK, B * TC])
        ctxb = sb("ctxb", [P, 2, DK, TC])
        wg = sb("wg", [P, DK, E])
        ident = sb("ident", [P, P])
        identb = sb("identb", [P, P], BF16)
        onesf = sb("onesf", [P, P])
        onesb = sb("onesb", [P, P], BF16)
        trib = sb("trib", [P, P], BF16)
        headmask = sb("headmask", [P, P // DH])
        iota8 = sb("iota8", [P, E])
        iotaT = sb("iotaT", [P, TQ])
        mhalf = sb("mhalf", [P, 2])
        epsc = sb("epsc", [P, 2])
        zeroc = sb("zeroc", [P, 2])
        magicc = sb("magicc", [P, 1])
        nmagic = sb("nmagic", [P, 1])
        gates4 = sb("gates4", [P, 4])
        clips = sb("clips", [P, 2])
        clipr = sb("clipr", [P, 2])
        bkv = sb("bkv", [TC, 2 * D])
        bq = sb("bq", [1, D])
        bo = sb("bo", [P, D])
        b1 = sb("b1", [P, E * FK])
        dft = sb("dft", [P, DK, TQ])
        idft = sb("idft", [P, DK, TQ])
        corrm = sb("corrm", [P, 4, TQ])
        wdft = sb("wdft", [P, 4, DK, P])
        dcrow = sb("dcrow", [1, P])

        st = sb("st", [P, 2, 6])
        mv = sb("mv", [P, 2, 2])
        vare = sb("vare", [P, 2])
        nmean = sb("nmean", [P, 2])
        nmr = sb("nmr", [P, 2])
        rstd = sb("rstd", [P, 2])
        st2 = sb("st2", [P, 2, 6])
        mv2 = sb("mv2", [P, 2, 2])
        vare2 = sb("vare2", [P, 2])
        nmean2 = sb("nmean2", [P, 2])
        nmr2 = sb("nmr2", [P, 2])
        rstd2 = sb("rstd2", [P, 2])
        xn = sb("xn", [P, 2, 2, D])
        xn2 = sb("xn2", [P, 2, 2, D])
        mx = sb("mx", [P, 2, H])
        rden = sb("rden", [P, 2, H])
        top = sb("top", [P, 2, 8])
        topi = sb("topi", [P, 2, 8], U32)
        eidx = sb("eidx", [P, 2, 2])
        ntop = sb("ntop", [P, 2])
        mask = sb("mask", [P, 2, 2, E], BF16)
        seen = sb("seen", [P, 2, E], BF16)
        seen1 = sb("seen1", [P, E])
        gexp = sb("gexp", [P, 2, E])
        gsum = sb("gsum", [P, NT])
        lm = sb("lm", [P, 2, E])
        pos = sb("pos", [P, 2])
        slot = sb("slot", [P, NT])
        keep = sb("keep", [P, NT])
        skip = sb("skip", [P, 2])
        grec = sb("grec", [P, NT])
        slots = sb("slots", [P, 2, 2], U32)
        slotg = sb("slotg", [P, NT], U32)
        gk = sb("gk", [P, NT])
        b2 = sb("b2", [P, 2, D])
        dsp = sb("dsp", [P, 2, CAP // P, D])
        dspT = sb("dspT", [P, 2, DK, CAP])
        kv = sb("kv", [TC, 2, 2 * D])
        pc = sb("pc", [P, 4, B, H])
        c8 = sb("c8", [P, 8])
        ci = sb("ci", [P, 8], U32)
        cif = sb("cif", [P, 8])
        nc0 = sb("nc0", [P, 1])
        cw = sb("cw", [P, TOPK])
        cs = sb("cs", [P, 1])
        cr = sb("cr", [P, 1])
        amax = sb("amax", [P, NT])
        am1 = sb("am1", [P, 1])
        am2 = sb("am2", [P, 1])
        sx = sb("sx", [P, 2])
        wnat = sb("wnat", [P, IK, D])
        wab = sb("wab", [P, IK])
        wrec = sb("wrec", [P, IK])
        wsc = sb("wsc", [P, 3, IK])
        wq0 = sb("wq0", [P, IK, D], BF16)
        hmaxs = sb("hmaxs", [P, IK * B * TQ // NB])
        sgu = sb("sgu", [P, 2, IK])
        diag = sb("diag", [P, DK, P])
        dscale = sb("dscale", [P, D])
        xq = sb("xq", [P, 2, 2, D], BF16)

        def as_wq(m):
            return m[:, 0:IK * D // 2].bitcast(BF16).rearrange("p (m d) -> p m d", m=IK)
        wqs = (wq0[:], as_wq(ctxT[:].rearrange("p k s -> p (k s)")), as_wq(xn2[:].rearrange("p u t d -> p (u t d)")))
        wqd = wqs[2].rearrange("p m d -> p (m d)")[:, 0:2 * I].rearrange("p (h i) -> p h i", h=2)
        wnd = wnat[:].rearrange("p m d -> p (m d)")[:, 0:2 * I].rearrange("p (h i) -> p h i", h=2)

        ps = ctx.enter_context(nc.psum_tensor("ps", [P, 8, 512], F32))

        vdram = nc.dram_tensor("values_by_head", [HB, TCP, B * 2 * DH], F32, kind="Internal").ap()
        disp = nc.dram_tensor("dispatched", [SLOTS, D], F32, kind="Internal").ap()
        yexp = nc.dram_tensor("expert_rows", [SLOTS, D], F32, kind="Internal").ap()

        ld = {n: sem("loaded_" + n) for n in (
            "x0", "x1", "w0", "w1a", "ctxT", "small", "b1", "bias", "dft", "idft", "corrm", "wdft", "wnat0", "wnat1", "wnat2")}
        ldw1 = [sem(f"loaded_w1_{u}") for u in range(2)]
        ldw2 = [sem(f"loaded_w2_{u}") for u in range(2)]
        ldb2 = [sem(f"loaded_b2_{u}") for u in range(2)]
        lddsp = [sem(f"loaded_dispatched_{u}") for u in range(2)]
        zeroed = sem("dispatched_zeroed")
        scat = [[sem(f"scattered_{u}{t}") for t in range(2)] for u in range(2)]
        stored = [sem(f"expert_rows_stored_{u}") for u in range(2)]
        gath = [sem(f"gathered_{t % 2}{t // 2}") for t in range(NT)]
        outs = sem("out_stored")
        passed = sem("waits_passed")
        wtail = sem("weights_tail_set")

        consts = stage("consts_ready", 1)
        tan = stage("gates_tanh", 1)
        ln1, rs1, ap1 = stage("ln1_statistics", 4), stage("ln1_rstd", 4), stage("ln1", 2)
        kb, vb = stage("keys_block_diagonal", 1), stage("values_block_diagonal", 1)
        pV, eV = sem("values_product"), sem("values_copied")
        vpad, vst, vld, vones = sem("values_padded"), sem("values_stored"), sem("values_loaded"), sem("value_ones")
        pk0, ek0 = stage("k0T_product", 1), stage("k0T_copied", 1)
        pA, eA = stage("xT_q_product", 2), stage("xT_q_copied", 2)
        pS, ms, ex = stage("scores", 2), stage("scores_less_max", 4), stage("probabilities", 2)
        pPT, ePT, pAV = stage("prob_transposed", 2 * NG), stage("probT_copied", 2 * NG), stage("attended", 2)
        nv = stage("attended_normalised", 4)
        pOT, eOT, pWO, x1s = stage("ao_transposed", 2), stage("aoT_copied", 2), stage("ao_projected", 2), stage("x1", 2)
        ln2, rs2, ap2 = stage("ln2_statistics", 4), stage("ln2_rstd", 4), stage("ln2", 2)
        pX2, eX2, pLG = stage("x2_transposed", 2), stage("x2T_copied", 2), stage("router_logits", 1)
        ga, gx, pLOC, sl = stage("chosen", 9), stage("gate_exp", 2), stage("positions", 1), stage("slots_known", 6)
        bulk = sem("gates_and_slots")
        pD, eD = stage("dsp_transposed", 1), stage("dspT_copied", 1)
        pG1, gl, pG2, ye = stage("hidden_product", 4), stage("hidden_gelu", 8), stage("expert_product", 1), stage("expert_rows", 1)
        cb2, pKV, eKV, pKF, eKF = stage("ctx_batch2", 1), stage("kv_product", 1), stage("kv_biased", 1), stage("kv_spectrum", 1), stage("kv_spectrum_copied", 2)
        x2s, ln3, rs3, ap3, x2b = stage("x2", 2), stage("ln3_statistics", 4), stage("ln3_rstd", 4), stage("ln3", 2), stage("x2_bias", 1)
        pXH, eXH, pQF, pr = stage("xn_spectrum", 1), stage("xn_spectrum_copied", 1), stage("q_spectrum", 1), stage("spectra_products", 4)
        pCO, tk, tx, pWT, eWT, pWF, eWF = (stage("correlation", 1), stage("delays", 16), stage("delays_exp", 1), stage("delays_transposed", 1),
                                          stage("delaysT_copied", 1), stage("delay_spectra", 1), stage("delay_spectra_copied", 1))
        uv = stage("rolled_parts_crossed", 1)
        uu, uf, pOI, eOI, pY, x3s = stage("rolled_parts", 1), stage("rolled_spectrum", 1), stage("rolled_time", 1), stage("rolled_copied", 1), stage("rolled_projected", 1), stage("x3", 1)
        ln4, rs4, ap4, mx4 = stage("ln4_statistics", 4), stage("ln4_rstd", 4), stage("ln4", 2), stage("ln4_max", 1)
        bosc = sem("bias_scaled")
        wp, pwp, ewp = sem("weights_quantised"), sem("weights_transposed"), sem("weightsT_copied")
        sc, arx = sem("activation_scale"), sem("activation_max_all")
        xq1 = stage("x_rounded", 1)
        xqs, pXQ, eXQ = stage("x_quantised", 2), stage("xq_transposed", 1), stage("xqT_copied", 1)
        pGU, si, hh = stage("gate_up_product", IK), stage("gate_silu", IK), stage("hidden_gated", IK)
        hmx, arh = sem("hidden_max"), sem("hidden_max_all")
        hq1, hqc, hqa, hqv = stage("hidden_rounded", 1), stage("hidden_clipped", 1), stage("hidden_quantised_act", 1), stage("hidden_quantised_vector", 1)
        sch = sem("hidden_scale")
        pDN, dns, fin = stage("down_product", 1), stage("down_scaled", 1), stage("final", 1)


        NQ = B * TQ // NB

        def batch_of(n, t):
            return Round(0, 2 * n + t, B)

        sil = xn2[:].rearrange("p u t d -> p u (t d)")

        block = ctx.enter_context(nc.Block())

        def alone(eng):
            eng.sem_inc(passed, 1)

        def load_gu(eng, m):
            eng.dma_start(wnat[:, 0:IK - 1, :], a["wgu"][m, 0:P * (IK - 1), :].rearrange("(m p) d -> p m d", p=P)).then_inc(ld[f"wnat{m}"], 16)
            eng.dma_start(wnat[0:TAIL, IK - 1, :], a["wgu"][m, P * (IK - 1):I, :]).then_inc(ld[f"wnat{m}"], 16)

        @block.sync
        def _(sp):
            xv = a["x"].rearrange("(t p) d -> p t d", p=P)
            sp.dma_start(x[:, 0:4, :], xv[:, 0:4, :]).then_inc(ld["x0"], 16)
            sp.dma_start(ctxT[:], a["ctxT"]).then_inc(ld["ctxT"], 16)
            sp.dma_start(w0[:], a["w0"]).then_inc(ld["w0"], 16)
            sp.dma_start(x[:, 4:NT, :], xv[:, 4:NT, :]).then_inc(ld["x1"], 16)
            for dst, src in ((wg[:], a["wg"]), (gates4[:], a["gates"].partition_broadcast(P)), (clips[:], a["clips"].partition_broadcast(P))):
                sp.dma_start(dst, src).then_inc(ld["small"], 16)
            sp.dma_start(b1[:], a["b1"]).then_inc(ld["b1"], 16)
            sp.wait_ge(eV, B)
            sp.dma_start(vdram[:, 0:TC, :].rearrange("h k n -> k h n"), v0s.rearrange("k h b g d -> k h (b g d)")).then_inc(vst, 16)
            sp.wait_ge(vpad, 16)
            sp.wait_ge(vst, 16)
            sp.dma_start(vpk.rearrange("p c b g d -> p c (b g d)"), vdram.rearrange("h (k c) n -> (h k) c n", c=KC)).then_inc(vld, 16)
            for e in range(2):
                sp.dma_start(w1[:, e], a["w1"][e]).then_inc(ldw1[e], 16)
                sp.dma_start(w2[:, e], a["w2"][e]).then_inc(ldw2[e], 16)
                sp.dma_start(b2[:, e], a["b2"][e].partition_broadcast(P)).then_inc(ldb2[e], 16)
            sp.wait_ge(wtail, 1)
            load_gu(sp, 0)
            sp.dma_start(w1a[:], a["w1a"]).then_inc(ld["w1a"], 16)
            sp.dma_start(dft[:], a["dft"]).then_inc(ld["dft"], 16)
            sp.dma_start(idft[:], a["idft"]).then_inc(ld["idft"], 16)
            sp.dma_start(corrm[:], a["corrm"]).then_inc(ld["corrm"], 16)
            sp.dma_start(wdft[:], a["wdft"]).then_inc(ld["wdft"], 16)
            for dst, src in ((bkv[:], a["bkv"].partition_broadcast(TC)), (bq[:], a["bq"]), (bo[:], a["bo"].partition_broadcast(P)), (dcrow[:], a["dcrow"])):
                sp.dma_start(dst, src).then_inc(ld["bias"], 16)
            for u in range(2):
                for t in range(2):
                    sp.wait_ge(scat[u][t], 16 * (B // 2))
            dv = disp.rearrange("(e t p) d -> e p t d", e=E, p=P)

            def load_dsp(r):
                sp.dma_start(dsp[:, r.parity], dv[r.n]).then_inc(lddsp[r.parity], 16)

            def body(r):
                nx = r.shift(2)
                if nx.valid:
                    sp.wait_ge(pD.sem, pD.at(r))
                    load_dsp(nx)
                    sp.wait_ge(pG1.sem, pG1.at(r))
                    sp.dma_start(w1[:, r.parity], a["w1"][nx.n]).then_inc(ldw1[r.parity], 16)
                q = r.shift(-1)
                if q.valid and q.shift(2).valid:
                    sp.wait_ge(ye.sem, ye.at(q))
                    sp.dma_start(w2[:, q.parity], a["w2"][q.shift(2).n]).then_inc(ldw2[q.parity], 16)
                    sp.dma_start(b2[:, q.parity], a["b2"][q.shift(2).n].partition_broadcast(P)).then_inc(ldb2[q.parity], 16)

            load_dsp(Round(0, 0, E))
            load_dsp(Round(0, 1, E))
            rounds(sp, body, E, 0, E - 2, 1, (E - 2) // 2)
            ov = out.rearrange("(b t p) d -> b p t d", t=2, p=P)

            def store(r):
                sp.wait_ge(fin.sem, fin.at(r))
                sp.dma_start(ov[r.n], x[:, bass.ds(r.n * 2, 2), :]).then_inc(outs, 16)
            rounds(sp, store, B, 0, B - 1, 0, B // 2)
            sp.wait_ge(outs, 16 * B)

        @block.gpsimd
        def _(gp):
            c = 0

            def const(ins):
                nonlocal c
                c += 1
                ins.then_inc(consts.sem, 1)

            const(gp.memset(zeros[:], 0.0))
            const(gp.memset(ident[:], 0.0))
            const(gp.memset(headmask[:], 1.0))
            const(gp.memset(mhalf[:], -0.5))
            const(gp.memset(epsc[:], EPS))
            const(gp.memset(zeroc[:], 0.0))
            const(gp.memset(magicc[:], MAGIC))
            const(gp.memset(nmagic[:], -MAGIC))
            const(gp.memset(onesf[:], 1.0))
            const(gp.memset(onesb[:], 1.0))
            const(gp.memset(prob, 0.0))
            const(gp.memset(seen[:], 0.0))
            const(gp.iota(iota8[:], [[1, E]], base=0, channel_multiplier=0, allow_small_or_imprecise_dtypes=True))
            const(gp.iota(iotaT[:], [[1, TQ]], base=0, channel_multiplier=0, allow_small_or_imprecise_dtypes=True))
            gp.wait_ge(consts.sem, c)
            for e in range(SLOTS * D // (P * 1024)):
                gp.dma_start(disp.rearrange("(e p t) d -> e p (t d)", p=P, t=4)[e], zeros[:]).then_inc(zeroed, 16)
            gp.dma_start(vdram[:, TC:TCP, :], zeros[0:HB, 0:(TCP - TC) * B * 2 * DH].rearrange("h (k n) -> h k n", k=TCP - TC)).then_inc(vpad, 16)
            const(gp.affine_select(out=ident[:], in_=ident[:], compare_op=ALU.not_equal, fill=1.0, base=0, pattern=[[-1, P]], channel_multiplier=1))
            const(gp.affine_select(out=trib[:], in_=onesb[:], compare_op=ALU.is_ge, fill=0.0, base=0, pattern=[[1, P]], channel_multiplier=-1))
            const(gp.affine_select(out=headmask[:], in_=headmask[:], compare_op=ALU.is_ge, fill=0.0, base=0, pattern=[[-DH, P // DH]], channel_multiplier=1))
            gp.wait_ge(consts.sem, c)
            const(gp.affine_select(out=headmask[:], in_=headmask[:], compare_op=ALU.is_ge, fill=0.0, base=DH - 1, pattern=[[DH, P // DH]], channel_multiplier=-1))
            const(gp.tensor_copy(identb[:], ident[:]))
            assert c == CONSTS
            gp.wait_ge(consts.sem, c)

            def scales_of(r, ln, rs, ap, m, v, o, nm, nr):
                gp.wait_ge(ln.sem, ln.at(r, 4))
                gp.tensor_tensor(nm[:], zeroc[:], m[:, :, 0], ALU.subtract).then_inc(rs.sem, 1)
                gp.tensor_tensor(v[:], m[:, :, 1], epsc[:], ALU.add).then_inc(rs.sem, 1)
                gp.wait_ge(rs.sem, rs.at(r, 2))
                if r.shift(-1).valid:
                    gp.wait_ge(ap.sem, ap.at(r.shift(-1)))
                gp.tensor_tensor(o[:], v[:], mhalf[:], ALU.pow).then_inc(rs.sem, 1)
                gp.wait_ge(rs.sem, rs.at(r, 3))
                gp.tensor_tensor(nr[:], nm[:], o[:], ALU.mult).then_inc(rs.sem, 1)

            def keys(r):
                if r.shift(-2).valid:
                    gp.wait_ge(pS.sem, pS.at(r.shift(-2)))
                for k in range(DK):
                    ins = gp.tensor_tensor(kbd[:, r.parity, k], k0T[:, k, None, bass.ds(r.n * TC, TC)].broadcast_to([P, P // DH, TC]),
                                           headmask[:, :, None].broadcast_to([P, P // DH, TC]), ALU.mult)
                ins.then_inc(kb.sem, 1)

            def values(r):
                if r.shift(-2).valid:
                    gp.wait_ge(pAV.sem, pAV.at(r.shift(-2)))
                for g in range(2):
                    ins = gp.tensor_tensor(vblk[:, r.parity, g * KC:(g + 1) * KC, :, 0:DH],
                                           vpk[:, :, r.n, g, None, :].broadcast_to([P, KC, HB, DH]),
                                           headmask[:, None, :, None].broadcast_to([P, KC, HB, DH]), ALU.mult)
                ins.then_inc(vb.sem, 1)

            def scatter(r):
                gp.wait_ge(sl.sem, sl.at(r))
                alone(gp)
                for t in range(2):
                    gp.indirect_dma_start(out=disp, out_offset=bass.IndirectOffsetOnAxis(ap=slots[:, r.parity, t:t + 1], axis=0),
                                          in_=xn2[:, r.parity, t, :], in_offset=None, bounds_check=SLOTS - 1,
                                          oob_is_err=False).then_inc(scat[r.parity][t], 16)

            scales_of(Round(0, 0, B), ln1, rs1, ap1, mv, vare, rstd, nmean, nmr)
            gp.wait_ge(ek0.sem, 4)
            keys(Round(0, 0, B))
            scales_of(Round(0, 1, B), ln1, rs1, ap1, mv, vare, rstd, nmean, nmr)
            gp.wait_ge(vld, 16)
            for u in range(2):
                ins = gp.tensor_copy(vblk[:, u, :, :, DH], headmask[:, None, :].broadcast_to([P, NC, HB]))
            ins.then_inc(vones, 1)
            gp.wait_ge(vones, 1)
            values(Round(0, 0, B))

            def ctx2(r):
                if r.shift(-2).valid:
                    gp.wait_ge(pKV.sem, pKV.at(r.shift(-2)))
                gp.tensor_copy(ctxb[:, r.parity], ctxT[:, :, bass.ds(r.n * TC, TC)]).then_inc(cb2.sem, 1)
            ctx2(Round(0, 0, B))
            ctx2(Round(0, 1, B))
            gp.wait_ge(zeroed, 16 * (SLOTS * D // (P * 1024)))

            def body(r):
                if r.shift(1).valid:
                    keys(r.shift(1))
                    values(r.shift(1))
                if r.shift(-1).valid:
                    scales_of(r.shift(-1), ln2, rs2, ap2, mv2, vare2, rstd2, nmean2, nmr2)
                if r.shift(2).valid:
                    scales_of(r.shift(2), ln1, rs1, ap1, mv, vare, rstd, nmean, nmr)
                if r.shift(-1).valid:
                    scatter(r.shift(-1))
            rounds(gp, body, B, 0, B, 1, 3)
            with gp.Fori(1, B // 2) as i:
                ctx2(Round(i, 0, B))
                ctx2(Round(i, 1, B))

            gp.wait_ge(tan.sem, 2)
            gp.wait_ge(ld["bias"], 64)
            gp.tensor_scalar(bo[:], bo[:], gates4[:, 1:2], None, ALU.mult).then_inc(bosc, 1)
            gp.wait_ge(wp, 5)
            load_gu(gp, 1)
            gp.wait_ge(wp, 10)
            gp.dma_start(wnd, a["wd"].rearrange("(h p) i -> p h i", p=P)).then_inc(ld["wnat2"], 16)
            gp.wait_ge(bulk, 5)
            for u in range(2):
                gp.wait_ge(stored[u], 16 * (E // 2))

            def gather(lo, hi):
                for t in range(lo, hi):
                    gp.indirect_dma_start(out=yg[:, t, :], out_offset=None, in_=yexp,
                                          in_offset=bass.IndirectOffsetOnAxis(ap=slotg[:, t:t + 1], axis=0)).then_inc(gath[t], 16)

            def body3(r):
                if r.valid:
                    scales_of(r, ln3, rs3, ap3, mv, vare, rstd, nmean, nmr)
                q = r.shift(-1)
                if q.valid:
                    gp.wait_ge(ap3.sem, ap3.at(q))
                    gp.tensor_tensor(x[:, bass.ds(q.n * 2, 2), :], x[:, bass.ds(q.n * 2, 2), :],
                                     bo[:, None, :].broadcast_to([P, 2, D]), ALU.add).then_inc(x2b.sem, 1)

            gather(0, 6)
            gp.wait_ge(bosc, 1)
            body3(Round(0, 0, B))
            gather(6, 10)
            body3(Round(0, 1, B))
            gather(10, NT)
            with gp.Fori(1, B // 2) as i:
                body3(Round(i, 0, B))
                body3(Round(i, 1, B))
            body3(Round(0, B, B))

            def crossed(r):
                if r.shift(-2).valid:
                    gp.wait_ge(uf.sem, uf.at(r.shift(-2)))
                for m in range(2):
                    ins = gp.tensor_tensor(u2[:, r.parity, m].rearrange("p (h d) -> p h d", h=H),
                                           KVF[:, r.n, 1 - m, D:2 * D].rearrange("p (h d) -> p h d", h=H),
                                           wf[:, 2 + m, bass.ds(r.n * H, H)][:, :, None].broadcast_to([P, H, DH]), ALU.mult)
                ins.then_inc(uv.sem, 1)

            def body4(r):
                if r.shift(1).valid:
                    crossed(r.shift(1))
                if r.shift(-2).valid:
                    scales_of(r.shift(-2), ln4, rs4, ap4, mv2, vare2, rstd2, nmean2, nmr2)
            gp.wait_ge(eWF.sem, 1)
            rounds(gp, body4, B, -1, B + 1, 2, 3)
            gp.wait_ge(sc, 1)
            gp.partition_all_reduce(am2[:], am1[:], P, ABSMAX).then_inc(arx, 1)
            gp.wait_ge(hmx, IK * NQ + 3)
            gp.partition_all_reduce(am2[:], am1[:], P, ABSMAX).then_inc(arh, 1)

            def last(r):
                gp.wait_ge(dns.sem, dns.at(r))
                gp.tensor_tensor(x[:, bass.ds(r.n * 2, 2), :], x[:, bass.ds(r.n * 2, 2), :], xn[:, r.parity], ALU.add).then_inc(fin.sem, 1)
            rounds(gp, last, B, 0, B - 1, 0, B // 2)

        @block.tensor
        def _(pe):
            ring = (ps[:, 4], ps[:, 5])

            def mm(o, l, r, k, n):
                return pe.matmul(o, l, r, start=(k == 0), stop=(k == n - 1))

            def k0():
                pe.wait_ge(ld["ctxT"], 16)
                pe.wait_ge(ld["w0"], 16)
                for c in range(DK):
                    for n in range(2):
                        cols = slice(n * B * TC // 2, (n + 1) * B * TC // 2)
                        for k in range(DK):
                            ins = mm(ps[:, 2 * c + n, 0:B * TC // 2], w0[:, 1, k, c * P:(c + 1) * P], ctxT[:, k, cols], k, DK)
                        ins.then_inc(pk0.sem, 1)

            def v0():
                for b in range(B):
                    for k in range(DK):
                        ins = mm(ps[0:TC, 4 + b // 2, (b % 2) * D:(b % 2 + 1) * D], ctxT[:, k, b * TC:(b + 1) * TC], w0[:, 2, k], k, DK)
                    if b % 2:
                        ins.then_inc(pV, 1)

            def proj(r):
                pe.wait_ge(ap1.sem, ap1.at(r))
                prev = r.shift(-1)
                if prev.valid:
                    pe.wait_ge(ePT.sem, ePT.at(prev, 2))
                for t in range(2):
                    for k in range(DK):
                        ins = pe.transpose(ring[1][:, k * TQ + t * P:k * TQ + (t + 1) * P], xn[:, r.parity, t, k * P:(k + 1) * P], ident[:])
                ins.then_inc(pA.sem, 1)
                pe.wait_ge(eA.sem, eA.at(r, 1))
                if prev.valid:
                    pe.wait_ge(ePT.sem, ePT.at(prev, 3))
                for c in range(DK):
                    for k in range(DK):
                        ins = mm(ring[0][:, c * TQ:(c + 1) * TQ], w0[:, 0, k, c * P:(c + 1) * P], xnT[:, k], k, DK)
                ins.then_inc(pA.sem, 1)

            def scores(r, t):
                pe.wait_ge(eA.sem, eA.at(r))
                pe.wait_ge(kb.sem, kb.at(r))
                p = r if t else r.shift(-1)
                if p.valid:
                    pe.wait_ge(ms.sem, ms.at(p, 2 if t else 4))
                for h0, h1 in ((0, 6), (6, 8), (8, 12), (12, 16)):
                    c, n = h0 // 8, h0 // SH
                    ins = pe.matmul(ps[:, n, (h0 - n * SH) * TC:(h1 - n * SH) * TC], qT[:, r.parity, c, t * P:(t + 1) * P],
                                    kbd[:, r.parity, c, h0 - 8 * c:h1 - 8 * c, :].rearrange("p h k -> p (h k)"), start=True, stop=True)
                ins.then_inc(pS.sem, 1)

            def attend(r, t):
                pe.wait_ge(ex.sem, ex.at(r, t + 1))

                def turn(g):
                    n = r.shift(1)
                    if g == 2:
                        pe.wait_ge(ePT.sem, ePT.at(r, NG * t + 1))
                    elif not t and r.shift(-1).valid:
                        pe.wait_ge(ePT.sem, ePT.at(r.shift(-1), NG + 2 + g))
                    elif not t:
                        pe.wait_ge(eA.sem, eA.at(r))
                    elif n.valid:
                        pe.wait_ge(eA.sem, eA.at(n, 1 + g))
                    else:
                        pe.wait_ge(ePT.sem, ePT.at(r, 2 + g))
                    blocks = [prob[:, t, h:h + HB].rearrange("p h k -> p (h k)") for h in range(0, H, HB)]
                    for c in range(*GROUPS[g]):
                        o = c - GROUPS[g][0]
                        ins = pe.transpose(ring[(g + t) % 2][:, o * P:(o + 1) * P], blocks[c // KC][:, c % KC::KC], ident[:])
                    ins.then_inc(pPT.sem, 1)

                def values(g):
                    pe.wait_ge(ePT.sem, ePT.at(r, NG * t + g + 1))
                    for c in range(*GROUPS[g]):
                        n = HB * (DH + 1)
                        ins = mm(ps[:, 6, c // KC * n:(c // KC + 1) * n], probT[:, t, c], vblk[:, r.parity, c].rearrange("p h d -> p (h d)"), c % KC, KC)
                    return ins

                turn(0)
                turn(1)
                turn(2)
                p = r if t else r.shift(-1)
                if p.valid:
                    pe.wait_ge(nv.sem, nv.at(p, 2 if t else 4))
                pe.wait_ge(vb.sem, vb.at(r))
                values(0)
                values(1)
                values(2).then_inc(pAV.sem, 1)

            def turn_out(r, t):
                pe.wait_ge(nv.sem, nv.at(r, 2 * t + 2))
                if t == 1 and r.shift(-1).valid:
                    pe.wait_ge(eX2.sem, eX2.at(r.shift(-1), 2))
                for k in range(DK):
                    ins = pe.transpose(ps[:, 7, k * P:(k + 1) * P], ao[:, t, k * P:(k + 1) * P], ident[:])
                ins.then_inc(pOT.sem, 1)

            def project(r, t):
                pe.wait_ge(eOT.sem, eOT.at(r, t + 1))
                if t and r.shift(-1).valid:
                    pe.wait_ge(sl.sem, sl.at(r.shift(-1), 1))
                if not t and r.shift(-1).valid:
                    pe.wait_ge(gx.sem, gx.at(r.shift(-1)))
                if t and not r.shift(-1).valid:
                    pe.wait_ge(x1s.sem, x1s.at(r, 1))
                for k in range(DK):
                    ins = mm(ps[:, 3, 0:D], aoT[:, t, k], w0[:, 3, k], k, DK)
                ins.then_inc(pWO.sem, 1)

            def router(r):
                pe.wait_ge(ap2.sem, ap2.at(r))
                for t in range(2):
                    if t == 1:
                        pe.wait_ge(eX2.sem, eX2.at(r, 1))
                    elif r.shift(1).valid:
                        pe.wait_ge(eOT.sem, eOT.at(r.shift(1), 1))
                    for k in range(DK):
                        ins = pe.transpose(ps[:, 7, k * P:(k + 1) * P], xn2[:, r.parity, t, k * P:(k + 1) * P], ident[:])
                    ins.then_inc(pX2.sem, 1)
                for t in range(2):
                    pe.wait_ge(eX2.sem, eX2.at(r, t + 1))
                    for k in range(DK):
                        ins = mm(ps[:, 3, t * E:(t + 1) * E], x2T[:, t, k], wg[:, k], k, DK)
                ins.then_inc(pLG.sem, 1)

            def positions(r):
                pe.wait_ge(ga.sem, ga.at(r))
                pe.wait_ge(gx.sem, gx.at(r))
                if r.shift(1).valid:
                    pe.wait_ge(x1s.sem, x1s.at(r.shift(1), 1))
                for t in range(2):
                    o = ps[:, 3, t * E:(t + 1) * E]
                    pe.matmul(o, onesb[:], seen[:, r.parity], start=True, stop=False)
                    if t:
                        pe.matmul(o, onesb[:], mask[:, r.parity, 0], start=False, stop=False)
                    ins = pe.matmul(o, trib[:], mask[:, r.parity, t], start=False, stop=True)
                ins.then_inc(pLOC.sem, 1)

            def body(r):
                b, p, n = r, r.shift(-1), r.shift(1)
                if b.valid:
                    scores(b, 1)
                if p.valid:
                    turn_out(p, 1)
                if b.valid:
                    attend(b, 0)
                if p.valid:
                    project(p, 1)
                if n.valid:
                    proj(n)
                    scores(n, 0)
                if b.valid:
                    turn_out(b, 0)
                if p.valid:
                    router(p)
                if b.valid:
                    attend(b, 1)
                    project(b, 0)
                if p.valid:
                    positions(p)

            pe.wait_ge(consts.sem, CONSTS)
            k0()
            v0()
            pe.wait_ge(ek0.sem, 4)
            pe.wait_ge(eV, B)
            pe.wait_ge(ld["small"], 48)
            rounds(pe, body, B, -1, B, 1, 3)

            pe.wait_ge(ld["w1a"], 16)
            pe.wait_ge(ld["dft"], 16)

            def kv_time(r):
                pe.wait_ge(cb2.sem, cb2.at(r))
                if r.shift(-1).valid:
                    pe.wait_ge(eKV.sem, eKV.at(r.shift(-1)))
                else:
                    pe.wait_ge(ms.sem, ms.at(Round(0, B - 1, B)))
                for half in range(2):
                    for k in range(DK):
                        ins = mm(ps[0:TC, 0, half * D:(half + 1) * D], ctxb[:, r.parity, k], w1a[:, 1 + half, k], k, DK)
                ins.then_inc(pKV.sem, 1)

            def kv_freq(r):
                pe.wait_ge(eKV.sem, eKV.at(r))
                if r.shift(-1).valid:
                    pe.wait_ge(eKF.sem, eKF.at(r.shift(-1)))
                for m in range(2):
                    ins = pe.matmul(ps[:, 2 + m, :], dft[0:TC, 0, m * P:(m + 1) * P], kv[:, r.parity], start=True, stop=True)
                ins.then_inc(pKF.sem, 1)

            def kv_body(r):
                if r.valid:
                    kv_time(r)
                if r.shift(-1).valid:
                    kv_freq(r.shift(-1))
            rounds(pe, kv_body, B, 0, B, 1, B // 2)

            def dsp_turn(r):
                pe.wait_ge(lddsp[r.parity], 16 * (r.half + 1))
                if r.shift(-2).valid:
                    pe.wait_ge(eD.sem, eD.at(r.shift(-2)))
                else:
                    pe.wait_ge(eKF.sem, eKF.at(Round(0, B - 1, B)))
                for t in range(2):
                    for k in range(DK):
                        ins = pe.transpose(ps[:, r.parity, k * CAP + t * P:k * CAP + (t + 1) * P], dsp[:, r.parity, t, k * P:(k + 1) * P], ident[:])
                ins.then_inc(pD.sem, 1)

            def up(r):
                pe.wait_ge(ldw1[r.parity], 16 * (r.half + 1))
                pe.wait_ge(eD.sem, eD.at(r))
                for g in range(FK // 2):
                    if r.shift(-1).valid:
                        pe.wait_ge(gl.sem, gl.at(r.shift(-1), 2 * g + 2))
                    for j in range(2):
                        f = 2 * g + j
                        for k in range(DK):
                            ins = mm(ps[:, 2 + g, j * CAP:(j + 1) * CAP], w1[:, r.parity, k, f * P:(f + 1) * P], dspT[:, r.parity, k], k, DK)
                    ins.then_inc(pG1.sem, 1)

            def down(r):
                pe.wait_ge(ldw2[r.parity], 16 * (r.half + 1))
                pe.wait_ge(gl.sem, gl.at(r))
                if r.shift(-2).valid:
                    pe.wait_ge(ye.sem, ye.at(r.shift(-2)))
                for t in range(2):
                    for f in range(FK):
                        ins = mm(ps[:, 6 + r.parity, t * D:(t + 1) * D], hid[:, r.parity, f, t * P:(t + 1) * P], w2[:, r.parity, f], f, FK)
                ins.then_inc(pG2.sem, 1)

            def expert(r):
                if r.shift(1).valid:
                    dsp_turn(r.shift(1))
                if r.valid:
                    up(r)
                if r.shift(-1).valid:
                    down(r.shift(-1))
            rounds(pe, expert, E, -1, E, 1, 3)

            def turn_gu(m, first):
                pe.wait_ge(wp, 5 * (m + 1))
                for k in range(DK):
                    dst = ps[:, 4 + k, 0:IK * P // 2].bitcast(BF16)
                    if m == 1:
                        pe.wait_ge(ewp, k + 1)
                    else:
                        pe.wait_ge(gl.sem, gl.at(Round(0, E - 1, E)))
                    for i in range(IK):
                        n = P if i < IK - 1 else TAIL
                        ins = pe.transpose(dst[:, i * P:i * P + n], wqs[m][0:n, i, k * P:(k + 1) * P], identb[0:n, 0:n])
                    ins.then_inc(pwp, 1)
            for m in range(2):
                turn_gu(m, m == 0)
            pe.wait_ge(wp, 15)
            for g in range(2):
                pe.wait_ge(ewp, 3 + g)
                dst = ps[:, 4 + g, 0:3 * D // 2].bitcast(BF16).rearrange("p (m d) -> p m d", m=3)
                for i in range(3):
                    m = 3 * g + i
                    n = P if m < IK - 1 else TAIL
                    for h in range(2):
                        ins = pe.transpose(dst[0:n, i, h * P:(h + 1) * P], wqd[:, h, m * P:m * P + n], identb[:])
                ins.then_inc(pwp, 1)
            pe.wait_ge(wp, 17)
            for h in range(2):
                ins = pe.matmul(ps[:, 2, h * P:(h + 1) * P], onesf[:], diag[:, h], start=True, stop=True)
            ins.then_inc(pwp, 1)

            def xspec(r):
                pe.wait_ge(ap3.sem, ap3.at(r))
                if r.shift(-2).valid:
                    pe.wait_ge(eXH.sem, eXH.at(r.shift(-2)))
                for m in range(DK):
                    for k in range(DK):
                        ins = mm(ps[:, r.parity, m * TQ:(m + 1) * TQ], xn[:, r.parity, k, m * P:(m + 1) * P], dft[:, k], k, DK)
                ins.then_inc(pXH.sem, 1)

            def qspec(r):
                pe.wait_ge(eXH.sem, eXH.at(r))
                if r.shift(-2).valid:
                    pe.wait_ge(pr.sem, pr.at(r.shift(-2), 3))
                else:
                    pe.wait_ge(ye.sem, ye.at(Round(0, E - 1, E)))
                for m in range(2):
                    o = ps[:, 6 + r.parity, m * D:(m + 1) * D]
                    for k in range(DK):
                        ins = pe.matmul(o, xh[:, r.parity, k, m * P:(m + 1) * P], w1a[:, 0, k], start=(k == 0), stop=(m == 1 and k == 1))
                    if m == 0:
                        pe.matmul(o, dcrow[:], bq[:], start=False, stop=True)
                ins.then_inc(pQF.sem, 1)

            def spectra(r):
                if r.valid:
                    xspec(r)
                if r.shift(-1).valid:
                    qspec(r.shift(-1))
            pe.wait_ge(ld["bias"], 64)
            rounds(pe, spectra, B, 0, B, 2, B // 2)
            pe.wait_ge(pr.sem, pr.at(Round(0, B - 1, B)))
            pe.wait_ge(ld["corrm"], 16)
            for j in range(4):
                ins = mm(ps[:, 3, 0:TQ], pc[:, j].rearrange("p b h -> p (b h)"), corrm[:, j], j, 4)
            ins.then_inc(pCO.sem, 1)
            pe.wait_ge(tk.sem, tk.per)
            for k in range(DK):
                ins = pe.transpose(ps[:, 3, TQ + k * P:TQ + (k + 1) * P], wts[:, 0, k * P:(k + 1) * P], ident[:])
            ins.then_inc(pWT.sem, 1)
            pe.wait_ge(eWT.sem, 1)
            pe.wait_ge(ld["wdft"], 16)
            for j in range(4):
                for k in range(DK):
                    ins = mm(ps[:, 7, j * P:(j + 1) * P], wdft[:, j, k], wtT[:, k], k, DK)
            ins.then_inc(pWF.sem, 1)

            def back(r):
                pe.wait_ge(uf.sem, uf.at(r))
                if r.shift(-2).valid:
                    pe.wait_ge(eOI.sem, eOI.at(r.shift(-2)))
                for m in range(DK):
                    for k in range(DK):
                        ins = mm(ps[:, r.parity, m * TQ:(m + 1) * TQ], of[:, r.parity, k, m * P:(m + 1) * P], idft[:, k], k, DK)
                ins.then_inc(pOI.sem, 1)

            def project1(r):
                pe.wait_ge(eOI.sem, eOI.at(r))
                if r.shift(-2).valid:
                    pe.wait_ge(x3s.sem, x3s.at(r.shift(-2)))
                for t in range(2):
                    for k in range(DK):
                        ins = mm(ps[:, 4 + r.parity, t * D:(t + 1) * D], oT[:, r.parity, k, t * P:(t + 1) * P], w1a[:, 3, k], k, DK)
                ins.then_inc(pY.sem, 1)

            def backs(r):
                if r.valid:
                    back(r)
                if r.shift(-1).valid:
                    project1(r.shift(-1))
            pe.wait_ge(ld["idft"], 16)
            pe.wait_ge(ewp, 8)
            rounds(pe, backs, B, 0, B, 2, B // 2)

            def turn_x(r):
                pe.wait_ge(xqs.sem, xqs.at(r))
                if r.shift(-2).valid:
                    pe.wait_ge(eXQ.sem, eXQ.at(r.shift(-2)))
                dst = ps[:, r.parity, 0:TQ].bitcast(BF16).rearrange("p (k s) -> p k s", k=DK)
                for t in range(2):
                    for k in range(DK):
                        ins = pe.transpose(dst[:, k, t * P:(t + 1) * P], xq[:, r.parity, t, k * P:(k + 1) * P], identb[:])
                ins.then_inc(pXQ.sem, 1)

            def gate_up(r):
                pe.wait_ge(eXQ.sem, (r.n + 1) * 2)
                for m in range(IK):
                    n = P if m < IK - 1 else TAIL
                    q = (r, m - 3) if m >= 3 else (r.shift(-1), m + 3)
                    if q[0].valid:
                        pe.wait_ge(hh.sem, hh.at(q[0], q[1] + 1))
                    for g in range(2):
                        for k in range(DK):
                            ins = mm(ps[0:n, 2 + 2 * (m % 3) + g, :], wgT[:, g, k, m * P:m * P + n], xqT[:, k, bass.ds(r.n * NB, NB)], k, DK)
                    ins.then_inc(pGU.sem, 1)
                    if m == 2 and r.n < NQ - 1:
                        for t in range(2):
                            turn_x(batch_of(r.n + 1, t))
            for t in range(2):
                turn_x(batch_of(0, t))
            for n in range(NQ):
                gate_up(Round(0, n, NQ))

            def down_last(r):
                pe.wait_ge(hqa.sem, hqa.at(r))
                pe.wait_ge(hqv.sem, hqv.at(r))
                if r.shift(-2).valid:
                    pe.wait_ge(dns.sem, dns.at(r.shift(-2)))
                for t in range(2):
                    for m in range(IK):
                        n = P if m < IK - 1 else TAIL
                        ins = mm(ps[:, r.parity, t * D:(t + 1) * D], hq[0:n, r.parity, m, t * P:(t + 1) * P], wdT[0:n, m], m, IK)
                ins.then_inc(pDN.sem, 1)
            rounds(pe, down_last, B, 0, B - 1, 1, B // 2)

        @block.scalar
        def _(act):
            act.wait_ge(ld["small"], 48)
            act.activation(gates4[:], gates4[:], ACT.Tanh).then_inc(tan.sem, 1)
            act.activation(clips[:], clips[:], ACT.Exp, scale=-1.0).then_inc(tan.sem, 1)
            for n in range(4):
                act.wait_ge(pk0.sem, n + 1)
                act.copy(k0T[:, n // 2, (n % 2) * B * TC // 2:(n % 2 + 1) * B * TC // 2], ps[:, n, 0:B * TC // 2]).then_inc(ek0.sem, 1)

            def probs(r, t):
                act.wait_ge(ms.sem, ms.at(r, 2 * t + 2))
                v = prob[:, t, :, 0:TC]
                act.activation(v, v, ACT.Exp).then_inc(ex.sem, 1)

            def copy_out(r, t):
                act.wait_ge(pOT.sem, pOT.at(r, t + 1))
                if r.shift(-1).valid:
                    act.wait_ge(pWO.sem, pWO.at(r.shift(-1), t + 1))
                act.copy(aoT[:, t].rearrange("p k s -> p (k s)"), ps[:, 7, 0:2 * P]).then_inc(eOT.sem, 1)

            def copy_probs(r, t):
                if r.shift(-1).valid:
                    act.wait_ge(pAV.sem, pAV.at(r.shift(-1), t + 1))
                for g, (lo, hi) in enumerate(GROUPS):
                    act.wait_ge(pPT.sem, pPT.at(r, NG * t + g + 1))
                    act.copy(probT[:, t, lo:hi].rearrange("p c s -> p (c s)"), ps[:, 4 + (g + t) % 2, 0:(hi - lo) * P]).then_inc(ePT.sem, 1)

            def copy_proj(r):
                act.wait_ge(pA.sem, pA.at(r, 1))
                if r.shift(-1).valid:
                    act.wait_ge(pA.sem, pA.at(r.shift(-1), 2))
                act.copy(xnT[:].rearrange("p k s -> p (k s)"), ps[:, 5, :]).then_inc(eA.sem, 1)
                act.wait_ge(pA.sem, pA.at(r, 2))
                if r.shift(-2).valid:
                    act.wait_ge(pS.sem, pS.at(r.shift(-2)))
                act.mul(qT[:, r.parity].rearrange("p k s -> p (k s)"), ps[:, 4, :], DH ** -0.5).then_inc(eA.sem, 1)

            def normalise_with(r, rs, ap, rr, nr, dst):
                act.wait_ge(rs.sem, rs.at(r))
                for t in range(2):
                    act.activation(dst(t), x[:, r.n * 2 + t, :], ACT.Identity, bias=nr[:, t:t + 1], scale=rr[:, t:t + 1]).then_inc(ap.sem, 1)

            def norm1(r):
                if r.shift(-2).valid:
                    act.wait_ge(pA.sem, pA.at(r.shift(-2), 1))
                normalise_with(r, rs1, ap1, rstd, nmr, lambda t: xn[:, r.parity, t])

            def norm2(r):
                if r.shift(-2).valid:
                    for t in range(2):
                        act.wait_ge(scat[r.parity][t], 16 * r.half)
                    act.wait_ge(pX2.sem, pX2.at(r.shift(-2)))
                normalise_with(r, rs2, ap2, rstd2, nmr2, lambda t: xn2[:, r.parity, t])

            def copy_router(r):
                if r.shift(-1).valid:
                    act.wait_ge(pLG.sem, pLG.at(r.shift(-1)))
                for t in range(2):
                    act.wait_ge(pX2.sem, pX2.at(r, t + 1))
                    act.copy(x2T[:, t].rearrange("p k s -> p (k s)"), ps[:, 7, 0:2 * P]).then_inc(eX2.sem, 1)

            def gate(r):
                act.wait_ge(ga.sem, ga.at(r, 5))
                for t in range(2):
                    act.activation(gexp[:, t], ps[:, 3, t * E:(t + 1) * E], ACT.Exp, bias=ntop[:, t:t + 1],
                                   accum_out=gsum[:, bass.ds(r.n * 2 + t, 1)]).then_inc(gx.sem, 1)

            def body(r):
                b, p, n = r, r.shift(-1), r.shift(1)
                if p.valid:
                    copy_out(p, 1)
                if b.valid:
                    copy_probs(b, 0)
                    probs(b, 1)
                if n.valid:
                    copy_proj(n)
                if p.valid:
                    norm2(p)
                if b.valid:
                    copy_out(b, 0)
                if p.valid:
                    copy_router(p)
                if b.valid:
                    copy_probs(b, 1)
                if p.valid:
                    gate(p)
                if n.valid:
                    probs(n, 0)
                if r.shift(2).valid:
                    norm1(r.shift(2))
            act.wait_ge(consts.sem, CONSTS)
            norm1(Round(0, 0, B))
            rounds(act, body, B, -1, B, 1, 3)

            def copy_kf(r):
                act.wait_ge(pKF.sem, pKF.at(r))
                for m in range(2):
                    act.copy(KVF[:, r.n, m, :], ps[:, 2 + m, :]).then_inc(eKF.sem, 1)
            rounds(act, copy_kf, B, 0, B - 1, 1, B // 2)

            def gelu(r):
                if r.shift(-2).valid:
                    act.wait_ge(pG2.sem, pG2.at(r.shift(-2)))
                for f in range(FK):
                    act.wait_ge(pG1.sem, pG1.at(r, f // 2 + 1))
                    act.activation(hid[:, r.parity, f], ps[:, 2 + f // 2, (f % 2) * CAP:(f % 2 + 1) * CAP], ACT.Gelu_apprx_tanh,
                                   bias=b1[:, bass.ds(r.n * FK + f, 1)]).then_inc(gl.sem, 1)
            act.wait_ge(ld["b1"], 16)
            yv = yexp.rearrange("(e t p) d -> e p t d", e=E, p=P)

            def gelu_store(r):
                if r.valid:
                    gelu(r)
                q = r.shift(-1)
                if q.valid:
                    act.wait_ge(ye.sem, ye.at(q))
                    act.dma_start(yv[q.n], yex[:, q.parity]).then_inc(stored[q.parity], 16)
            rounds(act, gelu_store, E, 0, E, 1, E // 2)

            for m in range(2):
                for k in range(DK):
                    act.wait_ge(pwp, 2 * m + k + 1)
                    act.copy(wgT[:, m, k], ps[:, 4 + k, 0:I // 2].bitcast(BF16)).then_inc(ewp, 1)
            for g in range(2):
                act.wait_ge(pwp, 5 + g)
                src = ps[:, 4 + g, 0:3 * D // 2].bitcast(BF16)
                if g == 0:
                    act.copy(wdT[:, 0:3].rearrange("p m d -> p (m d)"), src).then_inc(ewp, 1)
                else:
                    act.copy(wdT[:, 3:5].rearrange("p m d -> p (m d)"), src[:, 0:2 * D]).then_inc(ewp, 1)
                    act.copy(wdT[0:TAIL, 5], src[0:TAIL, 2 * D:3 * D]).then_inc(ewp, 1)
            act.wait_ge(pwp, 7)
            act.copy(dscale[:], ps[:, 2, 0:D]).then_inc(ewp, 1)

            def copy_xh(r):
                act.wait_ge(pXH.sem, pXH.at(r))
                if r.shift(-2).valid:
                    act.wait_ge(pQF.sem, pQF.at(r.shift(-2)))
                act.copy(xh[:, r.parity].rearrange("p k s -> p (k s)"), ps[:, r.parity, :]).then_inc(eXH.sem, 1)

            def spectra(r):
                if r.valid:
                    if r.shift(-2).valid:
                        act.wait_ge(pXH.sem, pXH.at(r.shift(-2)))
                    normalise_with(r, rs3, ap3, rstd, nmr, lambda t: xn[:, r.parity, t])
                if r.shift(-1).valid:
                    copy_xh(r.shift(-1))
            rounds(act, spectra, B, 0, B, 2, B // 2)

            act.wait_ge(tk.sem, 4)
            act.activation(cw[:], c8[:, 0:TOPK], ACT.Exp, bias=nc0[:], accum_out=cs[:]).then_inc(tx.sem, 1)
            act.wait_ge(pWT.sem, 1)
            act.copy(wtT[:].rearrange("p k s -> p (k s)"), ps[:, 3, TQ:2 * TQ]).then_inc(eWT.sem, 1)
            act.wait_ge(pWF.sem, 1)
            act.copy(wf[:].rearrange("p j s -> p (j s)"), ps[:, 7, :]).then_inc(eWF.sem, 1)

            def copy_back(r):
                act.wait_ge(pOI.sem, pOI.at(r))
                if r.shift(-2).valid:
                    act.wait_ge(pY.sem, pY.at(r.shift(-2)))
                act.copy(oT[:, r.parity].rearrange("p k s -> p (k s)"), ps[:, r.parity, :]).then_inc(eOI.sem, 1)

            def back(r):
                if r.valid:
                    copy_back(r)
                q = r.shift(-2)
                if q.valid:
                    normalise_with(q, rs4, ap4, rstd2, nmr2, lambda t: yg[:, q.n * 2 + t, :])
            rounds(act, back, B, 0, B + 1, 1, B // 2)

            def round_x(r):
                f = yg[:, bass.ds(r.n * 2, 2), :]
                act.activation(f, f, ACT.Identity, bias=magicc[:], scale=sx[:, 1:2]).then_inc(xq1.sem, 1)

            def copy_xq(r):
                act.wait_ge(pXQ.sem, pXQ.at(r))
                act.copy(xqT[:, :, bass.ds(r.n * TQ, TQ)],
                         ps[:, r.parity, 0:TQ].bitcast(BF16).rearrange("p (k s) -> p k s", k=DK)).then_inc(eXQ.sem, 1)

            def silu(r):
                for m in range(IK):
                    n = P if m < IK - 1 else TAIL
                    act.wait_ge(pGU.sem, pGU.at(r, m + 1))
                    q = (r, m - 2) if m >= 2 else (r.shift(-1), m + IK - 2)
                    if q[0].valid:
                        act.wait_ge(hh.sem, hh.at(q[0], q[1] + 1))
                    act.activation(sil[0:n, m % 2], ps[0:n, 2 + 2 * (m % 3), :], ACT.Silu, scale=sgu[0:n, 0, m:m + 1]).then_inc(si.sem, 1)
                    if m == 3 and r.n < NQ - 1:
                        for t in range(2):
                            copy_xq(batch_of(r.n + 1, t))
            act.wait_ge(sc, 4)
            for n in range(B):
                round_x(Round(0, n, B))
            for t in range(2):
                copy_xq(batch_of(0, t))
            for n in range(NQ):
                silu(Round(0, n, NQ))

            act.wait_ge(sch, 5)

            def quant_h(r):
                if r.valid:
                    if r.shift(-2).valid:
                        act.wait_ge(hqv.sem, hqv.at(r.shift(-2)))
                        act.wait_ge(hqa.sem, hqa.at(r.shift(-2)))
                    act.activation(hr[:, r.parity], hT[:, :, bass.ds(r.n * TQ, TQ)], ACT.Identity, bias=magicc[:], scale=sx[:, 1:2]).then_inc(hq1.sem, 1)
                q = r.shift(-1)
                if q.valid:
                    act.wait_ge(hqc.sem, hqc.at(q))
                    if q.shift(-2).valid:
                        act.wait_ge(pDN.sem, pDN.at(q.shift(-2)))
                    act.activation(hq[:, q.parity, 0:HA], hr[:, q.parity, 0:HA], ACT.Identity, bias=nmagic[:]).then_inc(hqa.sem, 1)
            rounds(act, quant_h, B, 0, B, 2, B // 2)

        @block.vector
        def _(dv):
            def statistics(r, ln, rs, s, m):
                if r.shift(-1).valid:
                    dv.wait_ge(rs.sem, rs.at(r.shift(-1)))
                alone(dv)
                for t in range(2):
                    dv.bn_stats(s[:, t], tile_of(r, t)).then_inc(ln.sem, 1)
                dv.wait_ge(ln.sem, ln.at(r, 2))
                alone(dv)
                for t in range(2):
                    dv.bn_aggr(m[:, t], s[:, t]).then_inc(ln.sem, 1)

            def tile_of(r, t):
                return x[:, r.n * 2 + t, :]

            def norm1(r):
                statistics(r, ln1, rs1, st, mv)

            def less_max(r, t):
                dv.wait_ge(pS.sem, pS.at(r, t + 1))
                whole, n = H // SH, H % SH
                s = ps[:, 0:whole, 0:SH * TC].rearrange("p n (h k) -> p n h k", h=SH)
                s4 = ps[:, whole, 0:n * TC].rearrange("p (h k) -> p h k", h=n)
                dv.tensor_reduce(mx[:, t, 0:whole * SH].rearrange("p (n h) -> p n h", h=SH), s, AX_X, ALU.max)
                dv.tensor_reduce(mx[:, t, whole * SH:H], s4, AX_X, ALU.max).then_inc(ms.sem, 1)
                dv.wait_ge(ms.sem, ms.at(r, 2 * t + 1))
                if r.shift(-1).valid:
                    dv.wait_ge(pPT.sem, pPT.at(r.shift(-1), NG * (t + 1)))
                dv.tensor_tensor(prob[:, t, 0:whole * SH, 0:TC].rearrange("p (n h) k -> p n h k", h=SH), s,
                                 mx[:, t, 0:whole * SH].rearrange("p (n h) -> p n h", h=SH)[:, :, :, None].broadcast_to([P, whole, SH, TC]),
                                 ALU.subtract)
                dv.tensor_tensor(prob[:, t, whole * SH:H, 0:TC], s4, mx[:, t, whole * SH:H][:, :, None].broadcast_to([P, n, TC]),
                                 ALU.subtract).then_inc(ms.sem, 1)

            def normalise(r, t):
                dv.wait_ge(pAV.sem, pAV.at(r, t + 1))
                v = ps[:, 6, 0:H * (DH + 1)].rearrange("p (h d) -> p h d", h=H)
                dv.reciprocal(rden[:, t], v[:, :, DH]).then_inc(nv.sem, 1)
                dv.wait_ge(nv.sem, nv.at(r, 2 * t + 1))
                if r.shift(-1).valid:
                    dv.wait_ge(pOT.sem, pOT.at(r.shift(-1), t + 1))
                dv.tensor_tensor(ao[:, t].rearrange("p (h d) -> p h d", h=H), v[:, :, 0:DH],
                                 rden[:, t][:, :, None].broadcast_to([P, H, DH]), ALU.mult).then_inc(nv.sem, 1)

            def residual1(r, t):
                dv.wait_ge(pWO.sem, pWO.at(r, t + 1))
                dv.scalar_tensor_tensor(tile_of(r, t), ps[:, 3, 0:D], gates4[:, 0:1], tile_of(r, t), ALU.mult, ALU.add).then_inc(x1s.sem, 1)

            def norm2(r):
                dv.wait_ge(x1s.sem, x1s.at(r))
                statistics(r, ln2, rs2, st2, mv2)

            def choose(r):
                dv.wait_ge(pLG.sem, pLG.at(r))
                alone(dv)
                lg = ps[:, 3, 0:2 * E].rearrange("p (t e) -> p t e", t=2)
                for t in range(2):
                    dv.max(top[:, t], lg[:, t]).then_inc(ga.sem, 1)
                dv.wait_ge(ga.sem, ga.at(r, 2))
                if r.shift(-1).valid:
                    dv.wait_ge(gx.sem, gx.at(r.shift(-1)))
                dv.tensor_scalar(ntop[:], top[:, :, 0], -1.0, None, ALU.mult).then_inc(ga.sem, 1)
                for t in range(2):
                    dv.max_index(topi[:, t], top[:, t], lg[:, t]).then_inc(ga.sem, 1)
                dv.wait_ge(ga.sem, ga.at(r, 5))
                dv.tensor_copy(eidx[:, r.parity], topi[:, :, 0]).then_inc(ga.sem, 1)
                dv.wait_ge(ga.sem, ga.at(r, 6))
                if r.shift(-2).valid:
                    dv.wait_ge(pLOC.sem, pLOC.at(r.shift(-2)))
                dv.tensor_tensor(mask[:, r.parity], iota8[:, None, :].broadcast_to([P, 2, E]),
                                 eidx[:, r.parity][:, :, None].broadcast_to([P, 2, E]), ALU.is_equal).then_inc(ga.sem, 1)
                dv.wait_ge(ga.sem, ga.at(r, 7))
                dv.tensor_tensor(seen1[:], mask[:, r.parity, 0], mask[:, r.parity, 1], ALU.add).then_inc(ga.sem, 1)
                dv.wait_ge(ga.sem, ga.at(r, 8))
                if r.shift(-1).valid:
                    dv.wait_ge(pLOC.sem, pLOC.at(r.shift(-1)))
                dv.tensor_tensor(seen[:, 1 - r.parity], seen[:, r.parity], seen1[:], ALU.add).then_inc(ga.sem, 1)

            def place(r):
                n = 0

                def step(ins):
                    nonlocal n
                    n += 1
                    ins.then_inc(sl.sem, 1)
                    dv.wait_ge(sl.sem, sl.at(r, n))
                dv.wait_ge(pLOC.sem, pLOC.at(r))
                dv.wait_ge(gx.sem, gx.at(r))
                lo = ps[:, 3, 0:2 * E].rearrange("p (t e) -> p t e", t=2)
                step(dv.tensor_tensor(lm[:], lo, mask[:, r.parity], ALU.mult))
                step(dv.tensor_reduce(pos[:], lm[:], AX_X, ALU.add))
                at = bass.ds(r.n * 2, 2)
                step(dv.scalar_tensor_tensor(slot[:, at], eidx[:, r.parity], float(CAP), pos[:], ALU.mult, ALU.add))
                step(dv.tensor_scalar(keep[:, at], pos[:], float(CAP), None, ALU.is_le))
                step(dv.tensor_scalar(skip[:], keep[:, at], -2.0 * SLOTS, 2.0 * SLOTS - 1, ALU.mult, ALU.add))
                if r.shift(-2).valid:
                    for t in range(2):
                        dv.wait_ge(scat[r.parity][t], 16 * r.half)
                step(dv.tensor_tensor(slots[:, r.parity], slot[:, at], skip[:], ALU.add))
                assert n == sl.per

            def body(r):
                b, p, n = r, r.shift(-1), r.shift(1)
                if b.valid:
                    less_max(b, 1)
                    normalise(b, 0)
                if p.valid:
                    residual1(p, 1)
                    norm2(p)
                if n.valid:
                    less_max(n, 0)
                if r.shift(2).valid:
                    norm1(r.shift(2))
                if p.valid:
                    choose(p)
                if b.valid:
                    normalise(b, 1)
                    residual1(b, 0)
                if p.valid:
                    place(p)
            dv.memset(wnat[TAIL:P, IK - 1, :], 1.0).then_inc(wtail, 1)
            dv.wait_ge(ld["x0"], 16)
            norm1(Round(0, 0, B))
            norm1(Round(0, 1, B))
            for b in range(B):
                dv.wait_ge(pV, b // 2 + 1)
                dv.tensor_copy(v0s[:, :, b], ps[0:TC, 4 + b // 2, (b % 2) * D:(b % 2 + 1) * D].rearrange("k (g h d) -> k h g d", g=2, h=HB)).then_inc(eV, 1)
            dv.wait_ge(tan.sem, 2)
            dv.wait_ge(consts.sem, CONSTS)
            dv.wait_ge(ld["x1"], 16)
            less_max(Round(0, 0, B), 0)
            rounds(dv, body, B, 0, B, 1, 3)

            dv.tensor_scalar(slot[:], slot[:], -1.0, float(SLOTS - 1), ALU.add, ALU.min).then_inc(bulk, 1)
            dv.reciprocal(grec[:], gsum[:]).then_inc(bulk, 1)
            dv.wait_ge(bulk, 2)
            dv.tensor_copy(slotg[:], slot[:]).then_inc(bulk, 1)
            dv.tensor_scalar(grec[:], grec[:], gates4[:, 2:3], None, ALU.mult).then_inc(bulk, 1)
            dv.wait_ge(bulk, 4)
            dv.tensor_tensor(gk[:], grec[:], keep[:], ALU.mult).then_inc(bulk, 1)

            dv.tensor_scalar(clips[:], clips[:], QMAX, QMAX, ALU.mult, ALU.add).then_inc(sch, 1)
            dv.wait_ge(sch, 1)
            dv.reciprocal(clipr[:], clips[:]).then_inc(sch, 1)

            dv.wait_ge(ld["bias"], 64)

            def bias_kv(r):
                dv.wait_ge(pKV.sem, pKV.at(r))
                if r.shift(-2).valid:
                    dv.wait_ge(pKF.sem, pKF.at(r.shift(-2)))
                dv.tensor_tensor(kv[:, r.parity], ps[0:TC, 0, :], bkv[:], ALU.add).then_inc(eKV.sem, 1)
            rounds(dv, bias_kv, B, 0, B - 1, 1, B // 2)

            def quantise(m, v, o):
                nr = v.shape[1]
                dv.wait_ge(ld[f"wnat{m}"], 32 if m < 2 else 16)
                dv.tensor_reduce(wab[:, 0:nr], v, AX_X, ALU.max, apply_absolute_value=True).then_inc(wp, 1)
                dv.wait_ge(wp, 5 * m + 1)
                dv.tensor_scalar(wsc[:, m, 0:nr], wab[:, 0:nr], 1.0 / QMAX, None, ALU.mult).then_inc(wp, 1)
                dv.wait_ge(wp, 5 * m + 2)
                dv.reciprocal(wrec[:, 0:nr], wsc[:, m, 0:nr]).then_inc(wp, 1)
                dv.wait_ge(wp, 5 * m + 3)
                dv.tensor_tensor(v, v, wrec[:, 0:nr][:, :, None].broadcast_to([P, nr, v.shape[2]]), ALU.mult).then_inc(wp, 1)
                dv.wait_ge(wp, 5 * m + 4)
                dv.tensor_scalar(o, v, MAGIC, MAGIC, ALU.add, ALU.subtract).then_inc(wp, 1)

            def quantise_one(m):
                if m < 2:
                    quantise(m, wnat[:], wqs[m])
                else:
                    quantise(m, wnd, wqd)
                    for h in range(2):
                        dv.tensor_scalar(diag[:, h], ident[:], wsc[:, 2, h:h + 1], None, ALU.mult).then_inc(wp, 1)

            def expert(r):
                if r.valid:
                    dv.wait_ge(pD.sem, pD.at(r))
                    if r.shift(-2).valid:
                        dv.wait_ge(pG1.sem, pG1.at(r.shift(-2)))
                    dv.tensor_copy(dspT[:, r.parity].rearrange("p k s -> p (k s)"), ps[:, r.parity, :]).then_inc(eD.sem, 1)
                if r.static and 1 <= r.n <= 3:
                    quantise_one(r.n - 1)
                q = r.shift(-2)
                if q.valid:
                    dv.wait_ge(pG2.sem, pG2.at(q))
                    dv.wait_ge(ldb2[q.parity], 16 * (q.half + 1))
                    if q.shift(-2).valid:
                        dv.wait_ge(stored[q.parity], 16 * q.half)
                    dv.tensor_tensor(yex[:, q.parity], ps[:, 6 + q.parity, :].rearrange("p (t d) -> p t d", t=2),
                                     b2[:, q.parity][:, None, :].broadcast_to([P, 2, D]), ALU.add).then_inc(ye.sem, 1)
            rounds(dv, expert, E, 0, E + 1, 2, 4)

            def residual2(r):
                for t in range(2):
                    dv.scalar_tensor_tensor(tile_of(r, t), yg[:, r.n * 2 + t, :], gk[:, bass.ds(r.n * 2 + t, 1)], tile_of(r, t),
                                            ALU.mult, ALU.add).then_inc(x2s.sem, 1)
                dv.wait_ge(x2s.sem, x2s.at(r))
                statistics(r, ln3, rs3, st, mv)

            def products(r):
                dv.wait_ge(pQF.sem, pQF.at(r))
                if r.shift(-1).valid:
                    dv.wait_ge(pr.sem, pr.at(r.shift(-1)))
                q = ps[:, 6 + r.parity, :].rearrange("p (m d) -> p m d", m=2)
                dv.tensor_tensor(prod[:, 0:2], q, KVF[:, r.n, :, 0:D], ALU.mult).then_inc(pr.sem, 1)
                dv.tensor_tensor(prod[:, 2], q[:, 1], KVF[:, r.n, 0, 0:D], ALU.mult).then_inc(pr.sem, 1)
                dv.tensor_tensor(prod[:, 3], q[:, 0], KVF[:, r.n, 1, 0:D], ALU.mult).then_inc(pr.sem, 1)
                dv.wait_ge(pr.sem, pr.at(r, 3))
                dv.tensor_reduce(pc[:, :, r.n, :], prod[:].rearrange("p j (h d) -> p j h d", h=H), AX_X, ALU.add).then_inc(pr.sem, 1)

            def layer1(r):
                if r.valid:
                    if r.static:
                        dv.wait_ge(gath[2 * r.n], 16)
                        dv.wait_ge(gath[2 * r.n + 1], 16)
                    residual2(r)
                if r.shift(-2).valid:
                    products(r.shift(-2))
            for n in range(4):
                layer1(Round(0, n, B))
            for t in range(8, NT):
                dv.wait_ge(gath[t], 16)
            with dv.Fori(2, B // 2) as i:
                layer1(Round(i, 0, B))
                layer1(Round(i, 1, B))
            for n in range(B, B + 2):
                layer1(Round(0, n, B))

            n = 0

            def step(ins):
                nonlocal n
                n += 1
                ins.then_inc(tk.sem, 1)
                dv.wait_ge(tk.sem, n)
            dv.wait_ge(pCO.sem, 1)
            step(dv.tensor_copy(corr[:], ps[:, 3, 0:TQ]))
            step(dv.max(c8[:], corr[:]))
            step(dv.max_index(ci[:], c8[:], corr[:]))
            step(dv.tensor_scalar(nc0[:], c8[:, 0:1], -1.0, None, ALU.mult))
            step(dv.tensor_copy(cif[:], ci[:]))
            dv.wait_ge(tx.sem, 1)
            step(dv.reciprocal(cr[:], cs[:]))
            step(dv.tensor_scalar(cw[:], cw[:], cr[:], None, ALU.mult))
            for k in range(TOPK):
                ins = dv.tensor_scalar(wts[:, k], iotaT[:], cif[:, k:k + 1], cw[:, k:k + 1], ALU.is_equal, ALU.mult)
                n += 1
                ins.then_inc(tk.sem, 1)
            dv.wait_ge(tk.sem, n)
            for k in range(1, TOPK):
                step(dv.tensor_tensor(wts[:, 0], wts[:, 0], wts[:, k], ALU.add))
            assert n == tk.per

            dv.wait_ge(eWF.sem, 1)

            def parts(r):
                if r.shift(-2).valid:
                    dv.wait_ge(uf.sem, uf.at(r.shift(-2)))
                dv.tensor_tensor(u1[:, r.parity].rearrange("p m (h d) -> p m h d", h=H),
                                 KVF[:, r.n, :, D:2 * D].rearrange("p m (h d) -> p m h d", h=H),
                                 wf[:, 0:2, bass.ds(r.n * H, H)][:, :, :, None].broadcast_to([P, 2, H, DH]), ALU.mult).then_inc(uu.sem, 1)

            def rolled(r):
                dv.wait_ge(uu.sem, uu.at(r))
                dv.wait_ge(uv.sem, uv.at(r))
                if r.shift(-2).valid:
                    dv.wait_ge(pOI.sem, pOI.at(r.shift(-2)))
                dv.tensor_tensor(of[:, r.parity], u1[:, r.parity], u2[:, r.parity], ALU.add).then_inc(uf.sem, 1)

            def residual3(r):
                dv.wait_ge(pY.sem, pY.at(r))
                dv.wait_ge(x2b.sem, x2b.at(r))
                xv = x[:, bass.ds(r.n * 2, 2), :]
                dv.scalar_tensor_tensor(xv, ps[:, 4 + r.parity, :].rearrange("p (t d) -> p t d", t=2), gates4[:, 1:2], xv,
                                        ALU.mult, ALU.add).then_inc(x3s.sem, 1)
                dv.wait_ge(x3s.sem, x3s.at(r))
                statistics(r, ln4, rs4, st2, mv2)

            def largest(r):
                dv.wait_ge(ap4.sem, ap4.at(r))
                dv.tensor_reduce(amax[:, bass.ds(r.n * 2, 2)], yg[:, bass.ds(r.n * 2, 2), :], AX_X, ALU.max,
                                 apply_absolute_value=True).then_inc(mx4.sem, 1)

            def layer1b(r):
                if r.valid:
                    rolled(r)
                if r.shift(1).valid:
                    parts(r.shift(1))
                if r.shift(-2).valid:
                    residual3(r.shift(-2))
                if r.shift(-3).valid:
                    largest(r.shift(-3))
            rounds(dv, layer1b, B, -1, B + 2, 2, 3)

            dv.wait_ge(mx4.sem, mx4.at(Round(0, B - 1, B)))
            dv.tensor_reduce(am1[:], amax[:], AX_X, ALU.max).then_inc(sc, 1)
            dv.wait_ge(arx, 1)
            dv.tensor_scalar(sx[:, 0:1], am2[:], clipr[:, 0:1], None, ALU.mult).then_inc(sc, 1)
            dv.wait_ge(sc, 2)
            dv.reciprocal(sx[:, 1:2], sx[:, 0:1]).then_inc(sc, 1)
            dv.tensor_scalar(sgu[:], wsc[:, 0:2], sx[:, 0:1], None, ALU.mult).then_inc(sc, 1)
            dv.wait_ge(sc, 4)

            def quant_x(r):
                f = yg[:, bass.ds(r.n * 2, 2), :]
                dv.wait_ge(xq1.sem, xq1.at(r))
                dv.tensor_scalar(f, f, MAGIC, QMAX, ALU.subtract, ALU.min).then_inc(xqs.sem, 1)
                dv.wait_ge(xqs.sem, xqs.at(r, 1))
                if r.shift(-2).valid:
                    dv.wait_ge(pXQ.sem, pXQ.at(r.shift(-2)))
                dv.tensor_scalar(xq[:, r.parity], f, -QMAX - 1.0, None, ALU.max).then_inc(xqs.sem, 1)

            dv.memset(hmaxs[:], 0.0).then_inc(hmx, 1)
            for t in range(2):
                quant_x(batch_of(0, t))
            dv.wait_ge(hmx, 1)

            def gated(r):
                for m in range(IK):
                    n = P if m < IK - 1 else TAIL
                    dv.wait_ge(si.sem, si.at(r, m + 1))
                    h = hT[0:n, m, r.n * NB:(r.n + 1) * NB]
                    dv.scalar_tensor_tensor(h, ps[0:n, 3 + 2 * (m % 3), :], sgu[0:n, 1, m:m + 1], sil[0:n, m % 2], ALU.mult, ALU.mult).then_inc(hh.sem, 1)
                    if m:
                        hidden_max(r, m - 1)
                hidden_max(r, IK - 1)

            def hidden_max(r, m):
                n = P if m < IK - 1 else TAIL
                dv.wait_ge(hh.sem, hh.at(r, m + 1))
                at = r.n * IK + m
                dv.tensor_reduce(hmaxs[0:n, at:at + 1], hT[0:n, m, r.n * NB:(r.n + 1) * NB], AX_X, ALU.max,
                                 apply_absolute_value=True).then_inc(hmx, 1)

            for n in range(NQ):
                if n < NQ - 1:
                    for t in range(2):
                        quant_x(batch_of(n + 1, t))
                gated(Round(0, n, NQ))
            dv.memset(hT[TAIL:P, IK - 1, :], 0.0).then_inc(hmx, 1)
            dv.wait_ge(hmx, 2 + IK * NQ)
            dv.tensor_reduce(am1[:], hmaxs[:], AX_X, ALU.max).then_inc(hmx, 1)
            dv.wait_ge(arh, 1)
            dv.tensor_scalar(sx[:, 0:1], am2[:], clipr[:, 1:2], None, ALU.mult).then_inc(sch, 1)
            dv.wait_ge(sch, 3)
            dv.wait_ge(ewp, 8)
            dv.reciprocal(sx[:, 1:2], sx[:, 0:1]).then_inc(sch, 1)
            dv.tensor_scalar(dscale[:], dscale[:], sx[:, 0:1], gates4[:, 3:4], ALU.mult, ALU.mult).then_inc(sch, 1)
            dv.wait_ge(sch, 5)

            def quant_h(r):
                f = hr[:, r.parity]
                dv.wait_ge(hq1.sem, hq1.at(r))
                dv.tensor_scalar(f, f, MAGIC - QMAX - 1.0, MAGIC + QMAX, ALU.max, ALU.min).then_inc(hqc.sem, 1)
                dv.wait_ge(hqc.sem, hqc.at(r))
                if r.shift(-2).valid:
                    dv.wait_ge(pDN.sem, pDN.at(r.shift(-2)))
                dv.tensor_scalar(hq[:, r.parity, HA:], f[:, HA:], MAGIC, None, ALU.subtract).then_inc(hqv.sem, 1)

            def scale_down(r):
                dv.wait_ge(pDN.sem, pDN.at(r))
                if r.shift(-2).valid:
                    dv.wait_ge(fin.sem, fin.at(r.shift(-2)))
                dv.tensor_tensor(xn[:, r.parity], ps[:, r.parity, :].rearrange("p (t d) -> p t d", t=2),
                                 dscale[:, None, :].broadcast_to([P, 2, D]), ALU.mult).then_inc(dns.sem, 1)

            def last(r):
                if r.valid:
                    quant_h(r)
                if r.shift(-1).valid:
                    scale_down(r.shift(-1))
            rounds(dv, last, B, 0, B, 2, B // 2)


CONSTS = 19


def constants():
    n = np.arange(TQ)
    cos = lambda f: np.cos(2 * np.pi * ((np.outer(n, f)) % TQ) / TQ)
    sin = lambda f: np.sin(2 * np.pi * ((np.outer(n, f)) % TQ) / TQ)
    f = np.arange(P)
    c, s, nyq = cos(f), sin(f), cos([P])
    s0 = s.copy()
    s0[:, 0:1] = nyq
    dft = np.concatenate([c, s0], 1)
    weight = np.where(f == 0, 1.0, 2.0) / TQ
    ic, is_ = (c * weight).T, (s * weight).T
    isn = is_.copy()
    isn[0] = nyq[:, 0] / TQ
    idft = np.concatenate([ic, isn], 0)
    m1 = ic.copy()
    m2 = ic.copy()
    m2[0] = nyq[:, 0] / TQ
    corrm = np.stack([m1, m2, is_, -is_]) / DH
    cn = c.copy()
    cn[:, 0:1] = nyq
    wd = np.stack([c, cn, s, -s])
    g = lambda m: np.ascontiguousarray(m, dtype=np.float32)
    dc = np.zeros((1, P))
    dc[0, 0] = TQ
    return {
        "dft": g(dft.reshape(DK, P, TQ).transpose(1, 0, 2)),
        "idft": g(idft.reshape(DK, P, TQ).transpose(1, 0, 2)),
        "corrm": g(corrm.transpose(1, 0, 2)),
        "wdft": g(wd.reshape(4, DK, P, P).transpose(2, 0, 1, 3)),
        "dcrow": g(dc),
    }


def kernel(**inputs):
    import concourse.bacc as bacc
    from concourse.bass_utils import run_bass_kernel_spmd

    v = {n: np.asarray(t) for n, t in inputs.items()}

    def rows(m):
        return m.reshape(DK, P, -1).transpose(1, 0, 2)

    arrays = {
        "x": v["x"].reshape(B * TQ, D),
        "ctxT": rows(v["ctx_1024"].reshape(B * TC, D).T),
        "w0": np.stack([rows(v["L0_xattn_" + n].T) for n in ("Wq", "Wk", "Wv", "Wo")], 1),
        "w1a": np.stack([rows(v["L1_xattn_" + n]) for n in ("Wq", "Wk", "Wv", "Wo")], 1),
        "wg": rows(v["L0_ffn_wg"]),
        "gates": np.concatenate([v["g_xattn"], v["g_ffn"]]),
        "clips": np.concatenate([v["L1_ffn_clip_x"], v["L1_ffn_clip_down"]]),
        "b1": v["L0_ffn_b1"].reshape(E, FK, P).transpose(2, 0, 1).reshape(P, E * FK),
        "w1": v["L0_ffn_w1"].reshape(E, DK, P, F).transpose(0, 2, 1, 3),
        "w2": v["L0_ffn_w2"].reshape(E, FK, P, D).transpose(0, 2, 1, 3),
        "b2": v["L0_ffn_b2"],
        "bkv": np.concatenate([v["L1_xattn_bk"], v["L1_xattn_bv"]]),
        "bq": v["L1_xattn_bq"][None],
        "bo": v["L1_xattn_bo"],
        "wgu": np.stack([v["L1_ffn_w_gate"], v["L1_ffn_w_up"]]),
        "wd": v["L1_ffn_w_down"],
        **constants(),
    }
    arrays = {"in_" + n: np.ascontiguousarray(m) for n, m in arrays.items()}
    nc = bacc.Bacc("TRN2", target_bir_lowering=False, num_devices=1)
    args = {n[3:]: nc.dram_tensor(n, list(m.shape), F32, kind="ExternalInput").ap() for n, m in arrays.items()}
    out = nc.dram_tensor("out", [B * TQ, D], F32, kind="ExternalOutput").ap()
    build(nc, args, out)
    r = run_bass_kernel_spmd(nc, [arrays], core_ids=[0])
    return r.results[0]["out"].reshape(B, TQ, D)
```

```python
from contextlib import ExitStack

import numpy as np

import concourse.bass as bass
from concourse import mybir

F32 = mybir.dt.float32
BF16 = mybir.dt.bfloat16
U32 = mybir.dt.uint32
ALU = mybir.AluOpType
ACT = mybir.ActivationFunctionType
AX_X = mybir.AxisListType.X
ABSMAX = bass.bass_isa.ReduceOp.absmax

P = 128
B, TQ, D = 8, 256, 256
TC = 77
H, DH = 16, 16
DK = D // P
NT = B * TQ // P
E, F = 8, 1024
FK = F // P
CAP = B * TQ // E
SLOTS = E * CAP
I = 704
IK = (I + P - 1) // P
TAIL = I - (IK - 1) * P
NB = 512
TOPK = 5
EPS = 1e-5
QMAX = 127.0
MAGIC = 1.5 * 2.0 ** 23
GC = (1, 4)
VC = tuple(m for m in range(IK) if m not in GC)
HR = 3
HA = 4
SH = 6
TCP = 80
HB, KB = 8, 16
KC = TCP // KB
NC = (H // HB) * KC
GROUPS = ((0, 4), (4, 8), (8, NC))
NG = len(GROUPS)


class Round:

    def __init__(self, i, off, count):
        self.i, self.off, self.count = i, off, count
        self.parity = off % 2
        self.static = isinstance(i, int)
        self.n = 2 * i + off if self.static else i * 2 + off

    def shift(self, k):
        return Round(self.i, self.off + k, self.count)

    @property
    def valid(self):
        return not self.static or 0 <= self.n < self.count

    @property
    def half(self):
        return self.i + self.off // 2


class Stage:

    def __init__(self, sem, per):
        self.sem, self.per = sem, per

    def at(self, r, step=None):
        return r.n * self.per + (self.per if step is None else step)


def rounds(eng, body, count, first, last, lo, hi):
    for n in range(first, 2 * lo):
        body(Round(0, n, count))
    with eng.Fori(lo, hi) as i:
        body(Round(i, 0, count))
        body(Round(i, 1, count))
    for n in range(2 * hi, last + 1):
        body(Round(0, n, count))


def build(nc, a, out):
    with ExitStack() as ctx:
        def sb(name, shape, dt=F32):
            return ctx.enter_context(nc.sbuf_tensor(name, shape, dt))

        def sem(name):
            return ctx.enter_context(nc.semaphore(name))

        def stage(name, per):
            return Stage(sem(name), per)

        def carve(base, shapes):
            at, out = 0, []
            for shape in shapes:
                size = int(np.prod(shape))
                axes = "abcde"[:len(shape)]
                v = base[:, at:at + size]
                if len(shape) > 1:
                    v = v.rearrange(f"p ({' '.join(axes)}) -> p {' '.join(axes)}", **dict(zip(axes, shape)))
                out.append(v)
                at += size
            assert at <= base.shape[1], (at, base.shape)
            return out

        pool = sb("pool", [P, 9 * 2048])
        (kbd, prob, probT, k0T, xnT, qT, ao, aoT, x2T, zeros, vblk, vpk) = carve(pool, [
            (2, DK, P // DH, TC),
            (2, H, TCP), (2, NC, P), (DK, B * TC), (DK, TQ), (2, DK, TQ), (2, D), (2, DK, P), (2, DK, P), (1024,),
            (2, NC, HB, DH + 1),
            (KC, B, 2, DH)])
        v0s, = carve(vblk[0:TC].rearrange("p u c h d -> p (u c h d)"), [(HB, B, 2, DH)])
        (hid, yex, kvf, yg, wdTw) = carve(pool, [
            (2, FK, CAP), (2, CAP // P, D),
            (2, B // 2, 2, 2, D),
            (NT, D),
            (IK * D // 2,)])
        wdT = wdTw.bitcast(BF16).rearrange("p (m d) -> p m d", m=IK)
        hT = pool[:, 0:IK * B * TQ].rearrange("p (m s) -> p m s", m=IK)
        wbuf = sb("wbuf", [P, 4 * DK * F])
        w1, w2 = carve(wbuf, [(2, DK, F), (2, FK, D)])
        (_, wtT, wf, of, oT) = carve(wbuf, [(4096,), (DK, P), (4, P), (2, DK, D), (2, DK, TQ)])
        (xh, prod, qs) = carve(wbuf, [(2, DK, TQ), (2, 4, D), (2, 2, D)])
        (corr, wts) = carve(wbuf, [(TQ,), (TOPK, TQ)])
        (u1, u2) = carve(wbuf, [(2, 2, D), (2, 2, D)])
        hqw, silp, upp = carve(wbuf, [(2 * IK * TQ // 2,), (2, NB), (2, NB)])
        hq = hqw.bitcast(BF16).rearrange("p (u m s) -> p u m s", u=2, m=IK)
        w0b = sb("w0b", [P, 4 * DK * D])
        w0, = carve(w0b, [(4, DK, D)])
        wgT = w0b[:, 0:DK * I].bitcast(BF16).rearrange("p (g k i) -> p g k i", g=2, k=DK)
        w1b = sb("w1b", [P, 4 * DK * D])
        w1a, = carve(w1b, [(4, DK, D)])
        xqT = w1b[:].bitcast(BF16).rearrange("p (k s) -> p k s", k=DK)

        x = sb("x", [P, NT, D])
        ctxT = sb("ctxT", [P, DK, B * TC])
        wg = sb("wg", [P, DK, E])
        ident = sb("ident", [P, P])
        identb = sb("identb", [P, P], BF16)
        onesf = sb("onesf", [P, P])
        onesb = sb("onesb", [P, P], BF16)
        trib = sb("trib", [P, P], BF16)
        headmask = sb("headmask", [P, P // DH])
        iota8 = sb("iota8", [P, E])
        iotaT = sb("iotaT", [P, TQ])
        mhalf = sb("mhalf", [P, 2])
        epsc = sb("epsc", [P, 2])
        zeroc = sb("zeroc", [P, 2])
        magicc = sb("magicc", [P, 1])
        nmagic = sb("nmagic", [P, 1])
        gates4 = sb("gates4", [P, 4])
        clips = sb("clips", [P, 2])
        clipr = sb("clipr", [P, 2])
        bkv = sb("bkv", [TC, 2 * D])
        bq = sb("bq", [1, D])
        bo = sb("bo", [P, D])
        b1 = sb("b1", [P, E * FK])
        dft = sb("dft", [P, DK, TQ])
        idft = sb("idft", [P, DK, TQ])
        corrm = sb("corrm", [P, 4, TQ])
        wdft = sb("wdft", [P, 4, DK, P])
        dcrow = sb("dcrow", [1, P])

        st = sb("st", [P, 2, 6])
        mv = sb("mv", [P, 2, 2])
        vare = sb("vare", [P, 2])
        nmean = sb("nmean", [P, 2])
        nmr = sb("nmr", [P, 2])
        rstd = sb("rstd", [P, 2])
        st2 = sb("st2", [P, 2, 6])
        mv2 = sb("mv2", [P, 2, 2])
        vare2 = sb("vare2", [P, 2])
        nmean2 = sb("nmean2", [P, 2])
        nmr2 = sb("nmr2", [P, 2])
        rstd2 = sb("rstd2", [P, 2])
        xn = sb("xn", [P, 2, 2, D])
        xn2 = sb("xn2", [P, 2, 2, D])
        mx = sb("mx", [P, 2, H])
        rden = sb("rden", [P, 2, H])
        top = sb("top", [P, 2, 8])
        topi = sb("topi", [P, 2, 8], U32)
        eidx = sb("eidx", [P, 2, 2])
        ntop = sb("ntop", [P, 2])
        mask = sb("mask", [P, 2, 2, E], BF16)
        seen = sb("seen", [P, 2, E], BF16)
        seen1 = sb("seen1", [P, E])
        gexp = sb("gexp", [P, 2, E])
        gsum = sb("gsum", [P, NT])
        lm = sb("lm", [P, 2, E])
        pos = sb("pos", [P, 2])
        slot = sb("slot", [P, NT])
        keep = sb("keep", [P, NT])
        skip = sb("skip", [P, 2])
        grec = sb("grec", [P, NT])
        slots = sb("slots", [P, 2, 2], U32)
        slotg = sb("slotg", [P, NT], U32)
        gk = sb("gk", [P, NT])
        b2 = sb("b2", [P, 2, D])
        dsp = sb("dsp", [P, 2, CAP // P, D])
        dspT = sb("dspT", [P, 2, DK, CAP])
        kv = sb("kv", [TC, 2, 2 * D])
        pc = sb("pc", [P, 4, B, H])
        c8 = sb("c8", [P, 8])
        ci = sb("ci", [P, 8], U32)
        cif = sb("cif", [P, 8])
        nc0 = sb("nc0", [P, 1])
        cw = sb("cw", [P, TOPK])
        cs = sb("cs", [P, 1])
        cr = sb("cr", [P, 1])
        amax = sb("amax", [P, NT])
        am1 = sb("am1", [P, 1])
        am2 = sb("am2", [P, 1])
        sx = sb("sx", [P, 2])
        wnat = sb("wnat", [P, IK, D])
        wab = sb("wab", [P, IK])
        wrec = sb("wrec", [P, IK])
        wsc = sb("wsc", [P, 3, IK])
        wq0 = sb("wq0", [P, IK, D], BF16)
        hmaxs = sb("hmaxs", [P, IK * B * TQ // NB])
        sgu = sb("sgu", [P, 2, IK])
        diag = sb("diag", [P, DK, P])
        dscale = sb("dscale", [P, D])
        warm = sb("warm", [P, 1])

        def as_wq(m):
            return m[:, 0:IK * D // 2].bitcast(BF16).rearrange("p (m d) -> p m d", m=IK)
        wqs = (wq0[:], as_wq(xn[:].rearrange("p u t d -> p (u t d)")), as_wq(xn2[:].rearrange("p u t d -> p (u t d)")))
        wqd = wqs[2].rearrange("p m d -> p (m d)")[:, 0:2 * I].rearrange("p (h i) -> p h i", h=2)
        wnd = wnat[:].rearrange("p m d -> p (m d)")[:, 0:2 * I].rearrange("p (h i) -> p h i", h=2)

        ps = ctx.enter_context(nc.psum_tensor("ps", [P, 8, 512], F32))

        vdram = nc.dram_tensor("values_by_head", [HB, TCP, B * 2 * DH], F32, kind="Internal").ap()
        disp = nc.dram_tensor("dispatched", [SLOTS, D], F32, kind="Internal").ap()
        yexp = nc.dram_tensor("expert_rows", [SLOTS, D], F32, kind="Internal").ap()

        ld = {n: sem("loaded_" + n) for n in (
            "x0", "x1", "w0k", "w0v", "w0qo", "w1a", "ctxT", "small", "b1", "bias", "dft", "idft", "corrm", "wdft", "wnat0", "wnat1", "wnat2")}
        ldw1 = [sem(f"loaded_w1_{u}") for u in range(2)]
        ldw2 = [sem(f"loaded_w2_{u}") for u in range(2)]
        ldb2 = [sem(f"loaded_b2_{u}") for u in range(2)]
        lddsp = [sem(f"loaded_dispatched_{u}") for u in range(2)]
        zeroed = sem("dispatched_zeroed")
        scat = [[sem(f"scattered_{u}{t}") for t in range(2)] for u in range(2)]
        stored = [sem(f"expert_rows_stored_{u}") for u in range(2)]
        gath = [sem(f"gathered_{b}") for b in range(B)]
        outs = sem("out_stored")
        passed = sem("waits_passed")
        wtail = sem("weights_tail_set")

        consts = stage("consts_ready", 1)
        tan = stage("gates_tanh", 1)
        ln1, rs1, ap1 = stage("ln1_statistics", 4), stage("ln1_rstd", 4), stage("ln1", 2)
        kb, vb = stage("keys_block_diagonal", 1), stage("values_block_diagonal", 1)
        pV, eV = sem("values_product"), sem("values_copied")
        vpad, vst, vld, vones = sem("values_padded"), sem("values_stored"), sem("values_loaded"), sem("value_ones")
        pk0, ek0 = stage("k0T_product", 1), stage("k0T_copied", 1)
        pA, eA = stage("xT_q_product", 2), stage("xT_q_copied", 2)
        pS, ms, ex = stage("scores", 2), stage("scores_less_max", 4), stage("probabilities", 2)
        pPT, ePT, pAV = stage("prob_transposed", 2 * NG), stage("probT_copied", 2 * NG), stage("attended", 2)
        nv = stage("attended_normalised", 4)
        pOT, eOT, pWO, x1s = stage("ao_transposed", 2), stage("aoT_copied", 2), stage("ao_projected", 2), stage("x1", 2)
        ln2, rs2, ap2 = stage("ln2_statistics", 4), stage("ln2_rstd", 4), stage("ln2", 2)
        pX2, eX2, pLG = stage("x2_transposed", 1), stage("x2T_copied", 1), stage("router_logits", 1)
        ga, gx, pLOC, sl = stage("chosen", 9), stage("gate_exp", 2), stage("positions", 1), stage("slots_known", 6)
        bulk = sem("gates_and_slots")
        pD, eD = stage("dsp_transposed", 1), stage("dspT_copied", 1)
        pG1, gl, pG2, ye = stage("hidden_product", 4), stage("hidden_gelu", 8), stage("expert_product", 1), stage("expert_rows", 1)
        pKV, eKV = sem("kv_product"), [sem("keys_biased"), sem("values_biased")]
        pKF, eKF = sem("kv_spectrum"), sem("kv_spectrum_copied")
        x2s, ln3, rs3, ap3, x2b = stage("x2", 2), stage("ln3_statistics", 4), stage("ln3_rstd", 4), stage("ln3", 2), stage("x2_bias", 1)
        pXH, eXH, pQF, pr = stage("xn_spectrum", 1), stage("xn_spectrum_copied", 1), stage("q_spectrum", 1), stage("spectra_products", 1)
        eQF, pr2, sp = stage("q_spectrum_copied", 1), stage("crossed_products", 1), stage("products_summed", 1)
        pCO, tk, tx, pWT, eWT, pWF, eWF = (stage("correlation", 1), stage("delays", 16), stage("delays_exp", 1), stage("delays_transposed", 1),
                                          stage("delaysT_copied", 1), stage("delay_spectra", 1), stage("delay_spectra_copied", 1))
        uv = stage("rolled_parts_crossed", 1)
        uu, uf, pOI, eOI, pY, x3s = stage("rolled_parts", 1), stage("rolled_spectrum", 1), stage("rolled_time", 1), stage("rolled_copied", 1), stage("rolled_projected", 1), stage("x3", 1)
        ln4, rs4, ap4, mx4 = stage("ln4_statistics", 4), stage("ln4_rstd", 4), stage("ln4", 2), stage("ln4_max", 1)
        bosc = sem("bias_scaled")
        wp, pwp, ewp = sem("weights_quantised"), sem("weights_transposed"), sem("weightsT_copied")
        sc, arx = sem("activation_scale"), sem("max_of_all_partitions")
        xq1, xg1 = stage("x_rounded", 1), sem("x_rounded_gpsimd")
        xqs, pXQ, eXQ = stage("x_clipped", 1), stage("xq_transposed", 1), stage("xqT_copied", 1)
        pGU, si, hh = stage("gate_up_product", IK), stage("gate_silu", IK), stage("hidden_gated", len(VC))
        ue, hp = stage("up_scaled", len(GC)), stage("hidden_gated_gpsimd", len(GC))
        hmx, hqg = sem("hidden_max"), stage("hidden_rounded_gpsimd", 1)
        hq1, hqc, hqa, hqv = stage("hidden_rounded", 1), stage("hidden_clipped", 1), stage("hidden_quantised_act", 1), stage("hidden_quantised_vector", 1)
        sch = sem("hidden_scale")
        pDN, dns, fin = stage("down_product", 1), stage("down_scaled", 1), stage("final", 1)


        UNITS = [(j, u) for j in range(2) for u in range(B // 2)]

        def kv_unit(n):
            j, u = UNITS[n]
            freq = ((2, 3), (4, 5)) if j == 0 else ((4, 5), (2, 6))
            return j, u, n % 2, freq[n % 2]

        def bias_kv(eng, n):
            j, u, bank, _ = kv_unit(n)
            eng.wait_ge(pKV, n + 1)
            if n >= 2:
                eng.wait_ge(pKF, n - 1)
            eng.tensor_tensor(kv[:, n % 2].rearrange("p (b d) -> p b d", b=2), ps[0:TC, bank, :].rearrange("p (b d) -> p b d", b=2),
                              bkv[:, None, j * D:(j + 1) * D].broadcast_to([TC, 2, D]), ALU.add).then_inc(eKV[j], 1)

        def spectrum(r, j, m=slice(0, 2)):
            return kvf[:, j, r.half, m, r.parity, :]

        NQ = B * TQ // NB

        def batch_of(n, t):
            return Round(0, 2 * n + t, B)

        sil = xn2[:].rearrange("p u t d -> p u (t d)")

        block = ctx.enter_context(nc.Block())

        def alone(eng):
            eng.sem_inc(passed, 1)

        def load_gu(eng, m):
            eng.dma_start(wnat[:, 0:IK - 1, :], a["wgu"][m, 0:P * (IK - 1), :].rearrange("(m p) d -> p m d", p=P)).then_inc(ld[f"wnat{m}"], 16)
            eng.dma_start(wnat[0:TAIL, IK - 1, :], a["wgu"][m, P * (IK - 1):I, :]).then_inc(ld[f"wnat{m}"], 16)

        @block.sync
        def _(sp):
            xv = a["x"].rearrange("(t p) d -> p t d", p=P)
            sp.dma_start(w0[:, 1], a["w0"][:, 1]).then_inc(ld["w0k"], 16)
            sp.dma_start(ctxT[:], a["ctxT"]).then_inc(ld["ctxT"], 16)
            sp.dma_start(w0[:, 2], a["w0"][:, 2]).then_inc(ld["w0v"], 16)
            sp.dma_start(x[:, 0:4, :], xv[:, 0:4, :]).then_inc(ld["x0"], 16)
            sp.dma_start(w0[:, 0], a["w0"][:, 0]).then_inc(ld["w0qo"], 16)
            sp.dma_start(w0[:, 3], a["w0"][:, 3]).then_inc(ld["w0qo"], 16)
            for dst, src in ((wg[:], a["wg"]), (gates4[:], a["gates"].partition_broadcast(P)), (clips[:], a["clips"].partition_broadcast(P))):
                sp.dma_start(dst, src).then_inc(ld["small"], 16)
            sp.dma_start(x[:, 4:NT, :], xv[:, 4:NT, :]).then_inc(ld["x1"], 16)
            sp.dma_start(b1[:], a["b1"]).then_inc(ld["b1"], 16)
            sp.wait_ge(consts.sem, ZEROS)
            sp.dma_start(vdram[:, TC:TCP, :], zeros[0:HB, 0:(TCP - TC) * B * 2 * DH].rearrange("h (k n) -> h k n", k=TCP - TC)).then_inc(vpad, 16)
            sp.wait_ge(eV, B)
            sp.dma_start(vdram[:, 0:TC, :].rearrange("h k n -> k h n"), v0s.rearrange("k h b g d -> k h (b g d)")).then_inc(vst, 16)
            sp.wait_ge(vpad, 16)
            sp.wait_ge(vst, 16)
            sp.dma_start(vpk.rearrange("p c b g d -> p c (b g d)"), vdram.rearrange("h (k c) n -> (h k) c n", c=KC)).then_inc(vld, 16)
            for e in range(SLOTS * D // (P * 1024)):
                sp.dma_start(disp.rearrange("(e p t) d -> e p (t d)", p=P, t=4)[e], zeros[:]).then_inc(zeroed, 16)
            for e in range(2):
                sp.dma_start(w1[:, e], a["w1"][e]).then_inc(ldw1[e], 16)
                sp.dma_start(w2[:, e], a["w2"][e]).then_inc(ldw2[e], 16)
                sp.dma_start(b2[:, e], a["b2"][e].partition_broadcast(P)).then_inc(ldb2[e], 16)
            sp.wait_ge(wtail, 1)
            load_gu(sp, 0)
            sp.dma_start(w1a[:], a["w1a"]).then_inc(ld["w1a"], 16)
            sp.dma_start(dft[:], a["dft"]).then_inc(ld["dft"], 16)
            sp.dma_start(idft[:], a["idft"]).then_inc(ld["idft"], 16)
            sp.dma_start(corrm[:], a["corrm"]).then_inc(ld["corrm"], 16)
            sp.dma_start(wdft[:], a["wdft"]).then_inc(ld["wdft"], 16)
            for dst, src in ((bkv[:], a["bkv"].partition_broadcast(TC)), (bq[:], a["bq"]), (bo[:], a["bo"].partition_broadcast(P)), (dcrow[:], a["dcrow"])):
                sp.dma_start(dst, src).then_inc(ld["bias"], 16)
            for u in range(2):
                for t in range(2):
                    sp.wait_ge(scat[u][t], 16 * (B // 2))
            dv = disp.rearrange("(e t p) d -> e p t d", e=E, p=P)

            def load_dsp(r):
                sp.dma_start(dsp[:, r.parity], dv[r.n]).then_inc(lddsp[r.parity], 16)

            def body(r):
                nx = r.shift(2)
                if nx.valid:
                    sp.wait_ge(pD.sem, pD.at(r))
                    load_dsp(nx)
                    sp.wait_ge(pG1.sem, pG1.at(r))
                    sp.dma_start(w1[:, r.parity], a["w1"][nx.n]).then_inc(ldw1[r.parity], 16)
                q = r.shift(-1)
                if q.valid and q.shift(2).valid:
                    sp.wait_ge(ye.sem, ye.at(q))
                    sp.dma_start(w2[:, q.parity], a["w2"][q.shift(2).n]).then_inc(ldw2[q.parity], 16)
                    sp.dma_start(b2[:, q.parity], a["b2"][q.shift(2).n].partition_broadcast(P)).then_inc(ldb2[q.parity], 16)

            load_dsp(Round(0, 0, E))
            load_dsp(Round(0, 1, E))
            rounds(sp, body, E, 0, E - 2, 1, (E - 2) // 2)
            ov = out.rearrange("(b t p) d -> b p t d", t=2, p=P)

            def store(r):
                sp.wait_ge(fin.sem, fin.at(r))
                sp.dma_start(ov[r.n], x[:, bass.ds(r.n * 2, 2), :]).then_inc(outs, 16)
            rounds(sp, store, B, 0, B - 1, 0, B // 2)
            sp.wait_ge(outs, 16 * B)

        @block.gpsimd
        def _(gp):
            c = 0

            def const(ins):
                nonlocal c
                c += 1
                ins.then_inc(consts.sem, 1)

            const(gp.memset(ident[:], 0.0))
            const(gp.memset(headmask[:], 1.0))
            const(gp.memset(mhalf[:], -0.5))
            const(gp.memset(epsc[:], EPS))
            const(gp.memset(zeroc[:], 0.0))
            const(gp.memset(magicc[:], MAGIC))
            const(gp.memset(nmagic[:], -MAGIC))
            const(gp.memset(onesf[:], 1.0))
            const(gp.memset(onesb[:], 1.0))
            const(gp.memset(prob[:, :, :, TC:], 0.0))
            const(gp.memset(seen[:], 0.0))
            const(gp.iota(iota8[:], [[1, E]], base=0, channel_multiplier=0, allow_small_or_imprecise_dtypes=True))
            const(gp.iota(iotaT[:], [[1, TQ]], base=0, channel_multiplier=0, allow_small_or_imprecise_dtypes=True))
            const(gp.memset(zeros[:], 0.0))
            assert c == ZEROS
            gp.wait_ge(consts.sem, c)
            const(gp.affine_select(out=ident[:], in_=ident[:], compare_op=ALU.not_equal, fill=1.0, base=0, pattern=[[-1, P]], channel_multiplier=1))
            const(gp.affine_select(out=trib[:], in_=onesb[:], compare_op=ALU.is_ge, fill=0.0, base=0, pattern=[[1, P]], channel_multiplier=-1))
            const(gp.affine_select(out=headmask[:], in_=headmask[:], compare_op=ALU.is_ge, fill=0.0, base=0, pattern=[[-DH, P // DH]], channel_multiplier=1))
            gp.wait_ge(consts.sem, c)
            const(gp.affine_select(out=headmask[:], in_=headmask[:], compare_op=ALU.is_ge, fill=0.0, base=DH - 1, pattern=[[DH, P // DH]], channel_multiplier=-1))
            const(gp.tensor_copy(identb[:], ident[:]))
            assert c == CONSTS
            gp.wait_ge(consts.sem, c)

            def scales_of(r, ln, rs, ap, m, v, o, nm, nr):
                gp.wait_ge(ln.sem, ln.at(r, 4))
                gp.tensor_tensor(nm[:], zeroc[:], m[:, :, 0], ALU.subtract).then_inc(rs.sem, 1)
                gp.tensor_tensor(v[:], m[:, :, 1], epsc[:], ALU.add).then_inc(rs.sem, 1)
                gp.wait_ge(rs.sem, rs.at(r, 2))
                if r.shift(-1).valid:
                    gp.wait_ge(ap.sem, ap.at(r.shift(-1)))
                gp.tensor_tensor(o[:], v[:], mhalf[:], ALU.pow).then_inc(rs.sem, 1)
                gp.wait_ge(rs.sem, rs.at(r, 3))
                gp.tensor_tensor(nr[:], nm[:], o[:], ALU.mult).then_inc(rs.sem, 1)

            def keys(r):
                if r.shift(-2).valid:
                    gp.wait_ge(pS.sem, pS.at(r.shift(-2)))
                for k in range(DK):
                    ins = gp.tensor_tensor(kbd[:, r.parity, k], k0T[:, k, None, bass.ds(r.n * TC, TC)].broadcast_to([P, P // DH, TC]),
                                           headmask[:, :, None].broadcast_to([P, P // DH, TC]), ALU.mult)
                ins.then_inc(kb.sem, 1)

            def values(r):
                if r.shift(-2).valid:
                    gp.wait_ge(pAV.sem, pAV.at(r.shift(-2)))
                for g in range(2):
                    ins = gp.tensor_tensor(vblk[:, r.parity, g * KC:(g + 1) * KC, :, 0:DH],
                                           vpk[:, :, r.n, g, None, :].broadcast_to([P, KC, HB, DH]),
                                           headmask[:, None, :, None].broadcast_to([P, KC, HB, DH]), ALU.mult)
                ins.then_inc(vb.sem, 1)

            def scatter(r):
                gp.wait_ge(sl.sem, sl.at(r))
                alone(gp)
                for t in range(2):
                    gp.indirect_dma_start(out=disp, out_offset=bass.IndirectOffsetOnAxis(ap=slots[:, r.parity, t:t + 1], axis=0),
                                          in_=xn2[:, r.parity, t, :], in_offset=None, bounds_check=SLOTS - 1,
                                          oob_is_err=False).then_inc(scat[r.parity][t], 16)

            scales_of(Round(0, 0, B), ln1, rs1, ap1, mv, vare, rstd, nmean, nmr)
            gp.wait_ge(ek0.sem, 4)
            keys(Round(0, 0, B))
            scales_of(Round(0, 1, B), ln1, rs1, ap1, mv, vare, rstd, nmean, nmr)
            gp.wait_ge(vld, 16)
            for u in range(2):
                ins = gp.tensor_copy(vblk[:, u, :, :, DH], headmask[:, None, :].broadcast_to([P, NC, HB]))
            ins.then_inc(vones, 1)
            gp.wait_ge(vones, 1)
            values(Round(0, 0, B))

            gp.wait_ge(zeroed, 16 * (SLOTS * D // (P * 1024)))

            def body(r):
                if r.shift(1).valid:
                    keys(r.shift(1))
                    values(r.shift(1))
                if r.shift(-1).valid:
                    scales_of(r.shift(-1), ln2, rs2, ap2, mv2, vare2, rstd2, nmean2, nmr2)
                if r.shift(-2).valid:
                    scatter(r.shift(-2))
                if r.shift(2).valid:
                    scales_of(r.shift(2), ln1, rs1, ap1, mv, vare, rstd, nmean, nmr)
                if r.static and r.n == B:
                    scatter(r.shift(-1))
            rounds(gp, body, B, 0, B, 1, 3)
            gp.wait_ge(tan.sem, 2)
            gp.wait_ge(ld["bias"], 64)
            gp.tensor_scalar(bo[:], bo[:], gates4[:, 1:2], None, ALU.mult).then_inc(bosc, 1)
            gp.wait_ge(wp, 5)
            load_gu(gp, 1)
            gp.wait_ge(wp, 10)
            gp.dma_start(wnd, a["wd"].rearrange("(h p) i -> p h i", p=P)).then_inc(ld["wnat2"], 16)
            gp.wait_ge(bulk, 5)
            for u in range(2):
                gp.wait_ge(stored[u], 16 * (E // 2))

            def gather(lo, hi):
                for t in range(lo, hi):
                    gp.indirect_dma_start(out=yg[:, t, :], out_offset=None, in_=yexp,
                                          in_offset=bass.IndirectOffsetOnAxis(ap=slotg[:, t:t + 1], axis=0)).then_inc(gath[t // 2], 16)

            def body3(r, tiles=None):
                if r.valid:
                    scales_of(r, ln3, rs3, ap3, mv, vare, rstd, nmean, nmr)
                c = r.shift(-3)
                if c.valid:
                    if c.n == 0:
                        gp.wait_ge(eKF, B)
                    gp.wait_ge(eQF.sem, eQF.at(c))
                    if c.shift(-2).valid:
                        gp.wait_ge(sp.sem, sp.at(c.shift(-2)))
                    for m in range(2):
                        ins = gp.tensor_tensor(prod[:, c.parity, 2 + m], qs[:, c.parity, 1 - m], spectrum(c, 0, m), ALU.mult)
                    ins.then_inc(pr2.sem, 1)
                if tiles:
                    gather(*tiles)

            gp.wait_ge(bosc, 1)
            gather(0, 5)
            gathers = (5, 7, 9, 11, 13, 15, NT)
            for n in range(len(gathers) - 1):
                body3(Round(0, n, B), gathers[n:n + 2])
            for n in range(len(gathers) - 1, B + 3):
                body3(Round(0, n, B))

            def add_bias(r):
                gp.wait_ge(ap3.sem, ap3.at(r))
                gp.tensor_tensor(x[:, bass.ds(r.n * 2, 2), :], x[:, bass.ds(r.n * 2, 2), :],
                                 bo[:, None, :].broadcast_to([P, 2, D]), ALU.add).then_inc(x2b.sem, 1)
            rounds(gp, add_bias, B, 0, B - 1, 0, B // 2)

            def crossed(r):
                if r.shift(-2).valid:
                    gp.wait_ge(uf.sem, uf.at(r.shift(-2)))
                for m in range(2):
                    ins = gp.tensor_tensor(u2[:, r.parity, m].rearrange("p (h d) -> p h d", h=H),
                                           spectrum(r, 1, 1 - m).rearrange("p (h d) -> p h d", h=H),
                                           wf[:, 2 + m, bass.ds(r.n * H, H)][:, :, None].broadcast_to([P, H, DH]), ALU.mult)
                ins.then_inc(uv.sem, 1)

            def body4(r):
                if r.static and r.n in (-1, 3):
                    gp.wait_ge(eKF, 3 * B // 2 if r.n < 0 else 2 * B)
                if r.shift(1).valid:
                    crossed(r.shift(1))
                if r.shift(-2).valid:
                    scales_of(r.shift(-2), ln4, rs4, ap4, mv2, vare2, rstd2, nmean2, nmr2)
            gp.wait_ge(eWF.sem, 1)
            rounds(gp, body4, B, -1, B + 1, 2, 3)
            gp.wait_ge(sc, 1)
            gp.partition_all_reduce(am2[:], am1[:], P, ABSMAX).then_inc(arx, 1)
            gp.wait_ge(sc, 4)

            for n in range(2, B):
                f = yg[:, 2 * n:2 * n + 2, :]
                gp.tensor_scalar(f, f, sx[:, 1:2], MAGIC, ALU.mult, ALU.add).then_inc(xg1, 1)
            gp.wait_ge(xg1, B - 2)
            gp.memset(hT[TAIL:P, IK - 1, :], 0.0).then_inc(xg1, 1)
            gp.wait_ge(xg1, B - 1)

            for b in range(NQ):
                r = Round(0, b, NQ)
                for j, m in enumerate(GC):
                    gp.wait_ge(ue.sem, ue.at(r, j + 1))
                    gp.wait_ge(si.sem, si.at(r, m + 1))
                    n = P if m < IK - 1 else TAIL
                    u = (b * len(GC) + j) % 2
                    gp.tensor_tensor(hT[0:n, m, b * NB:(b + 1) * NB], silp[0:n, u], upp[0:n, u], ALU.mult).then_inc(hp.sem, 1)
            gp.wait_ge(hmx, IK * NQ + 2)
            gp.partition_all_reduce(am2[:], am1[:], P, ABSMAX).then_inc(arx, 1)

            def round_h(r):
                f = hT[:, HR:, bass.ds(r.n * TQ, TQ)]
                gp.tensor_scalar(f, f, sx[:, 1:2], MAGIC, ALU.mult, ALU.add).then_inc(hqg.sem, 1)

            def last(r):
                gp.wait_ge(dns.sem, dns.at(r))
                gp.tensor_tensor(x[:, bass.ds(r.n * 2, 2), :], x[:, bass.ds(r.n * 2, 2), :], xn[:, r.parity], ALU.add).then_inc(fin.sem, 1)
            gp.wait_ge(sch, 5)
            for n in range(B):
                round_h(Round(0, n, B))
            rounds(gp, last, B, 0, B - 1, 0, B // 2)

        @block.tensor
        def _(pe):
            ring = (ps[:, 4], ps[:, 5])

            def mm(o, l, r, k, n):
                return pe.matmul(o, l, r, start=(k == 0), stop=(k == n - 1))

            def k0():
                pe.wait_ge(ld["ctxT"], 16)
                pe.wait_ge(ld["w0k"], 16)
                for c in range(DK):
                    for n in range(2):
                        cols = slice(n * B * TC // 2, (n + 1) * B * TC // 2)
                        for k in range(DK):
                            ins = mm(ps[:, 2 * c + n, 0:B * TC // 2], w0[:, 1, k, c * P:(c + 1) * P], ctxT[:, k, cols], k, DK)
                        ins.then_inc(pk0.sem, 1)

            def v0():
                pe.wait_ge(ld["w0v"], 16)
                for b in range(B):
                    for k in range(DK):
                        ins = mm(ps[0:TC, 4 + b // 2, (b % 2) * D:(b % 2 + 1) * D], ctxT[:, k, b * TC:(b + 1) * TC], w0[:, 2, k], k, DK)
                    if b % 2:
                        ins.then_inc(pV, 1)

            def kv_time(n):
                j, u, bank, _ = kv_unit(n)
                if n % (B // 2) in (0, 1):
                    pass
                else:
                    pe.wait_ge(eKV[j], n - j * B // 2 - 1)
                for b in range(2):
                    for k in range(DK):
                        t = (2 * u + b) * TC
                        ins = mm(ps[0:TC, bank, b * D:(b + 1) * D], ctxT[:, k, t:t + TC], w1a[:, 1 + j, k], k, DK)
                ins.then_inc(pKV, 1)

            def kv_freq(n):
                j, u, _, banks = kv_unit(n)
                pe.wait_ge(eKV[j], n - j * B // 2 + 1)
                if n % 4 > 1:
                    pe.wait_ge(eKF, 2 * (n - 1))
                for m in range(2):
                    ins = pe.matmul(ps[:, banks[m], :], dft[0:TC, 0, m * P:(m + 1) * P], kv[:, n % 2], start=True, stop=True)
                ins.then_inc(pKF, 1)

            def turn_in(r):
                pe.wait_ge(ap1.sem, ap1.at(r))
                prev = r.shift(-1)
                if prev.valid:
                    pe.wait_ge(ePT.sem, ePT.at(prev, 2))
                for t in range(2):
                    for k in range(DK):
                        ins = pe.transpose(ring[1][:, k * TQ + t * P:k * TQ + (t + 1) * P], xn[:, r.parity, t, k * P:(k + 1) * P], ident[:])
                ins.then_inc(pA.sem, 1)

            def proj(r):
                prev = r.shift(-1)
                pe.wait_ge(eA.sem, eA.at(r, 1))
                if prev.valid:
                    pe.wait_ge(ePT.sem, ePT.at(prev, 3))
                for c in range(DK):
                    for k in range(DK):
                        ins = mm(ring[0][:, c * TQ:(c + 1) * TQ], w0[:, 0, k, c * P:(c + 1) * P], xnT[:, k], k, DK)
                ins.then_inc(pA.sem, 1)

            def scores(r, t):
                pe.wait_ge(eA.sem, eA.at(r))
                pe.wait_ge(kb.sem, kb.at(r))
                p = r if t else r.shift(-1)
                if p.valid:
                    pe.wait_ge(ms.sem, ms.at(p, 2 if t else 4))
                for h0, h1 in ((0, 6), (6, 8), (8, 12), (12, 16)):
                    c, n = h0 // 8, h0 // SH
                    ins = pe.matmul(ps[:, n, (h0 - n * SH) * TC:(h1 - n * SH) * TC], qT[:, r.parity, c, t * P:(t + 1) * P],
                                    kbd[:, r.parity, c, h0 - 8 * c:h1 - 8 * c, :].rearrange("p h k -> p (h k)"), start=True, stop=True)
                ins.then_inc(pS.sem, 1)

            def attend(r, t, between=None, middle=None):
                pe.wait_ge(ex.sem, ex.at(r, t + 1))

                def turn(g):
                    n = r.shift(1)
                    if g == 2:
                        pe.wait_ge(ePT.sem, ePT.at(r, NG * t + 1))
                    elif not t and r.shift(-1).valid:
                        pe.wait_ge(ePT.sem, ePT.at(r.shift(-1), NG + 2 + g))
                    elif not t:
                        pe.wait_ge(eA.sem, eA.at(r))
                    elif n.valid:
                        pe.wait_ge(eA.sem, eA.at(n, 1 + g))
                    else:
                        pe.wait_ge(ePT.sem, ePT.at(r, 2 + g))
                    blocks = [prob[:, t, h:h + HB].rearrange("p h k -> p (h k)") for h in range(0, H, HB)]
                    for c in range(*GROUPS[g]):
                        o = c - GROUPS[g][0]
                        ins = pe.transpose(ring[(g + t) % 2][:, o * P:(o + 1) * P], blocks[c // KC][:, c % KC::KC], ident[:])
                    ins.then_inc(pPT.sem, 1)

                def values(g):
                    pe.wait_ge(ePT.sem, ePT.at(r, NG * t + g + 1))
                    for c in range(*GROUPS[g]):
                        n = HB * (DH + 1)
                        ins = mm(ps[:, 6, c // KC * n:(c // KC + 1) * n], probT[:, t, c], vblk[:, r.parity, c].rearrange("p h d -> p (h d)"), c % KC, KC)
                    return ins

                turn(0)
                turn(1)
                if between:
                    between()
                turn(2)
                p = r if t else r.shift(-1)
                if p.valid:
                    pe.wait_ge(nv.sem, nv.at(p, 2 if t else 4))
                pe.wait_ge(vb.sem, vb.at(r))
                values(0)
                values(1)
                if middle:
                    middle()
                values(2).then_inc(pAV.sem, 1)

            def turn_out(r, t):
                pe.wait_ge(nv.sem, nv.at(r, 2 * t + 2))
                if t == 1 and r.shift(-1).valid:
                    pe.wait_ge(eX2.sem, eX2.at(r.shift(-1)))
                for k in range(DK):
                    ins = pe.transpose(ps[:, 7, k * P:(k + 1) * P], ao[:, t, k * P:(k + 1) * P], ident[:])
                ins.then_inc(pOT.sem, 1)

            def project(r, t):
                pe.wait_ge(eOT.sem, eOT.at(r, t + 1))
                if t and r.shift(-1).valid:
                    pe.wait_ge(sl.sem, sl.at(r.shift(-1), 1))
                if not t and r.shift(-1).valid:
                    pe.wait_ge(x1s.sem, x1s.at(r.shift(-1)))
                if t and not r.shift(-1).valid:
                    pe.wait_ge(x1s.sem, x1s.at(r, 1))
                for k in range(DK):
                    ins = mm(ps[:, 3, 0:D], aoT[:, t, k], w0[:, 3, k], k, DK)
                ins.then_inc(pWO.sem, 1)

            def turn_router(r):
                pe.wait_ge(ap2.sem, ap2.at(r))
                if r.shift(1).valid:
                    pe.wait_ge(eOT.sem, eOT.at(r.shift(1), 1))
                for t in range(2):
                    for k in range(DK):
                        o = (t * DK + k) * P
                        ins = pe.transpose(ps[:, 7, o:o + P], xn2[:, r.parity, t, k * P:(k + 1) * P], ident[:])
                ins.then_inc(pX2.sem, 1)

            def router(r):
                pe.wait_ge(eX2.sem, eX2.at(r))
                if r.shift(1).valid:
                    pe.wait_ge(x1s.sem, x1s.at(r.shift(1), 1))
                for t in range(2):
                    for k in range(DK):
                        ins = mm(ps[:, 3, t * E:(t + 1) * E], x2T[:, t, k], wg[:, k], k, DK)
                ins.then_inc(pLG.sem, 1)

            def positions(r):
                pe.wait_ge(ga.sem, ga.at(r))
                pe.wait_ge(gx.sem, gx.at(r))
                for t in range(2):
                    o = ps[:, 3, t * E:(t + 1) * E]
                    pe.matmul(o, onesb[:], seen[:, r.parity], start=True, stop=False)
                    if t:
                        pe.matmul(o, onesb[:], mask[:, r.parity, 0], start=False, stop=False)
                    ins = pe.matmul(o, trib[:], mask[:, r.parity, t], start=False, stop=True)
                ins.then_inc(pLOC.sem, 1)

            def body(r):
                b, p, n, pp = r, r.shift(-1), r.shift(1), r.shift(-2)
                if b.valid:
                    scores(b, 1)
                if pp.valid:
                    positions(pp)
                if p.valid:
                    turn_out(p, 1)
                if b.valid:
                    attend(b, 0, (lambda: project(p, 1)) if p.valid else None, (lambda: turn_in(n)) if n.valid else None)
                else:
                    if p.valid:
                        project(p, 1)
                    if n.valid:
                        turn_in(n)
                if r.static and r.n == B:
                    pe.wait_ge(ld["w1a"], 16)
                    pe.wait_ge(ld["dft"], 16)
                    pe.wait_ge(ms.sem, ms.at(p))
                    kv_time(0)
                    kv_time(1)
                if n.valid:
                    proj(n)
                if b.valid:
                    turn_out(b, 0)
                if n.valid:
                    scores(n, 0)
                if b.valid:
                    project(b, 0)
                if p.valid:
                    turn_router(p)
                if b.valid:
                    attend(b, 1, (lambda: router(p)) if p.valid else None)
                elif p.valid:
                    router(p)
                if r.static and r.n == B:
                    positions(p)

            k0()
            v0()
            pe.wait_ge(consts.sem, CONSTS)
            pe.wait_ge(ld["w0qo"], 32)
            pe.wait_ge(ek0.sem, 4)
            pe.wait_ge(eV, B)
            pe.wait_ge(ld["small"], 48)
            rounds(pe, body, B, -1, B, 1, 3)

            pe.wait_ge(sl.sem, sl.at(Round(0, B - 1, B)))
            kv_freq(0)
            kv_freq(1)

            def dsp_turn(r):
                pe.wait_ge(lddsp[r.parity], 16 * (r.half + 1))
                if r.shift(-2).valid:
                    pe.wait_ge(eD.sem, eD.at(r.shift(-2)))
                else:
                    pe.wait_ge(eKV[0], 2)
                for t in range(2):
                    for k in range(DK):
                        ins = pe.transpose(ps[:, r.parity, k * CAP + t * P:k * CAP + (t + 1) * P], dsp[:, r.parity, t, k * P:(k + 1) * P], ident[:])
                ins.then_inc(pD.sem, 1)

            def up(r):
                pe.wait_ge(ldw1[r.parity], 16 * (r.half + 1))
                pe.wait_ge(eD.sem, eD.at(r))
                if r.static and r.n == 0:
                    pe.wait_ge(eKF, 4)
                for g in range(FK // 2):
                    if r.shift(-1).valid:
                        pe.wait_ge(gl.sem, gl.at(r.shift(-1), 2 * g + 2))
                    for j in range(2):
                        f = 2 * g + j
                        for k in range(DK):
                            ins = mm(ps[:, 2 + g, j * CAP:(j + 1) * CAP], w1[:, r.parity, k, f * P:(f + 1) * P], dspT[:, r.parity, k], k, DK)
                    ins.then_inc(pG1.sem, 1)

            def down(r):
                pe.wait_ge(ldw2[r.parity], 16 * (r.half + 1))
                pe.wait_ge(gl.sem, gl.at(r))
                if r.shift(-2).valid:
                    pe.wait_ge(ye.sem, ye.at(r.shift(-2)))
                for t in range(2):
                    for f in range(FK):
                        ins = mm(ps[:, 6 + r.parity, t * D:(t + 1) * D], hid[:, r.parity, f, t * P:(t + 1) * P], w2[:, r.parity, f], f, FK)
                ins.then_inc(pG2.sem, 1)

            def expert(r):
                if r.shift(1).valid:
                    dsp_turn(r.shift(1))
                if r.valid:
                    up(r)
                if r.shift(-1).valid:
                    down(r.shift(-1))
            rounds(pe, expert, E, -1, E, 1, 3)

            kv_time(2)
            kv_time(3)

            def turn_gu(m, first):
                pe.wait_ge(wp, 5 * (m + 1))
                for k in range(DK):
                    dst = ps[:, 4 + k, 0:IK * P // 2].bitcast(BF16)
                    if m == 1:
                        pe.wait_ge(ewp, k + 1)
                    else:
                        pe.wait_ge(gl.sem, gl.at(Round(0, E - 1, E)))
                    for i in range(IK):
                        n = P if i < IK - 1 else TAIL
                        ins = pe.transpose(dst[:, i * P:i * P + n], wqs[m][0:n, i, k * P:(k + 1) * P], identb[0:n, 0:n])
                    ins.then_inc(pwp, 1)
            for m in range(2):
                turn_gu(m, m == 0)
            pe.wait_ge(wp, 15)
            for g in range(2):
                pe.wait_ge(ewp, 3 + g)
                dst = ps[:, 4 + g, 0:3 * D // 2].bitcast(BF16).rearrange("p (m d) -> p m d", m=3)
                for i in range(3):
                    m = 3 * g + i
                    n = P if m < IK - 1 else TAIL
                    for h in range(2):
                        ins = pe.transpose(dst[0:n, i, h * P:(h + 1) * P], wqd[:, h, m * P:m * P + n], identb[:])
                ins.then_inc(pwp, 1)
            pe.wait_ge(wp, 17)
            pe.wait_ge(ye.sem, ye.at(Round(0, E - 1, E)))
            for h in range(2):
                ins = pe.matmul(ps[:, 7, h * P:(h + 1) * P], onesf[:], diag[:, h], start=True, stop=True)
            ins.then_inc(pwp, 1)

            kv_freq(2)
            pe.wait_ge(ewp, 7)
            kv_freq(3)

            def xspec(r):
                pe.wait_ge(ap3.sem, ap3.at(r))
                if r.shift(-2).valid:
                    pe.wait_ge(eXH.sem, eXH.at(r.shift(-2)))
                elif r.n == 0:
                    pe.wait_ge(eKV[0], B // 2)
                for m in range(DK):
                    for k in range(DK):
                        ins = mm(ps[:, r.parity, m * TQ:(m + 1) * TQ], xn[:, r.parity, k, m * P:(m + 1) * P], dft[:, k], k, DK)
                ins.then_inc(pXH.sem, 1)

            def qspec(r):
                pe.wait_ge(eXH.sem, eXH.at(r))
                if r.shift(-2).valid:
                    pe.wait_ge(eQF.sem, eQF.at(r.shift(-2)))
                elif r.n == 1:
                    pe.wait_ge(ewp, 8)
                for m in range(2):
                    o = ps[:, 6 + r.parity, m * D:(m + 1) * D]
                    for k in range(DK):
                        ins = pe.matmul(o, xh[:, r.parity, k, m * P:(m + 1) * P], w1a[:, 0, k], start=(k == 0), stop=(m == 1 and k == 1))
                    if m == 0:
                        pe.matmul(o, dcrow[:], bq[:], start=False, stop=True)
                ins.then_inc(pQF.sem, 1)

            def spectra(r):
                if r.valid:
                    xspec(r)
                if r.shift(-1).valid:
                    qspec(r.shift(-1))
            pe.wait_ge(ld["bias"], 64)
            rounds(pe, spectra, B, 0, B, 2, B // 2)
            pe.wait_ge(eXH.sem, eXH.at(Round(0, B - 1, B)))
            kv_time(4)
            kv_time(5)
            pe.wait_ge(sp.sem, sp.at(Round(0, B - 1, B)))
            pe.wait_ge(ld["corrm"], 16)
            for j in range(4):
                ins = mm(ps[:, 3, 0:TQ], pc[:, j].rearrange("p b h -> p (b h)"), corrm[:, j], j, 4)
            ins.then_inc(pCO.sem, 1)
            kv_freq(4)
            kv_freq(5)
            kv_time(6)
            kv_time(7)
            pe.wait_ge(tk.sem, tk.per)
            for k in range(DK):
                ins = pe.transpose(ps[:, 3, TQ + k * P:TQ + (k + 1) * P], wts[:, 0, k * P:(k + 1) * P], ident[:])
            ins.then_inc(pWT.sem, 1)
            pe.wait_ge(eWT.sem, 1)
            pe.wait_ge(ld["wdft"], 16)
            for j in range(4):
                for k in range(DK):
                    ins = mm(ps[:, 7, j * P:(j + 1) * P], wdft[:, j, k], wtT[:, k], k, DK)
            ins.then_inc(pWF.sem, 1)
            kv_freq(6)
            kv_freq(7)

            def back(r):
                pe.wait_ge(uf.sem, uf.at(r))
                if r.shift(-2).valid:
                    pe.wait_ge(eOI.sem, eOI.at(r.shift(-2)))
                for m in range(DK):
                    for k in range(DK):
                        ins = mm(ps[:, r.parity, m * TQ:(m + 1) * TQ], of[:, r.parity, k, m * P:(m + 1) * P], idft[:, k], k, DK)
                ins.then_inc(pOI.sem, 1)

            def project1(r):
                pe.wait_ge(eOI.sem, eOI.at(r))
                if r.shift(-2).valid:
                    pe.wait_ge(x3s.sem, x3s.at(r.shift(-2)))
                for t in range(2):
                    for k in range(DK):
                        ins = mm(ps[:, 4 + r.parity, t * D:(t + 1) * D], oT[:, r.parity, k, t * P:(t + 1) * P], w1a[:, 3, k], k, DK)
                ins.then_inc(pY.sem, 1)

            def backs(r):
                if r.valid:
                    back(r)
                if r.static and r.n == 1:
                    pe.wait_ge(eKF, 2 * (B - 1))
                if r.shift(-1).valid:
                    project1(r.shift(-1))
            pe.wait_ge(ld["idft"], 16)
            pe.wait_ge(eKV[1], B // 2)
            rounds(pe, backs, B, 0, B, 2, B // 2)

            def turn_x(r):
                pe.wait_ge(xqs.sem, xqs.at(r))
                if r.n >= 2:
                    pe.wait_ge(eXQ.sem, eXQ.at(r.shift(-2)))
                for t in range(2):
                    for k in range(DK):
                        o = k * TQ + t * P
                        ins = pe.transpose(ps[:, r.parity, o:o + P], yg[:, r.n * 2 + t, k * P:(k + 1) * P], ident[:])
                ins.then_inc(pXQ.sem, 1)

            def gate_up(r):
                pe.wait_ge(eXQ.sem, (r.n + 1) * 2)
                for m in range(IK):
                    n = P if m < IK - 1 else TAIL
                    q = (r, m - 3) if m >= 3 else (r.shift(-1), m + 3)
                    if q[0].valid:
                        if q[1] in GC:
                            pe.wait_ge(ue.sem, ue.at(q[0], GC.index(q[1]) + 1))
                        else:
                            pe.wait_ge(hh.sem, hh.at(q[0], VC.index(q[1]) + 1))
                    for g in range(2):
                        for k in range(DK):
                            ins = mm(ps[0:n, 2 + 2 * (m % 3) + g, :], wgT[:, g, k, m * P:m * P + n], xqT[:, k, bass.ds(r.n * NB, NB)], k, DK)
                    ins.then_inc(pGU.sem, 1)
                    if m == 2 and r.n < NQ - 1:
                        for t in range(2):
                            turn_x(batch_of(r.n + 1, t))
            for t in range(2):
                turn_x(batch_of(0, t))
            for n in range(NQ):
                gate_up(Round(0, n, NQ))

            def down_last(r):
                pe.wait_ge(hqa.sem, hqa.at(r))
                pe.wait_ge(hqv.sem, hqv.at(r))
                if r.shift(-2).valid:
                    pe.wait_ge(dns.sem, dns.at(r.shift(-2)))
                for t in range(2):
                    for m in range(IK):
                        n = P if m < IK - 1 else TAIL
                        ins = mm(ps[:, r.parity, t * D:(t + 1) * D], hq[0:n, r.parity, m, t * P:(t + 1) * P], wdT[0:n, m], m, IK)
                ins.then_inc(pDN.sem, 1)
            rounds(pe, down_last, B, 0, B - 1, 1, B // 2)

        @block.scalar
        def _(act):
            act.wait_ge(ld["small"], 48)
            act.activation(gates4[:], gates4[:], ACT.Tanh).then_inc(tan.sem, 1)
            act.activation(clips[:], clips[:], ACT.Exp, scale=-1.0).then_inc(tan.sem, 1)
            for n in range(4):
                act.wait_ge(pk0.sem, n + 1)
                act.copy(k0T[:, n // 2, (n % 2) * B * TC // 2:(n % 2 + 1) * B * TC // 2], ps[:, n, 0:B * TC // 2]).then_inc(ek0.sem, 1)

            def probs(r, t):
                act.wait_ge(ms.sem, ms.at(r, 2 * t + 2))
                v = prob[:, t, :, 0:TC]
                act.activation(v, v, ACT.Exp).then_inc(ex.sem, 1)

            def copy_out(r, t):
                act.wait_ge(pOT.sem, pOT.at(r, t + 1))
                if r.shift(-1).valid:
                    act.wait_ge(pWO.sem, pWO.at(r.shift(-1), t + 1))
                act.copy(aoT[:, t].rearrange("p k s -> p (k s)"), ps[:, 7, 0:2 * P]).then_inc(eOT.sem, 1)

            def copy_probs(r, t):
                if r.shift(-1).valid:
                    act.wait_ge(pAV.sem, pAV.at(r.shift(-1), t + 1))
                for g, (lo, hi) in enumerate(GROUPS):
                    act.wait_ge(pPT.sem, pPT.at(r, NG * t + g + 1))
                    act.copy(probT[:, t, lo:hi].rearrange("p c s -> p (c s)"), ps[:, 4 + (g + t) % 2, 0:(hi - lo) * P]).then_inc(ePT.sem, 1)

            def copy_in(r):
                act.wait_ge(pA.sem, pA.at(r, 1))
                if r.shift(-1).valid:
                    act.wait_ge(pA.sem, pA.at(r.shift(-1), 2))
                act.copy(xnT[:].rearrange("p k s -> p (k s)"), ps[:, 5, :]).then_inc(eA.sem, 1)

            def copy_proj(r):
                act.wait_ge(pA.sem, pA.at(r, 2))
                if r.shift(-2).valid:
                    act.wait_ge(pS.sem, pS.at(r.shift(-2)))
                act.mul(qT[:, r.parity].rearrange("p k s -> p (k s)"), ps[:, 4, :], DH ** -0.5).then_inc(eA.sem, 1)

            def normalise_with(r, rs, ap, rr, nr, dst):
                act.wait_ge(rs.sem, rs.at(r))
                for t in range(2):
                    act.activation(dst(t), x[:, r.n * 2 + t, :], ACT.Identity, bias=nr[:, t:t + 1], scale=rr[:, t:t + 1]).then_inc(ap.sem, 1)

            def norm1(r):
                if r.shift(-2).valid:
                    act.wait_ge(pA.sem, pA.at(r.shift(-2), 1))
                normalise_with(r, rs1, ap1, rstd, nmr, lambda t: xn[:, r.parity, t])

            def norm2(r):
                if r.shift(-2).valid:
                    for t in range(2):
                        act.wait_ge(scat[r.parity][t], 16 * r.half)
                    act.wait_ge(pX2.sem, pX2.at(r.shift(-2)))
                normalise_with(r, rs2, ap2, rstd2, nmr2, lambda t: xn2[:, r.parity, t])

            def copy_router(r):
                if r.shift(-1).valid:
                    act.wait_ge(pLG.sem, pLG.at(r.shift(-1)))
                act.wait_ge(pX2.sem, pX2.at(r))
                act.copy(x2T[:].rearrange("p t k s -> p (t k s)"), ps[:, 7, :]).then_inc(eX2.sem, 1)

            def gate(r):
                act.wait_ge(ga.sem, ga.at(r, 5))
                for t in range(2):
                    act.activation(gexp[:, t], ps[:, 3, t * E:(t + 1) * E], ACT.Exp, bias=ntop[:, t:t + 1],
                                   accum_out=gsum[:, bass.ds(r.n * 2 + t, 1)]).then_inc(gx.sem, 1)

            def body(r):
                b, p, n = r, r.shift(-1), r.shift(1)
                if p.valid:
                    copy_out(p, 1)
                if b.valid:
                    copy_probs(b, 0)
                if n.valid:
                    copy_in(n)
                if b.valid:
                    probs(b, 1)
                if n.valid:
                    copy_proj(n)
                if b.valid:
                    copy_out(b, 0)
                if p.valid:
                    norm2(p)
                    copy_router(p)
                if b.valid:
                    copy_probs(b, 1)
                if n.valid:
                    probs(n, 0)
                if p.valid:
                    gate(p)
                if r.shift(2).valid:
                    norm1(r.shift(2))
            act.wait_ge(consts.sem, CONSTS)
            norm1(Round(0, 0, B))
            rounds(act, body, B, -1, B, 1, 3)

            def copy_kf(n):
                j, u, _, banks = kv_unit(n)
                act.wait_ge(pKF, n + 1)
                for m in range(2):
                    act.copy(kvf[:, j, u, m].rearrange("p b d -> p (b d)"), ps[:, banks[m], :]).then_inc(eKF, 1)
            for n in range(2):
                copy_kf(n)

            def gelu(r):
                if r.shift(-2).valid:
                    act.wait_ge(pG2.sem, pG2.at(r.shift(-2)))
                for f in range(FK):
                    act.wait_ge(pG1.sem, pG1.at(r, f // 2 + 1))
                    act.activation(hid[:, r.parity, f], ps[:, 2 + f // 2, (f % 2) * CAP:(f % 2 + 1) * CAP], ACT.Gelu_apprx_tanh,
                                   bias=b1[:, bass.ds(r.n * FK + f, 1)]).then_inc(gl.sem, 1)
            act.wait_ge(ld["b1"], 16)
            yv = yexp.rearrange("(e t p) d -> e p t d", e=E, p=P)

            def gelu_store(r):
                if r.valid:
                    gelu(r)
                q = r.shift(-1)
                if q.valid:
                    act.wait_ge(ye.sem, ye.at(q))
                    act.dma_start(yv[q.n], yex[:, q.parity]).then_inc(stored[q.parity], 16)
            rounds(act, gelu_store, E, 0, E, 1, E // 2)

            for m in range(2):
                for k in range(DK):
                    act.wait_ge(pwp, 2 * m + k + 1)
                    act.copy(wgT[:, m, k], ps[:, 4 + k, 0:I // 2].bitcast(BF16)).then_inc(ewp, 1)
            for g in range(2):
                act.wait_ge(pwp, 5 + g)
                src = ps[:, 4 + g, 0:3 * D // 2].bitcast(BF16)
                if g == 0:
                    act.copy(wdT[:, 0:3].rearrange("p m d -> p (m d)"), src).then_inc(ewp, 1)
                else:
                    act.copy(wdT[:, 3:5].rearrange("p m d -> p (m d)"), src[:, 0:2 * D]).then_inc(ewp, 1)
                    act.copy(wdT[0:TAIL, 5], src[0:TAIL, 2 * D:3 * D]).then_inc(ewp, 1)
            act.wait_ge(pwp, 7)
            act.copy(dscale[:], ps[:, 7, 0:D]).then_inc(ewp, 1)
            copy_kf(2)
            copy_kf(3)

            def copy_xh(r):
                act.wait_ge(pXH.sem, pXH.at(r))
                if r.shift(-2).valid:
                    act.wait_ge(pQF.sem, pQF.at(r.shift(-2)))
                act.copy(xh[:, r.parity].rearrange("p k s -> p (k s)"), ps[:, r.parity, :]).then_inc(eXH.sem, 1)

            def spectra(r):
                if r.valid:
                    if r.shift(-2).valid:
                        act.wait_ge(pXH.sem, pXH.at(r.shift(-2)))
                    normalise_with(r, rs3, ap3, rstd, nmr, lambda t: xn[:, r.parity, t])
                if r.shift(-1).valid:
                    copy_xh(r.shift(-1))
                q = r.shift(-2)
                if q.valid:
                    act.wait_ge(pQF.sem, pQF.at(q))
                    if q.shift(-2).valid:
                        act.wait_ge(pr.sem, pr.at(q.shift(-2)))
                        act.wait_ge(pr2.sem, pr2.at(q.shift(-2)))
                    act.copy(qs[:, q.parity].rearrange("p m d -> p (m d)"), ps[:, 6 + q.parity, :]).then_inc(eQF.sem, 1)
            rounds(act, spectra, B, 0, B + 1, 2, B // 2)

            act.wait_ge(tk.sem, 4)
            act.activation(cw[:], c8[:, 0:TOPK], ACT.Exp, bias=nc0[:], accum_out=cs[:]).then_inc(tx.sem, 1)
            copy_kf(4)
            copy_kf(5)
            act.wait_ge(pWT.sem, 1)
            act.copy(wtT[:].rearrange("p k s -> p (k s)"), ps[:, 3, TQ:2 * TQ]).then_inc(eWT.sem, 1)
            act.wait_ge(pWF.sem, 1)
            act.copy(wf[:].rearrange("p j s -> p (j s)"), ps[:, 7, :]).then_inc(eWF.sem, 1)
            copy_kf(6)
            copy_kf(7)

            def copy_back(r):
                act.wait_ge(pOI.sem, pOI.at(r))
                if r.shift(-2).valid:
                    act.wait_ge(pY.sem, pY.at(r.shift(-2)))
                act.copy(oT[:, r.parity].rearrange("p k s -> p (k s)"), ps[:, r.parity, :]).then_inc(eOI.sem, 1)

            def back(r):
                if r.valid:
                    copy_back(r)
                q = r.shift(-2)
                if q.valid:
                    normalise_with(q, rs4, ap4, rstd2, nmr2, lambda t: yg[:, q.n * 2 + t, :])
            rounds(act, back, B, 0, B + 1, 1, B // 2)

            def round_x(r):
                f = yg[:, bass.ds(r.n * 2, 2), :]
                act.activation(f, f, ACT.Identity, bias=magicc[:], scale=sx[:, 1:2]).then_inc(xq1.sem, 1)

            def copy_xq(r):
                act.wait_ge(pXQ.sem, pXQ.at(r))
                act.activation(xqT[:, :, r.n * TQ:(r.n + 1) * TQ], ps[:, r.parity, :].rearrange("p (k s) -> p k s", k=DK),
                               ACT.Identity, bias=nmagic[:]).then_inc(eXQ.sem, 1)

            def silu(r):
                for m in range(IK):
                    n = P if m < IK - 1 else TAIL
                    act.wait_ge(pGU.sem, pGU.at(r, m + 1))
                    j = (GC if m in GC else VC).index(m)
                    if m in GC:
                        g = r.n * len(GC) + j
                        if g >= 2:
                            act.wait_ge(hp.sem, g - 1)
                        act.activation(silp[0:n, g % 2], ps[0:n, 2 + 2 * (m % 3), :], ACT.Silu, scale=sgu[0:n, 0, m:m + 1]).then_inc(si.sem, 1)
                        act.activation(upp[0:n, g % 2], ps[0:n, 3 + 2 * (m % 3), :], ACT.Identity, scale=sgu[0:n, 1, m:m + 1]).then_inc(ue.sem, 1)
                    else:
                        g = r.n * len(VC) + j
                        if g >= 2:
                            act.wait_ge(hh.sem, g - 1)
                        act.activation(sil[0:n, g % 2], ps[0:n, 2 + 2 * (m % 3), :], ACT.Silu, scale=sgu[0:n, 0, m:m + 1]).then_inc(si.sem, 1)
                    if m == 2 and r.n < NQ - 1:
                        for t in range(2):
                            copy_xq(batch_of(r.n + 1, t))
            act.activation(warm[:], epsc[:, 0:1], ACT.Silu)
            act.wait_ge(sc, 4)
            for n in range(2):
                round_x(Round(0, n, B))
            for t in range(2):
                copy_xq(batch_of(0, t))
            for n in range(NQ):
                silu(Round(0, n, NQ))

            act.wait_ge(sch, 5)

            def quant_h(r):
                if r.valid:
                    f = hT[:, 0:HR, bass.ds(r.n * TQ, TQ)]
                    act.activation(f, f, ACT.Identity, bias=magicc[:], scale=sx[:, 1:2]).then_inc(hq1.sem, 1)
                q = r.shift(-1)
                if q.valid:
                    act.wait_ge(hqc.sem, hqc.at(q))
                    if q.shift(-2).valid:
                        act.wait_ge(pDN.sem, pDN.at(q.shift(-2)))
                    act.activation(hq[:, q.parity, 0:HA], hT[:, 0:HA, bass.ds(q.n * TQ, TQ)], ACT.Identity, bias=nmagic[:]).then_inc(hqa.sem, 1)
            for n in range(B + 1):
                quant_h(Round(0, n, B))

        @block.vector
        def _(dv):
            def statistics(r, ln, rs, s, m):
                if r.shift(-1).valid:
                    dv.wait_ge(rs.sem, rs.at(r.shift(-1)))
                alone(dv)
                for t in range(2):
                    dv.bn_stats(s[:, t], tile_of(r, t)).then_inc(ln.sem, 1)
                dv.wait_ge(ln.sem, ln.at(r, 2))
                alone(dv)
                for t in range(2):
                    dv.bn_aggr(m[:, t], s[:, t]).then_inc(ln.sem, 1)

            def tile_of(r, t):
                return x[:, r.n * 2 + t, :]

            def norm1(r):
                statistics(r, ln1, rs1, st, mv)

            def less_max(r, t):
                dv.wait_ge(pS.sem, pS.at(r, t + 1))
                whole, n = H // SH, H % SH
                s = ps[:, 0:whole, 0:SH * TC].rearrange("p n (h k) -> p n h k", h=SH)
                s4 = ps[:, whole, 0:n * TC].rearrange("p (h k) -> p h k", h=n)
                dv.tensor_reduce(mx[:, t, 0:whole * SH].rearrange("p (n h) -> p n h", h=SH), s, AX_X, ALU.max)
                dv.tensor_reduce(mx[:, t, whole * SH:H], s4, AX_X, ALU.max).then_inc(ms.sem, 1)
                dv.wait_ge(ms.sem, ms.at(r, 2 * t + 1))
                if r.shift(-1).valid:
                    dv.wait_ge(pPT.sem, pPT.at(r.shift(-1), NG * (t + 1)))
                dv.tensor_tensor(prob[:, t, 0:whole * SH, 0:TC].rearrange("p (n h) k -> p n h k", h=SH), s,
                                 mx[:, t, 0:whole * SH].rearrange("p (n h) -> p n h", h=SH)[:, :, :, None].broadcast_to([P, whole, SH, TC]),
                                 ALU.subtract)
                dv.tensor_tensor(prob[:, t, whole * SH:H, 0:TC], s4, mx[:, t, whole * SH:H][:, :, None].broadcast_to([P, n, TC]),
                                 ALU.subtract).then_inc(ms.sem, 1)

            def normalise(r, t):
                dv.wait_ge(pAV.sem, pAV.at(r, t + 1))
                v = ps[:, 6, 0:H * (DH + 1)].rearrange("p (h d) -> p h d", h=H)
                dv.reciprocal(rden[:, t], v[:, :, DH]).then_inc(nv.sem, 1)
                dv.wait_ge(nv.sem, nv.at(r, 2 * t + 1))
                if r.shift(-1).valid:
                    dv.wait_ge(pOT.sem, pOT.at(r.shift(-1), t + 1))
                dv.tensor_tensor(ao[:, t].rearrange("p (h d) -> p h d", h=H), v[:, :, 0:DH],
                                 rden[:, t][:, :, None].broadcast_to([P, H, DH]), ALU.mult).then_inc(nv.sem, 1)

            def residual1(r, t):
                dv.wait_ge(pWO.sem, pWO.at(r, t + 1))
                dv.scalar_tensor_tensor(tile_of(r, t), ps[:, 3, 0:D], gates4[:, 0:1], tile_of(r, t), ALU.mult, ALU.add).then_inc(x1s.sem, 1)

            def norm2(r):
                dv.wait_ge(x1s.sem, x1s.at(r))
                statistics(r, ln2, rs2, st2, mv2)

            def choose(r):
                dv.wait_ge(pLG.sem, pLG.at(r))
                alone(dv)
                lg = ps[:, 3, 0:2 * E].rearrange("p (t e) -> p t e", t=2)
                for t in range(2):
                    dv.max(top[:, t], lg[:, t]).then_inc(ga.sem, 1)
                dv.wait_ge(ga.sem, ga.at(r, 2))
                if r.shift(-1).valid:
                    dv.wait_ge(gx.sem, gx.at(r.shift(-1)))
                dv.tensor_scalar(ntop[:], top[:, :, 0], -1.0, None, ALU.mult).then_inc(ga.sem, 1)
                for t in range(2):
                    dv.max_index(topi[:, t], top[:, t], lg[:, t]).then_inc(ga.sem, 1)
                dv.wait_ge(ga.sem, ga.at(r, 5))
                dv.tensor_copy(eidx[:, r.parity], topi[:, :, 0]).then_inc(ga.sem, 1)
                dv.wait_ge(ga.sem, ga.at(r, 6))
                if r.shift(-2).valid:
                    dv.wait_ge(pLOC.sem, pLOC.at(r.shift(-2)))
                dv.tensor_tensor(mask[:, r.parity], iota8[:, None, :].broadcast_to([P, 2, E]),
                                 eidx[:, r.parity][:, :, None].broadcast_to([P, 2, E]), ALU.is_equal).then_inc(ga.sem, 1)
                dv.wait_ge(ga.sem, ga.at(r, 7))
                dv.tensor_tensor(seen1[:], mask[:, r.parity, 0], mask[:, r.parity, 1], ALU.add).then_inc(ga.sem, 1)
                dv.wait_ge(ga.sem, ga.at(r, 8))
                if r.shift(-1).valid:
                    dv.wait_ge(pLOC.sem, pLOC.at(r.shift(-1)))
                dv.tensor_tensor(seen[:, 1 - r.parity], seen[:, r.parity], seen1[:], ALU.add).then_inc(ga.sem, 1)

            def place(r, first):
                n = 0 if first else 2

                def step(ins):
                    nonlocal n
                    n += 1
                    ins.then_inc(sl.sem, 1)
                    dv.wait_ge(sl.sem, sl.at(r, n))
                if first:
                    dv.wait_ge(pLOC.sem, pLOC.at(r))
                    lo = ps[:, 3, 0:2 * E].rearrange("p (t e) -> p t e", t=2)
                    step(dv.tensor_tensor(lm[:], lo, mask[:, r.parity], ALU.mult))
                    step(dv.tensor_reduce(pos[:], lm[:], AX_X, ALU.add))
                    return
                at = bass.ds(r.n * 2, 2)
                step(dv.scalar_tensor_tensor(slot[:, at], eidx[:, r.parity], float(CAP), pos[:], ALU.mult, ALU.add))
                step(dv.tensor_scalar(keep[:, at], pos[:], float(CAP), None, ALU.is_le))
                step(dv.tensor_scalar(skip[:], keep[:, at], -2.0 * SLOTS, 2.0 * SLOTS - 1, ALU.mult, ALU.add))
                if r.shift(-2).valid:
                    for t in range(2):
                        dv.wait_ge(scat[r.parity][t], 16 * r.half)
                step(dv.tensor_tensor(slots[:, r.parity], slot[:, at], skip[:], ALU.add))
                assert n == sl.per

            def body(r):
                b, p, n, pp = r, r.shift(-1), r.shift(1), r.shift(-2)
                if pp.valid:
                    place(pp, True)
                if b.valid:
                    less_max(b, 1)
                if p.valid:
                    residual1(p, 1)
                    norm2(p)
                if b.valid:
                    normalise(b, 0)
                if pp.valid:
                    place(pp, False)
                if b.valid:
                    residual1(b, 0)
                if n.valid:
                    less_max(n, 0)
                if r.shift(2).valid:
                    norm1(r.shift(2))
                if p.valid:
                    choose(p)
                if b.valid:
                    normalise(b, 1)
                if r.static and r.n == B:
                    place(p, True)
                    place(p, False)
            dv.memset(wnat[TAIL:P, IK - 1, :], 1.0).then_inc(wtail, 1)
            dv.wait_ge(ld["x0"], 16)
            norm1(Round(0, 0, B))
            norm1(Round(0, 1, B))
            for b in range(B):
                dv.wait_ge(pV, b // 2 + 1)
                dv.tensor_copy(v0s[:, :, b], ps[0:TC, 4 + b // 2, (b % 2) * D:(b % 2 + 1) * D].rearrange("k (g h d) -> k h g d", g=2, h=HB)).then_inc(eV, 1)
            dv.wait_ge(tan.sem, 2)
            dv.wait_ge(consts.sem, CONSTS)
            dv.wait_ge(ld["x1"], 16)
            less_max(Round(0, 0, B), 0)
            rounds(dv, body, B, 0, B, 1, 3)

            dv.tensor_scalar(slot[:], slot[:], -1.0, float(SLOTS - 1), ALU.add, ALU.min).then_inc(bulk, 1)
            dv.reciprocal(grec[:], gsum[:]).then_inc(bulk, 1)
            dv.wait_ge(bulk, 2)
            dv.tensor_copy(slotg[:], slot[:]).then_inc(bulk, 1)
            dv.tensor_scalar(grec[:], grec[:], gates4[:, 2:3], None, ALU.mult).then_inc(bulk, 1)
            dv.wait_ge(bulk, 4)
            dv.tensor_tensor(gk[:], grec[:], keep[:], ALU.mult).then_inc(bulk, 1)

            dv.tensor_scalar(clips[:], clips[:], QMAX, QMAX, ALU.mult, ALU.add).then_inc(sch, 1)
            dv.wait_ge(sch, 1)
            dv.reciprocal(clipr[:], clips[:]).then_inc(sch, 1)

            dv.wait_ge(ld["bias"], 64)

            for n in range(2):
                bias_kv(dv, n)

            def quantise(m, v, o):
                nr = v.shape[1]
                dv.wait_ge(ld[f"wnat{m}"], 32 if m < 2 else 16)
                dv.tensor_reduce(wab[:, 0:nr], v, AX_X, ALU.max, apply_absolute_value=True).then_inc(wp, 1)
                dv.wait_ge(wp, 5 * m + 1)
                dv.tensor_scalar(wsc[:, m, 0:nr], wab[:, 0:nr], 1.0 / QMAX, None, ALU.mult).then_inc(wp, 1)
                dv.wait_ge(wp, 5 * m + 2)
                dv.reciprocal(wrec[:, 0:nr], wsc[:, m, 0:nr]).then_inc(wp, 1)
                dv.wait_ge(wp, 5 * m + 3)
                dv.tensor_tensor(v, v, wrec[:, 0:nr][:, :, None].broadcast_to([P, nr, v.shape[2]]), ALU.mult).then_inc(wp, 1)
                dv.wait_ge(wp, 5 * m + 4)
                dv.tensor_scalar(o, v, MAGIC, MAGIC, ALU.add, ALU.subtract).then_inc(wp, 1)

            def quantise_one(m):
                if m < 2:
                    quantise(m, wnat[:], wqs[m])
                else:
                    quantise(m, wnd, wqd)
                    for h in range(2):
                        dv.tensor_scalar(diag[:, h], ident[:], wsc[:, 2, h:h + 1], None, ALU.mult).then_inc(wp, 1)

            def expert(r):
                if r.valid:
                    dv.wait_ge(pD.sem, pD.at(r))
                    if r.shift(-2).valid:
                        dv.wait_ge(pG1.sem, pG1.at(r.shift(-2)))
                    dv.tensor_copy(dspT[:, r.parity].rearrange("p k s -> p (k s)"), ps[:, r.parity, :]).then_inc(eD.sem, 1)
                if r.static and 1 <= r.n <= 3:
                    quantise_one(r.n - 1)
                q = r.shift(-2)
                if q.valid:
                    dv.wait_ge(pG2.sem, pG2.at(q))
                    dv.wait_ge(ldb2[q.parity], 16 * (q.half + 1))
                    if q.shift(-2).valid:
                        dv.wait_ge(stored[q.parity], 16 * q.half)
                    dv.tensor_tensor(yex[:, q.parity], ps[:, 6 + q.parity, :].rearrange("p (t d) -> p t d", t=2),
                                     b2[:, q.parity][:, None, :].broadcast_to([P, 2, D]), ALU.add).then_inc(ye.sem, 1)
            rounds(dv, expert, E, 0, E + 1, 2, 4)
            bias_kv(dv, 2)
            bias_kv(dv, 3)

            def residual2(r):
                for t in range(2):
                    dv.scalar_tensor_tensor(tile_of(r, t), yg[:, r.n * 2 + t, :], gk[:, bass.ds(r.n * 2 + t, 1)], tile_of(r, t),
                                            ALU.mult, ALU.add).then_inc(x2s.sem, 1)
                dv.wait_ge(x2s.sem, x2s.at(r))
                statistics(r, ln3, rs3, st, mv)

            def products(r):
                dv.wait_ge(eQF.sem, eQF.at(r))
                dv.tensor_tensor(prod[:, r.parity, 0:2], qs[:, r.parity], spectrum(r, 0), ALU.mult).then_inc(pr.sem, 1)

            def summed(r):
                dv.wait_ge(pr.sem, pr.at(r))
                dv.wait_ge(pr2.sem, pr2.at(r))
                dv.tensor_reduce(pc[:, :, r.n, :], prod[:, r.parity].rearrange("p j (h d) -> p j h d", h=H), AX_X, ALU.add).then_inc(sp.sem, 1)

            def layer1(r):
                if r.static and r.n == 2:
                    dv.wait_ge(eKF, B)
                if r.valid:
                    dv.wait_ge(gath[r.n], 32)
                    residual2(r)
                if r.shift(-4).valid:
                    summed(r.shift(-4))
                if r.shift(-3).valid:
                    products(r.shift(-3))
            for n in range(B + 4):
                layer1(Round(0, n, B))

            n = 0

            def step(ins):
                nonlocal n
                n += 1
                ins.then_inc(tk.sem, 1)
                dv.wait_ge(tk.sem, n)
            bias_kv(dv, 4)
            bias_kv(dv, 5)
            dv.wait_ge(pCO.sem, 1)
            step(dv.tensor_copy(corr[:], ps[:, 3, 0:TQ]))
            step(dv.max(c8[:], corr[:]))
            step(dv.max_index(ci[:], c8[:], corr[:]))
            step(dv.tensor_scalar(nc0[:], c8[:, 0:1], -1.0, None, ALU.mult))
            step(dv.tensor_copy(cif[:], ci[:]))
            dv.wait_ge(tx.sem, 1)
            step(dv.reciprocal(cr[:], cs[:]))
            step(dv.tensor_scalar(cw[:], cw[:], cr[:], None, ALU.mult))
            for k in range(TOPK):
                ins = dv.tensor_scalar(wts[:, k], iotaT[:], cif[:, k:k + 1], cw[:, k:k + 1], ALU.is_equal, ALU.mult)
                n += 1
                ins.then_inc(tk.sem, 1)
            dv.wait_ge(tk.sem, n)
            for k in range(1, TOPK):
                step(dv.tensor_tensor(wts[:, 0], wts[:, 0], wts[:, k], ALU.add))
            assert n == tk.per

            bias_kv(dv, 6)
            bias_kv(dv, 7)
            dv.wait_ge(eWF.sem, 1)

            def parts(r):
                if r.shift(-2).valid:
                    dv.wait_ge(uf.sem, uf.at(r.shift(-2)))
                dv.tensor_tensor(u1[:, r.parity].rearrange("p m (h d) -> p m h d", h=H),
                                 spectrum(r, 1).rearrange("p m (h d) -> p m h d", h=H),
                                 wf[:, 0:2, bass.ds(r.n * H, H)][:, :, :, None].broadcast_to([P, 2, H, DH]), ALU.mult).then_inc(uu.sem, 1)

            def rolled(r):
                dv.wait_ge(uu.sem, uu.at(r))
                dv.wait_ge(uv.sem, uv.at(r))
                if r.shift(-2).valid:
                    dv.wait_ge(pOI.sem, pOI.at(r.shift(-2)))
                dv.tensor_tensor(of[:, r.parity], u1[:, r.parity], u2[:, r.parity], ALU.add).then_inc(uf.sem, 1)

            def residual3(r):
                dv.wait_ge(pY.sem, pY.at(r))
                dv.wait_ge(x2b.sem, x2b.at(r))
                xv = x[:, bass.ds(r.n * 2, 2), :]
                dv.scalar_tensor_tensor(xv, ps[:, 4 + r.parity, :].rearrange("p (t d) -> p t d", t=2), gates4[:, 1:2], xv,
                                        ALU.mult, ALU.add).then_inc(x3s.sem, 1)
                dv.wait_ge(x3s.sem, x3s.at(r))
                statistics(r, ln4, rs4, st2, mv2)

            def largest(r):
                dv.wait_ge(ap4.sem, ap4.at(r))
                dv.tensor_reduce(amax[:, bass.ds(r.n * 2, 2)], yg[:, bass.ds(r.n * 2, 2), :], AX_X, ALU.max,
                                 apply_absolute_value=True).then_inc(mx4.sem, 1)

            def layer1b(r):
                if r.valid:
                    rolled(r)
                if r.static and r.n in (-1, 3):
                    dv.wait_ge(eKF, 3 * B // 2 if r.n < 0 else 2 * B)
                if r.shift(1).valid:
                    parts(r.shift(1))
                if r.shift(-2).valid:
                    residual3(r.shift(-2))
                if r.shift(-3).valid:
                    largest(r.shift(-3))
            rounds(dv, layer1b, B, -1, B + 2, 2, 3)

            dv.wait_ge(mx4.sem, mx4.at(Round(0, B - 1, B)))
            dv.tensor_reduce(am1[:], amax[:], AX_X, ALU.max).then_inc(sc, 1)
            dv.wait_ge(arx, 1)
            dv.tensor_scalar(sx[:, 0:1], am2[:], clipr[:, 0:1], None, ALU.mult).then_inc(sc, 1)
            dv.wait_ge(sc, 2)
            dv.reciprocal(sx[:, 1:2], sx[:, 0:1]).then_inc(sc, 1)
            dv.tensor_scalar(sgu[:], wsc[:, 0:2], sx[:, 0:1], None, ALU.mult).then_inc(sc, 1)
            dv.wait_ge(sc, 4)

            def clip_x(r):
                f = yg[:, bass.ds(r.n * 2, 2), :]
                if r.n < 2:
                    dv.wait_ge(xq1.sem, xq1.at(r))
                else:
                    dv.wait_ge(xg1, r.n - 1)
                dv.tensor_scalar(f, f, MAGIC + QMAX, MAGIC - QMAX - 1.0, ALU.min, ALU.max).then_inc(xqs.sem, 1)

            dv.memset(hmaxs[:], 0.0).then_inc(hmx, 1)
            for n in range(B):
                clip_x(Round(0, n, B))
            dv.wait_ge(hmx, 1)

            def gated(r):
                for j, m in enumerate(VC):
                    n = P if m < IK - 1 else TAIL
                    dv.wait_ge(si.sem, si.at(r, m + 1))
                    h = hT[0:n, m, r.n * NB:(r.n + 1) * NB]
                    dv.scalar_tensor_tensor(h, ps[0:n, 3 + 2 * (m % 3), :], sgu[0:n, 1, m:m + 1], sil[0:n, (r.n * len(VC) + j) % 2], ALU.mult, ALU.mult).then_inc(hh.sem, 1)
                    if j == 0 and r.shift(-1).valid:
                        hidden_max(r.shift(-1), VC[-1])
                        hidden_max(r.shift(-1), GC[-1])
                    for done in ((), (0,), (2, 1), (3,))[j]:
                        hidden_max(r, done)

            def hidden_max(r, m):
                n = P if m < IK - 1 else TAIL
                if m in GC:
                    dv.wait_ge(hp.sem, hp.at(r, GC.index(m) + 1))
                else:
                    dv.wait_ge(hh.sem, hh.at(r, VC.index(m) + 1))
                at = r.n * IK + m
                dv.tensor_reduce(hmaxs[0:n, at:at + 1], hT[0:n, m, r.n * NB:(r.n + 1) * NB], AX_X, ALU.max,
                                 apply_absolute_value=True).then_inc(hmx, 1)

            for n in range(NQ):
                gated(Round(0, n, NQ))
            hidden_max(Round(0, NQ - 1, NQ), VC[-1])
            hidden_max(Round(0, NQ - 1, NQ), GC[-1])
            dv.wait_ge(hmx, 1 + IK * NQ)
            dv.wait_ge(xg1, B - 1)
            dv.tensor_reduce(am1[:], hmaxs[:], AX_X, ALU.max).then_inc(hmx, 1)
            dv.wait_ge(arx, 2)
            dv.tensor_scalar(sx[:, 0:1], am2[:], clipr[:, 1:2], None, ALU.mult).then_inc(sch, 1)
            dv.wait_ge(sch, 3)
            dv.wait_ge(ewp, 8)
            dv.reciprocal(sx[:, 1:2], sx[:, 0:1]).then_inc(sch, 1)
            dv.tensor_scalar(dscale[:], dscale[:], sx[:, 0:1], gates4[:, 3:4], ALU.mult, ALU.mult).then_inc(sch, 1)
            dv.wait_ge(sch, 5)

            def clip_h(r):
                f = hT[:, :, bass.ds(r.n * TQ, TQ)]
                dv.wait_ge(hq1.sem, hq1.at(r))
                dv.wait_ge(hqg.sem, hqg.at(r))
                dv.tensor_scalar(f, f, MAGIC - QMAX - 1.0, MAGIC + QMAX, ALU.max, ALU.min).then_inc(hqc.sem, 1)

            def quant_h(r):
                dv.wait_ge(hqc.sem, hqc.at(r))
                if r.shift(-2).valid:
                    dv.wait_ge(pDN.sem, pDN.at(r.shift(-2)))
                dv.tensor_scalar(hq[:, r.parity, HA:], hT[:, HA:, bass.ds(r.n * TQ, TQ)], MAGIC, None, ALU.subtract).then_inc(hqv.sem, 1)

            def scale_down(r):
                dv.wait_ge(pDN.sem, pDN.at(r))
                if r.shift(-2).valid:
                    dv.wait_ge(fin.sem, fin.at(r.shift(-2)))
                dv.tensor_tensor(xn[:, r.parity], ps[:, r.parity, :].rearrange("p (t d) -> p t d", t=2),
                                 dscale[:, None, :].broadcast_to([P, 2, D]), ALU.mult).then_inc(dns.sem, 1)

            clip_h(Round(0, 0, B))
            for n in range(B + 1):
                r = Round(0, n, B)
                if n and r.shift(1).valid:
                    clip_h(r.shift(1))
                if r.valid:
                    quant_h(r)
                if n == 0:
                    clip_h(r.shift(1))
                if r.shift(-1).valid:
                    scale_down(r.shift(-1))


CONSTS = 19
ZEROS = 14


def constants():
    n = np.arange(TQ)
    cos = lambda f: np.cos(2 * np.pi * ((np.outer(n, f)) % TQ) / TQ)
    sin = lambda f: np.sin(2 * np.pi * ((np.outer(n, f)) % TQ) / TQ)
    f = np.arange(P)
    c, s, nyq = cos(f), sin(f), cos([P])
    s0 = s.copy()
    s0[:, 0:1] = nyq
    dft = np.concatenate([c, s0], 1)
    weight = np.where(f == 0, 1.0, 2.0) / TQ
    ic, is_ = (c * weight).T, (s * weight).T
    isn = is_.copy()
    isn[0] = nyq[:, 0] / TQ
    idft = np.concatenate([ic, isn], 0)
    m1 = ic.copy()
    m2 = ic.copy()
    m2[0] = nyq[:, 0] / TQ
    corrm = np.stack([m1, m2, is_, -is_]) / DH
    cn = c.copy()
    cn[:, 0:1] = nyq
    wd = np.stack([c, cn, s, -s])
    g = lambda m: np.ascontiguousarray(m, dtype=np.float32)
    dc = np.zeros((1, P))
    dc[0, 0] = TQ
    return {
        "dft": g(dft.reshape(DK, P, TQ).transpose(1, 0, 2)),
        "idft": g(idft.reshape(DK, P, TQ).transpose(1, 0, 2)),
        "corrm": g(corrm.transpose(1, 0, 2)),
        "wdft": g(wd.reshape(4, DK, P, P).transpose(2, 0, 1, 3)),
        "dcrow": g(dc),
    }


def kernel(**inputs):
    import concourse.bacc as bacc
    from concourse.bass_utils import run_bass_kernel_spmd

    v = {n: np.asarray(t) for n, t in inputs.items()}

    def rows(m):
        return m.reshape(DK, P, -1).transpose(1, 0, 2)

    arrays = {
        "x": v["x"].reshape(B * TQ, D),
        "ctxT": rows(v["ctx_1024"].reshape(B * TC, D).T),
        "w0": np.stack([rows(v["L0_xattn_" + n].T) for n in ("Wq", "Wk", "Wv", "Wo")], 1),
        "w1a": np.stack([rows(v["L1_xattn_" + n]) for n in ("Wq", "Wk", "Wv", "Wo")], 1),
        "wg": rows(v["L0_ffn_wg"]),
        "gates": np.concatenate([v["g_xattn"], v["g_ffn"]]),
        "clips": np.concatenate([v["L1_ffn_clip_x"], v["L1_ffn_clip_down"]]),
        "b1": v["L0_ffn_b1"].reshape(E, FK, P).transpose(2, 0, 1).reshape(P, E * FK),
        "w1": v["L0_ffn_w1"].reshape(E, DK, P, F).transpose(0, 2, 1, 3),
        "w2": v["L0_ffn_w2"].reshape(E, FK, P, D).transpose(0, 2, 1, 3),
        "b2": v["L0_ffn_b2"],
        "bkv": np.concatenate([v["L1_xattn_bk"], v["L1_xattn_bv"]]),
        "bq": v["L1_xattn_bq"][None],
        "bo": v["L1_xattn_bo"],
        "wgu": np.stack([v["L1_ffn_w_gate"], v["L1_ffn_w_up"]]),
        "wd": v["L1_ffn_w_down"],
        **constants(),
    }
    arrays = {"in_" + n: np.ascontiguousarray(m) for n, m in arrays.items()}
    nc = bacc.Bacc("TRN2", target_bir_lowering=False, num_devices=1)
    args = {n[3:]: nc.dram_tensor(n, list(m.shape), F32, kind="ExternalInput").ap() for n, m in arrays.items()}
    out = nc.dram_tensor("out", [B * TQ, D], F32, kind="ExternalOutput").ap()
    build(nc, args, out)
    r = run_bass_kernel_spmd(nc, [arrays], core_ids=[0])
    return r.results[0]["out"].reshape(B, TQ, D)
```
